# Optimizing a Trainium2 kernel written in Bass

```python
import numpy as np
import jax
import jax.numpy as jnp

def _softmax(x, axis=-1):
    return jax.nn.softmax(x, axis=axis)

def _gelu(x):
    return jax.nn.gelu(x, approximate=True)

def _silu(x):
    return jax.nn.silu(x)

def _sigmoid(x):
    return jax.nn.sigmoid(x)

def _layernorm(x, axis=-1, eps=1e-05):
    m = jnp.mean(x, axis=axis, keepdims=True)
    v = jnp.var(x, axis=axis, keepdims=True)
    return (x - m) / jnp.sqrt(v + eps)

def _scatter_add(tgt, idx, src, axis=0):
    return tgt.at[idx].add(src)

def _segment_sum(src, seg, n):
    return jax.ops.segment_sum(src, seg, n)
kernel_name = 'mk_adaln_d2_jaxref_r8_61f287'

def setup_inputs(seed: int=0):
    np.random.seed(seed)
    _w = jnp.asarray

    def _L0_attn_setup():
        import jax, jax.numpy as jnp
        from jax import lax
        import numpy as np
        HIDDEN = 256
        NHEADS = 64
        HEADDIM = 64
        INTER = NHEADS * HEADDIM
        NGROUPS = 8
        NSTATE = 128
        GN = NGROUPS * NSTATE
        CONV_DIM = INTER + 2 * GN
        K = 4
        EPS = 1e-05

        def silu(x):
            return x * jax.nn.sigmoid(x)
        key = jax.random.key(seed)
        ks = jax.random.split(key, 12)
        B, S = (2, 256)
        sh = 1.0 / np.sqrt(HIDDEN)
        si = 1.0 / np.sqrt(INTER)
        return {'hidden_states': jax.random.normal(ks[0], (B, S, HIDDEN), jnp.float32), 'Wz': jax.random.normal(ks[1], (HIDDEN, INTER), jnp.float32) * sh, 'Wx': jax.random.normal(ks[2], (HIDDEN, INTER), jnp.float32) * sh, 'WB': jax.random.normal(ks[3], (HIDDEN, GN), jnp.float32) * sh, 'WC': jax.random.normal(ks[4], (HIDDEN, GN), jnp.float32) * sh, 'Wdt': jax.random.normal(ks[5], (HIDDEN, NHEADS), jnp.float32) * sh, 'conv_w': jax.random.normal(ks[6], (CONV_DIM, K), jnp.float32) * 0.2, 'conv_b': jnp.zeros((CONV_DIM,), jnp.float32), 'dt_bias': jax.random.uniform(ks[7], (NHEADS,), jnp.float32, -4.0, -1.0), 'A_log': jnp.log(jnp.arange(1, NHEADS + 1, dtype=jnp.float32)), 'D': jnp.ones((NHEADS,), jnp.float32), 'norm_w': jnp.ones((INTER,), jnp.float32), 'Wout': jax.random.normal(ks[8], (INTER, HIDDEN), jnp.float32) * si}
    _L0_attn_in = _L0_attn_setup()

    def _L0_ffn_setup():
        import jax, jax.numpy as jnp
        import numpy as np
        H = 256
        I = 176
        E = 16
        K = 2
        N_SHARED = 2
        IS = I * N_SHARED
        ROUTED_SCALE = 1.0
        CAPACITY = 128

        def _moe_forward(hidden_states, gate_w, w_gate, w_up, w_down, ws_gate, ws_up, ws_down):
            B, S, _ = hidden_states.shape
            x = hidden_states.reshape(-1, H)
            T = x.shape[0]
            logits = jnp.einsum('th,eh->te', x.astype(jnp.float32), gate_w.astype(jnp.float32))
            scores = jax.nn.softmax(logits, axis=-1)
            topk_w, topk_idx = jax.lax.top_k(scores, K)
            topk_w = (topk_w * ROUTED_SCALE).astype(x.dtype)
            flat_idx = topk_idx.reshape(-1)
            order = jnp.argsort(flat_idx)
            sorted_e = flat_idx[order]
            sorted_t = order // K
            counts = jnp.bincount(flat_idx, length=E)
            starts = jnp.cumsum(counts) - counts
            pos = jnp.arange(T * K) - starts[sorted_e]
            buf = jnp.zeros((E, CAPACITY, H), x.dtype).at[sorted_e, pos].set(x[sorted_t], mode='drop')
            g = jax.nn.silu(jnp.einsum('ech,ehi->eci', buf, w_gate))
            u = jnp.einsum('ech,ehi->eci', buf, w_up)
            expert_out = jnp.einsum('eci,eih->ech', g * u, w_down)
            gathered = expert_out[sorted_e, pos]
            out_flat = jnp.zeros((T * K, H), x.dtype).at[order].set(gathered)
            y = (out_flat.reshape(T, K, H) * topk_w[..., None]).sum(axis=1)
            sh = jnp.einsum('ti,ih->th', jax.nn.silu(x @ ws_gate) * (x @ ws_up), ws_down)
            return (y + sh).reshape(B, S, H)
        key = jax.random.key(seed)
        ks = jax.random.split(key, 8)
        B, S = (2, 128)
        scale = 0.02
        return {'hidden_states': jax.random.normal(ks[0], (B, S, H), jnp.float32), 'gate_w': jax.random.normal(ks[1], (E, H), jnp.float32) * scale, 'w_gate': jax.random.normal(ks[2], (E, H, I), jnp.float32) * scale, 'w_up': jax.random.normal(ks[3], (E, H, I), jnp.float32) * scale, 'w_down': jax.random.normal(ks[4], (E, I, H), jnp.float32) * scale, 'ws_gate': jax.random.normal(ks[5], (H, IS), jnp.float32) * scale, 'ws_up': jax.random.normal(ks[6], (H, IS), jnp.float32) * scale, 'ws_down': jax.random.normal(ks[7], (IS, H), jnp.float32) * scale}
    _L0_ffn_in = _L0_ffn_setup()
    _L0_c = _w((lambda *s: np.random.randn(*s).astype(np.float32) * 0.05)(4, 256))
    _L0_wmod = _w((lambda *s: np.random.randn(*s).astype(np.float32) * 0.05)(256, 6 * 256) * 256 ** (-0.5))

    def _L1_attn_setup():
        import jax, jax.numpy as jnp
        import numpy as np
        B, T, D, H = (2, 256, 256, 16)
        DH = D // H
        ROPE_BASE = 10000.0

        def _rope(x, cos, sin):
            x0 = x[..., 0::2]
            x1 = x[..., 1::2]
            r0 = cos * x0 - sin * x1
            r1 = sin * x0 + cos * x1
            return jnp.stack((r0, r1), axis=-1).reshape(x.shape)
        key = jax.random.key(seed)
        ks = jax.random.split(key, 5)
        s = D ** (-0.5)
        return {'X': jax.random.normal(ks[0], (B, T, D), dtype=jnp.float32), 'Wq': jax.random.normal(ks[1], (D, D), dtype=jnp.float32) * s, 'Wk': jax.random.normal(ks[2], (D, D), dtype=jnp.float32) * s, 'Wv': jax.random.normal(ks[3], (D, D), dtype=jnp.float32) * s, 'Wo': jax.random.normal(ks[4], (D, D), dtype=jnp.float32) * s}
    _L1_attn_in = _L1_attn_setup()

    def _L1_ffn_setup():
        import jax, jax.numpy as jnp
        import numpy as np
        H, F, E, K = (256, 128, 16, 4)
        ROUTED_SCALE = 1.0
        key = jax.random.key(seed)
        ks = jax.random.split(key, 9)
        s = 0.02
        return {'x': jax.random.normal(ks[0], (4, 64, H), jnp.float32), 'router_w': jax.random.normal(ks[1], (E, H), jnp.float32) * s, 'router_bias': jnp.zeros((E,), jnp.float32), 'expert_gate_w': jax.random.normal(ks[2], (E, F, H), jnp.float32) * s, 'expert_up_w': jax.random.normal(ks[3], (E, F, H), jnp.float32) * s, 'expert_down_w': jax.random.normal(ks[4], (E, H, F), jnp.float32) * s, 'shared_gate_w': jax.random.normal(ks[5], (F, H), jnp.float32) * s, 'shared_up_w': jax.random.normal(ks[6], (F, H), jnp.float32) * s, 'shared_down_w': jax.random.normal(ks[7], (H, F), jnp.float32) * s}
    _L1_ffn_in = _L1_ffn_setup()
    _L1_c = _w((lambda *s: np.random.randn(*s).astype(np.float32) * 0.05)(4, 256))
    _L1_wmod = _w((lambda *s: np.random.randn(*s).astype(np.float32) * 0.05)(256, 6 * 256) * 256 ** (-0.5))
    _d = {'L0_attn_hidden_states': _L0_attn_in['hidden_states'], 'L0_attn_Wz': _L0_attn_in['Wz'], 'L0_attn_Wx': _L0_attn_in['Wx'], 'L0_attn_WB': _L0_attn_in['WB'], 'L0_attn_WC': _L0_attn_in['WC'], 'L0_attn_Wdt': _L0_attn_in['Wdt'], 'L0_attn_conv_w': _L0_attn_in['conv_w'], 'L0_attn_conv_b': _L0_attn_in['conv_b'], 'L0_attn_dt_bias': _L0_attn_in['dt_bias'], 'L0_attn_A_log': _L0_attn_in['A_log'], 'L0_attn_D': _L0_attn_in['D'], 'L0_attn_norm_w': _L0_attn_in['norm_w'], 'L0_attn_Wout': _L0_attn_in['Wout'], 'L0_ffn_gate_w': _L0_ffn_in['gate_w'], 'L0_ffn_w_gate': _L0_ffn_in['w_gate'], 'L0_ffn_w_up': _L0_ffn_in['w_up'], 'L0_ffn_w_down': _L0_ffn_in['w_down'], 'L0_ffn_ws_gate': _L0_ffn_in['ws_gate'], 'L0_ffn_ws_up': _L0_ffn_in['ws_up'], 'L0_ffn_ws_down': _L0_ffn_in['ws_down'], 'L0_c': _L0_c, 'L0_wmod': _L0_wmod, 'L1_attn_Wq': _L1_attn_in['Wq'], 'L1_attn_Wk': _L1_attn_in['Wk'], 'L1_attn_Wv': _L1_attn_in['Wv'], 'L1_attn_Wo': _L1_attn_in['Wo'], 'L1_ffn_router_w': _L1_ffn_in['router_w'], 'L1_ffn_router_bias': _L1_ffn_in['router_bias'], 'L1_ffn_expert_gate_w': _L1_ffn_in['expert_gate_w'], 'L1_ffn_expert_up_w': _L1_ffn_in['expert_up_w'], 'L1_ffn_expert_down_w': _L1_ffn_in['expert_down_w'], 'L1_ffn_shared_gate_w': _L1_ffn_in['shared_gate_w'], 'L1_ffn_shared_up_w': _L1_ffn_in['shared_up_w'], 'L1_ffn_shared_down_w': _L1_ffn_in['shared_down_w'], 'L1_c': _L1_c, 'L1_wmod': _L1_wmod}
    _x0 = _d['L0_attn_hidden_states']
    _d['L0_attn_hidden_states'] = jax.random.normal(jax.random.fold_in(jax.random.key(seed), 1), (4, 256, 256), dtype=_x0.dtype)
    del _x0
    return _d

def reference(L0_attn_hidden_states, L0_attn_Wz, L0_attn_Wx, L0_attn_WB, L0_attn_WC, L0_attn_Wdt, L0_attn_conv_w, L0_attn_conv_b, L0_attn_dt_bias, L0_attn_A_log, L0_attn_D, L0_attn_norm_w, L0_attn_Wout, L0_ffn_gate_w, L0_ffn_w_gate, L0_ffn_w_up, L0_ffn_w_down, L0_ffn_ws_gate, L0_ffn_ws_up, L0_ffn_ws_down, L0_c, L0_wmod, L1_attn_Wq, L1_attn_Wk, L1_attn_Wv, L1_attn_Wo, L1_ffn_router_w, L1_ffn_router_bias, L1_ffn_expert_gate_w, L1_ffn_expert_up_w, L1_ffn_expert_down_w, L1_ffn_shared_gate_w, L1_ffn_shared_up_w, L1_ffn_shared_down_w, L1_c, L1_wmod):

    def _L0_attn_ref(hidden_states, Wz, Wx, WB, WC, Wdt, conv_w, conv_b, dt_bias, A_log, D, norm_w, Wout):
        import jax, jax.numpy as jnp
        from jax import lax
        import numpy as np
        HIDDEN = 256
        NHEADS = 64
        HEADDIM = 64
        INTER = NHEADS * HEADDIM
        NGROUPS = 8
        NSTATE = 128
        GN = NGROUPS * NSTATE
        CONV_DIM = INTER + 2 * GN
        K = 4
        EPS = 1e-05

        def silu(x):
            return x * jax.nn.sigmoid(x)
        B, S, _ = hidden_states.shape
        gate = hidden_states @ Wz
        x_in = hidden_states @ Wx
        B_in = hidden_states @ WB
        C_in = hidden_states @ WC
        dt_raw = hidden_states @ Wdt
        xBC = jnp.concatenate([x_in, B_in, C_in], axis=-1)
        xp = jnp.pad(xBC, ((0, 0), (K - 1, 0), (0, 0)))
        acc = conv_b
        for k in range(K):
            acc = acc + xp[:, k:k + S, :] * conv_w[:, k]
        xBC = silu(acc)
        x = xBC[..., :INTER].reshape(B, S, NHEADS, HEADDIM)
        Bm = xBC[..., INTER:INTER + GN].reshape(B, S, NGROUPS, NSTATE)
        Cm = xBC[..., INTER + GN:].reshape(B, S, NGROUPS, NSTATE)
        dt = jax.nn.softplus(dt_raw + dt_bias)
        A = -jnp.exp(A_log)
        dA = jnp.exp(dt * A)
        hpg = NHEADS // NGROUPS
        Bh = jnp.repeat(Bm, hpg, axis=2)
        Ch = jnp.repeat(Cm, hpg, axis=2)

        def step(state, inp):
            dA_t, dt_t, x_t, B_t, C_t = inp
            dBx = dt_t[..., None, None] * x_t[..., None] * B_t[:, :, None, :]
            state = dA_t[..., None, None] * state + dBx
            y = jnp.einsum('bhdn,bhn->bhd', state, C_t)
            return (state, y)
        state0 = jnp.zeros((B, NHEADS, HEADDIM, NSTATE), jnp.float32)
        xs = (dA.transpose(1, 0, 2), dt.transpose(1, 0, 2), x.transpose(1, 0, 2, 3), Bh.transpose(1, 0, 2, 3), Ch.transpose(1, 0, 2, 3))
        _, ys = lax.scan(step, state0, xs)
        y = ys.transpose(1, 0, 2, 3) + D[None, None, :, None] * x
        scan_out = y.reshape(B, S, INTER)
        g = scan_out * silu(gate)
        var = jnp.mean(jnp.square(g), axis=-1, keepdims=True)
        normed = g * lax.rsqrt(var + EPS) * norm_w
        return normed @ Wout

    def _L0_ffn_ref(hidden_states, gate_w, w_gate, w_up, w_down, ws_gate, ws_up, ws_down):
        import jax, jax.numpy as jnp
        import numpy as np
        H = 256
        I = 176
        E = 16
        K = 2
        N_SHARED = 2
        IS = I * N_SHARED
        ROUTED_SCALE = 1.0
        CAPACITY = 128

        def _moe_forward(hidden_states, gate_w, w_gate, w_up, w_down, ws_gate, ws_up, ws_down):
            B, S, _ = hidden_states.shape
            x = hidden_states.reshape(-1, H)
            T = x.shape[0]
            logits = jnp.einsum('th,eh->te', x.astype(jnp.float32), gate_w.astype(jnp.float32))
            scores = jax.nn.softmax(logits, axis=-1)
            topk_w, topk_idx = jax.lax.top_k(scores, K)
            topk_w = (topk_w * ROUTED_SCALE).astype(x.dtype)
            flat_idx = topk_idx.reshape(-1)
            order = jnp.argsort(flat_idx)
            sorted_e = flat_idx[order]
            sorted_t = order // K
            counts = jnp.bincount(flat_idx, length=E)
            starts = jnp.cumsum(counts) - counts
            pos = jnp.arange(T * K) - starts[sorted_e]
            buf = jnp.zeros((E, CAPACITY, H), x.dtype).at[sorted_e, pos].set(x[sorted_t], mode='drop')
            g = jax.nn.silu(jnp.einsum('ech,ehi->eci', buf, w_gate))
            u = jnp.einsum('ech,ehi->eci', buf, w_up)
            expert_out = jnp.einsum('eci,eih->ech', g * u, w_down)
            gathered = expert_out[sorted_e, pos]
            out_flat = jnp.zeros((T * K, H), x.dtype).at[order].set(gathered)
            y = (out_flat.reshape(T, K, H) * topk_w[..., None]).sum(axis=1)
            sh = jnp.einsum('ti,ih->th', jax.nn.silu(x @ ws_gate) * (x @ ws_up), ws_down)
            return (y + sh).reshape(B, S, H)
        return _moe_forward(hidden_states, gate_w, w_gate, w_up, w_down, ws_gate, ws_up, ws_down)

    def _L1_attn_ref(X, Wq, Wk, Wv, Wo):
        import jax, jax.numpy as jnp
        import numpy as np
        B, T, D, H = (2, 256, 256, 16)
        DH = D // H
        ROPE_BASE = 10000.0

        def _rope(x, cos, sin):
            x0 = x[..., 0::2]
            x1 = x[..., 1::2]
            r0 = cos * x0 - sin * x1
            r1 = sin * x0 + cos * x1
            return jnp.stack((r0, r1), axis=-1).reshape(x.shape)
        b, t, d = X.shape
        Q = X @ Wq.T
        K = X @ Wk.T
        V = X @ Wv.T
        Qh = Q.reshape(b, t, H, DH).transpose(0, 2, 1, 3)
        Kh = K.reshape(b, t, H, DH).transpose(0, 2, 1, 3)
        Vh = V.reshape(b, t, H, DH).transpose(0, 2, 1, 3)
        theta = ROPE_BASE ** (-2.0 * jnp.arange(DH // 2, dtype=jnp.float32) / DH)
        angles = jnp.arange(t, dtype=jnp.float32)[:, None] * theta[None, :]
        cos = jnp.cos(angles).astype(X.dtype)
        sin = jnp.sin(angles).astype(X.dtype)
        Qr = _rope(Qh, cos, sin)
        Kr = _rope(Kh, cos, sin)
        scores = jnp.einsum('bhqd,bhkd->bhqk', Qr, Kr) * DH ** (-0.5)
        causal = jnp.triu(jnp.ones((t, t), dtype=bool), 1)
        scores = jnp.where(causal, jnp.finfo(scores.dtype).min, scores)
        pattern = jax.nn.softmax(scores, axis=-1)
        heads = jnp.einsum('bhqk,bhkd->bqhd', pattern, Vh).reshape(b, t, d)
        return heads @ Wo.T

    def _L1_ffn_ref(x, router_w, router_bias, expert_gate_w, expert_up_w, expert_down_w, shared_gate_w, shared_up_w, shared_down_w):
        import jax, jax.numpy as jnp
        import numpy as np
        H, F, E, K = (256, 128, 16, 4)
        ROUTED_SCALE = 1.0
        orig_shape = x.shape
        h = x.reshape(-1, orig_shape[-1])
        T = h.shape[0]
        logits = h @ router_w.T
        scores = jax.nn.sigmoid(logits)
        choice = scores + router_bias[None, :]
        _, topk_idx = jax.lax.top_k(choice, K)
        topk_w = jnp.take_along_axis(scores, topk_idx, axis=1)
        topk_w = topk_w / (topk_w.sum(-1, keepdims=True) + 1e-20)
        topk_w = topk_w * ROUTED_SCALE
        comb = jnp.zeros((T, E), h.dtype).at[jnp.arange(T)[:, None], topk_idx].set(topk_w)
        g = jnp.einsum('th,efh->tef', h, expert_gate_w)
        u = jnp.einsum('th,efh->tef', h, expert_up_w)
        a = jax.nn.silu(g) * u
        routed = jnp.einsum('tef,te,ehf->th', a, comb, expert_down_w)
        shared = jax.nn.silu(h @ shared_gate_w.T) * (h @ shared_up_w.T) @ shared_down_w.T
        return (routed + shared).reshape(orig_shape)
    x = L0_attn_hidden_states
    mod = (_silu(L0_c) @ L0_wmod).reshape(L0_c.shape[0], 6, 1, -1)
    sa, ca, ga, sb, cb, gb = (mod[:, 0], mod[:, 1], mod[:, 2], mod[:, 3], mod[:, 4], mod[:, 5])
    ga = (2 * (ga >= 0) - 1) * jnp.maximum(jnp.abs(ga), 0.25)
    gb = (2 * (gb >= 0) - 1) * jnp.maximum(jnp.abs(gb), 0.25)
    h = _layernorm(x, axis=-1) * (1 + ca) + sa
    x = x + ga * _L0_attn_ref(h, L0_attn_Wz, L0_attn_Wx, L0_attn_WB, L0_attn_WC, L0_attn_Wdt, L0_attn_conv_w, L0_attn_conv_b, L0_attn_dt_bias, L0_attn_A_log, L0_attn_D, L0_attn_norm_w, L0_attn_Wout)
    h = _layernorm(x, axis=-1) * (1 + cb) + sb
    x = x + gb * _L0_ffn_ref(h, L0_ffn_gate_w, L0_ffn_w_gate, L0_ffn_w_up, L0_ffn_w_down, L0_ffn_ws_gate, L0_ffn_ws_up, L0_ffn_ws_down)
    mod = (_silu(L1_c) @ L1_wmod).reshape(L1_c.shape[0], 6, 1, -1)
    sa, ca, ga, sb, cb, gb = (mod[:, 0], mod[:, 1], mod[:, 2], mod[:, 3], mod[:, 4], mod[:, 5])
    ga = (2 * (ga >= 0) - 1) * jnp.maximum(jnp.abs(ga), 0.25)
    gb = (2 * (gb >= 0) - 1) * jnp.maximum(jnp.abs(gb), 0.25)
    h = _layernorm(x, axis=-1) * (1 + ca) + sa
    x = x + ga * _L1_attn_ref(h, L1_attn_Wq, L1_attn_Wk, L1_attn_Wv, L1_attn_Wo)
    h = _layernorm(x, axis=-1) * (1 + cb) + sb
    x = x + gb * _L1_ffn_ref(h, L1_ffn_router_w, L1_ffn_router_bias, L1_ffn_expert_gate_w, L1_ffn_expert_up_w, L1_ffn_expert_down_w, L1_ffn_shared_gate_w, L1_ffn_shared_up_w, L1_ffn_shared_down_w)
    return x

_drawn_inputs = setup_inputs


def setup_inputs(seed=0):
    import zlib

    import numpy as np

    out = dict(_drawn_inputs(seed))
    spreads = {'L0_attn_conv_b': (0.0, 0.1),
     'L0_attn_D': (1.0, 0.2),
     'L0_attn_norm_w': (1.0, 0.2),
     'L1_ffn_router_bias': (0.0, 0.8)}
    factors = {'L0_attn_dt_bias': 2.796,
     'L0_attn_A_log': 47.464,
     'L0_ffn_gate_w': 8.0,
     'L0_ffn_w_gate': 8.0,
     'L0_ffn_w_up': 8.0,
     'L0_ffn_w_down': 8.0,
     'L0_ffn_ws_gate': 8.0,
     'L0_ffn_ws_up': 8.0,
     'L0_ffn_ws_down': 8.0,
     'L1_ffn_router_w': 8.0,
     'L1_ffn_expert_gate_w': 8.0,
     'L1_ffn_expert_up_w': 8.0,
     'L1_ffn_expert_down_w': 8.0,
     'L1_ffn_shared_gate_w': 8.0,
     'L1_ffn_shared_up_w': 8.0,
     'L1_ffn_shared_down_w': 8.0,
     'L0_attn_WB': 3.674,
     'L0_attn_WC': 4.16,
     'L1_attn_Wq': 3.11,
     'L1_attn_Wk': 3.148}
    for name, (base, spread) in spreads.items():
        noise = np.random.default_rng([zlib.crc32(name.encode()), seed]).standard_normal(out[name].shape)
        drawn = base * np.exp(spread * noise) if base else spread * noise
        out[name] = jnp.asarray(drawn.astype(out[name].dtype))
    for name, factor in factors.items():
        out[name] = (out[name] * factor).astype(out[name].dtype)
    return out
```

```python
from contextlib import ExitStack

import concourse.bass as bass
from concourse import mybir

F32 = mybir.dt.float32
U32 = mybir.dt.uint32
ALU = mybir.AluOpType
ACT = mybir.ActivationFunctionType
AX = mybir.AxisListType.X

P = 128
B, S, D = 4, 256, 256
NT = B * S // P
KD = D // P
HEADS, HD, GROUPS, NST = 64, 64, 8, 128
HG = HEADS // GROUPS
GC = HG * HD
XT = GC // P
TAPS = 4
INTER = HEADS * HD
E0, I0, CAP, IT = 16, 176, 128, 88
IS = 352
NIS = IS // IT
E1, F1, K1 = 16, 128, 4
AH, DH = 16, 16
EPS = 1e-5
CT = (INTER + 2 * GROUPS * NST) // P
COLS = (TAPS + 1) * CT + INTER // P + KD * B
C_ID, C_GT, C_LE, C_ONE, C_LE2, C_LT, C_NEG, C_IOTA, C_ROPE = [P * i for i in range(9)]
C_ALL = C_ROPE + 2 * 2 * DH
ARENA = 37300


def bc(ap, shape):
    return ap.broadcast_to(shape)


def build(nc, A, out):
    with ExitStack() as ctx:
        def sb(name, shape, dt=F32):
            return ctx.enter_context(nc.sbuf_tensor(name, shape, dt))

        def sem(name):
            return ctx.enter_context(nc.semaphore(name))

        bank = [ctx.enter_context(nc.psum_tensor(f"bank{i}", [P, 512], F32)) for i in range(8)]
        const = sb("const", [P, C_ALL])
        ident = const[:, C_ID:C_ID + P]
        tri_gt = const[:, C_GT:C_GT + P]
        tri_le = const[:, C_LE:C_LE + P]
        ones = const[:, C_ONE:C_ONE + P]
        causal3 = const[:, C_LE:C_LE + 3 * P]
        tri_lt = const[:, C_LT:C_LT + P]
        neg_mask = const[:, C_NEG:C_NEG + P]
        iota = const[:, C_IOTA:C_IOTA + P]
        rope = const[:, C_ROPE:C_ALL].rearrange("p (s c d) -> p s c d", s=2, c=2)
        x = sb("x", [P, NT, D])
        h = sb("h", [P, NT, D])
        hT = sb("hT", [P, KD, NT * P])
        mod = sb("mod", [P, B, 6 * D])
        stats = sb("stats", [P, NT, 6])
        mv = sb("mv", [P, NT, 2])
        rstd = sb("rstd", [P, NT])
        std = sb("std", [P, NT])
        y_acc = sb("y_acc", [P, NT, D])
        ss = sb("ss", [P, NT, GROUPS])
        arena = sb("arena", [P, ARENA])

        def carver():
            at = [0]

            def take(*shape, parts=P):
                n = 1
                for s in shape:
                    n *= s
                v = arena[0:parts, at[0]:at[0] + n]
                at[0] += n
                assert at[0] <= ARENA, at[0]
                if len(shape) == 1:
                    return v
                names = "abcd"[:len(shape)]
                return v.rearrange("p (" + " ".join(names) + ") -> p " + " ".join(names),
                                   **{c: s for c, s in zip(names, shape)})
            return take

        norm_stat = sem("norm_stat")
        norm_aggr = sem("norm_aggr")
        norm_var = sem("norm_var")
        norm_std = sem("norm_std")
        norm_rstd = sem("norm_rstd")
        norm_xn = sem("norm_xn")
        norm_hm = sem("norm_hm")
        norm_h = sem("norm_h")
        norm_tr = sem("norm_tr")
        norm_hT = sem("norm_hT")

        def norm_dve(dve, n, row_s, row_c):
            for t in range(NT):
                nc.vector.bn_stats(stats[:, t, :], x[:, t, :]).then_inc(norm_stat, 1)
            for t in range(NT):
                dve.wait_ge(norm_stat, n * NT + t + 1)
                nc.vector.bn_aggr(mv[:, t, :], stats[:, t, :]).then_inc(norm_aggr, 1)
            dve.wait_ge(norm_aggr, (n + 1) * NT)
            nc.vector.tensor_scalar(std[:, :], mv[:, :, 1], EPS, None, ALU.add).then_inc(norm_var, 1)
            dve.wait_ge(norm_std, n + 1)
            nc.vector.reciprocal(rstd[:, :], std[:, :]).then_inc(norm_rstd, 1)
            dve.wait_ge(norm_rstd, n + 1)
            for t in range(NT):
                nc.vector.tensor_scalar(h[:, t, :], x[:, t, :], mv[:, t, 0:1], rstd[:, t:t + 1],
                                        ALU.subtract, ALU.mult).then_inc(norm_xn, 1)
            for t in range(NT):
                dve.wait_ge(norm_xn, n * NT + t + 1)
                nc.vector.tensor_tensor(h[:, t, :], h[:, t, :], mod[:, t // 2, row_c * D:(row_c + 1) * D],
                                        ALU.mult).then_inc(norm_hm, 1)
            for t in range(NT):
                dve.wait_ge(norm_hm, n * NT + t + 1)
                nc.vector.tensor_tensor(h[:, t, :], h[:, t, :], mod[:, t // 2, row_s * D:(row_s + 1) * D],
                                        ALU.add).then_inc(norm_h, 1)

        def norm_act_sqrt(act, n):
            act.wait_ge(norm_var, n + 1)
            nc.scalar.activation(std[:, :], std[:, :], ACT.Sqrt).then_inc(norm_std, 1)

        def norm_pe(pe, n, banks):
            for j in range(NT // 2):
                pe.wait_ge(norm_h, n * NT + 2 * j + 2)
                if j >= 2:
                    pe.wait_ge(norm_hT, n * NT // 2 + j - 1)
                for k in range(KD):
                    for q in range(2):
                        last = nc.tensor.transpose(banks[j % 2][:, (2 * k + q) * P:(2 * k + q + 1) * P],
                                                   h[:, 2 * j + q, k * P:(k + 1) * P], ident)
                last.then_inc(norm_tr, 1)

        def norm_act_copy(act, n, banks):
            for j in range(NT // 2):
                act.wait_ge(norm_tr, n * NT // 2 + j + 1)
                nc.scalar.copy(hT[:, :, 2 * j * P:(2 * j + 2) * P],
                               banks[j % 2][:, :].rearrange("p (k t) -> p k t", k=KD)).then_inc(norm_hT, 1)

        def mod_pe(pe, rows_ready, wmod, csb, pe_mod, act_mod):
            pe.wait_ge(rows_ready, 1)
            for u in range(B * 3):
                if u >= 2:
                    pe.wait_ge(act_mod, u - 1)
                b, n = u // 3, u % 3
                for k in range(KD):
                    last = nc.tensor.matmul(bank[2 + u % 2][:, :], csb[:, k, b, :], wmod[:, k, n * 512:(n + 1) * 512],
                                            start=k == 0, stop=k == KD - 1)
                last.then_inc(pe_mod, 1)

        def mod_act(act, pe_mod, act_mod):
            for u in range(B * 3):
                act.wait_ge(pe_mod, u + 1)
                b, n = u // 3, u % 3
                nc.scalar.copy(mod[:, b, n * 512:(n + 1) * 512], bank[2 + u % 2][:, :]).then_inc(act_mod, 1)

        def mod_dve(dve, act_mod, scratch, chain):
            dve.wait_ge(act_mod, B * 3)
            m = mod[:, :, :].rearrange("p b (u r d) -> p b u r d", u=2, r=3)
            for b in range(B):
                nc.vector.tensor_scalar(m[:, b, :, 1, :], m[:, b, :, 1, :], 1.0, None, ALU.add).then_inc(chain, 1)
            for b in range(B):
                g = m[:, b, :, 2, :]
                n0 = B + 4 * b
                dve.wait_ge(chain, n0)
                nc.vector.tensor_scalar(scratch, g, 0.0, 2.0, ALU.is_ge, ALU.mult).then_inc(chain, 1)
                dve.wait_ge(chain, n0 + 1)
                nc.vector.tensor_scalar(scratch, scratch, -1.0, None, ALU.add).then_inc(chain, 1)
                dve.wait_ge(chain, n0 + 2)
                nc.vector.tensor_tensor(g, g, scratch, ALU.mult).then_inc(chain, 1)
                dve.wait_ge(chain, n0 + 3)
                nc.vector.scalar_tensor_tensor(out=g, in0=g, scalar=0.25, in1=scratch,
                                               op0=ALU.max, op1=ALU.mult).then_inc(chain, 1)
            dve.wait_ge(chain, 5 * B)

        take = carver()
        w_x = take(2, KD, GC)
        w_z = take(2, KD, GC)
        w_b = take(2, KD, NST)
        w_c = take(2, KD, NST)
        w_out = take(2, XT, D)
        cols = take(COLS)
        conv_w = cols[:, 0:TAPS * CT].rearrange("p (k t) -> p t k", k=TAPS)
        conv_b = cols[:, TAPS * CT:(TAPS + 1) * CT]
        norm_w = cols[:, (TAPS + 1) * CT:(TAPS + 1) * CT + INTER // P]
        cT0 = cols[:, COLS - KD * B:COLS].rearrange("p (k b) -> p k b", k=KD)
        a_log = take(HEADS)
        dt_bias = take(HEADS)
        d_skip = take(HEADS)
        dt = take(NT, HEADS)
        la = take(NT, HEADS)
        dte = take(B, HEADS)
        ef = take(2, B, HEADS)
        xc = take(2, 6, S)
        acc = take(3, 2, S)
        sg = take(2, 2, GC)
        rbuf = take(2, 4, P)
        ebuf = take(2, 4, P)
        mbuf = take(4, 4, P)
        xtok = take(2, GC)
        xd = take(2, GC)
        xdd = take(2, GC)
        xe = take(GC)
        gm = take(3 * P)
        gt = take(2, GC)
        gtT = take(2, XT, P)
        off = take(GC)
        junk = take(GC)
        flat = arena[:, :]
        base = 2 * 2 * KD * GC + 2 * 2 * KD * NST + 2 * XT * D + COLS + 3 * HEADS + 2 * NT * HEADS \
            + 3 * B * HEADS
        wmod0 = flat[:, base:base + 3072].rearrange("p (k n) -> p k n", k=KD)
        csb0 = flat[:, base + 3072:base + 4096].rearrange("p (k b m) -> p k b m", k=KD, b=B)
        raw = base + 4240 + 512 * 7
        conv_w_raw = flat[0:CT, raw:raw + P * TAPS].rearrange("t (p k) -> t k p", k=TAPS)
        conv_b_raw = flat[0:CT, raw + 512:raw + 640]
        norm_w_raw = flat[0:INTER // P, raw + 640:raw + 768]
        c_raw = flat[0:B, raw + 768:raw + 1024]
        wdt = flat[:, base + 4112:base + 4240].rearrange("p (k n) -> p k n", k=KD)
        tmp = [flat[:, base + 4240 + 512 * i:base + 4240 + 512 * (i + 1)] for i in range(7)]
        csi0 = flat[:, base + 4104:base + 4112].rearrange("p (k b) -> p k b", k=KD)

        ld_x, ld_const, ld_mod, ld_row, ld_wdt, ld_conv = (sem(n) for n in (
            "ld_x", "ld_const", "ld_mod", "ld_row", "ld_wdt", "ld_conv"))
        ld_w = [sem("ld_w_even"), sem("ld_w_odd")]
        act_cs, dve_csb, pe_mod, act_mod, mod_chain = (sem(n) for n in (
            "act_cs", "dve_csb", "pe_mod", "act_mod", "mod_chain"))
        pe_dt, dt_chain, act_e1, act_a, pe_ef, act_ef, dve_setup = (sem(n) for n in (
            "pe_dt", "dt_chain", "act_e1", "act_a", "pe_ef", "act_ef", "dve_setup"))
        pe_cols, act_cols, dve_alog = sem("pe_cols"), sem("act_cols"), sem("dve_alog")

        x_in = A["L0_attn_hidden_states"].rearrange("b (c p) d -> p (b c) d", p=P)
        NW = 5

        def load_group(eng, g):
            s = ld_w[g % 2]
            k = g % 2
            eng.dma_start(w_x[:, k], A["L0_attn_Wx"][:, g * GC:(g + 1) * GC].rearrange("(k p) n -> p k n", p=P)).then_inc(s, 16)
            eng.dma_start(w_b[:, k], A["L0_attn_WB"][:, g * NST:(g + 1) * NST].rearrange("(k p) n -> p k n", p=P)).then_inc(s, 16)
            eng.dma_start(w_c[:, k], A["L0_attn_WC"][:, g * NST:(g + 1) * NST].rearrange("(k p) n -> p k n", p=P)).then_inc(s, 16)
            eng.dma_start(w_z[:, k], A["L0_attn_Wz"][:, g * GC:(g + 1) * GC].rearrange("(k p) n -> p k n", p=P)).then_inc(s, 16)
            eng.dma_start(w_out[:, k], A["L0_attn_Wout"][g * GC:(g + 1) * GC, :].rearrange("(k p) n -> p k n", p=P)).then_inc(s, 16)

        with nc.Block() as block:
            @block.sync
            def _(sp):
                sp.dma_start(x[:, :, :], x_in).then_inc(ld_x, 16)
                sp.dma_start(c_raw, A["L0_c"]).then_inc(ld_conv, 16)
                sp.dma_start(flat[0:CT, raw:raw + P * TAPS],
                             A["L0_attn_conv_w"].rearrange("(t p) k -> t (p k)", p=P)).then_inc(ld_conv, 16)
                sp.dma_start(conv_b_raw, A["L0_attn_conv_b"].rearrange("(t p) -> t p", p=P)).then_inc(ld_conv, 16)
                sp.dma_start(norm_w_raw, A["L0_attn_norm_w"].rearrange("(t p) -> t p", p=P)).then_inc(ld_conv, 16)
                sp.dma_start(const[:, :], A["const"]).then_inc(ld_const, 16)
                sp.dma_start(wmod0, A["L0_wmod"].rearrange("(k p) n -> p k n", p=P)).then_inc(ld_mod, 16)
                sp.dma_start(wdt, A["L0_attn_Wdt"].rearrange("(k p) n -> p k n", p=P)).then_inc(ld_wdt, 16)
                sp.dma_start(a_log, A["L0_attn_A_log"].partition_broadcast(P)).then_inc(ld_row, 16)
                sp.dma_start(dt_bias, A["L0_attn_dt_bias"].partition_broadcast(P)).then_inc(ld_row, 16)
                sp.dma_start(d_skip, A["L0_attn_D"].partition_broadcast(P)).then_inc(ld_row, 16)
                load_group(sp, 0)
                load_group(sp, 1)

            @block.scalar
            def _(act):
                act.wait_ge(pe_cols, 1)
                nc.scalar.copy(cols, bank[6][:, 0:COLS]).then_inc(act_cols, 1)
                act.wait_ge(act_cols, 1)
                nc.scalar.activation(csi0, cT0, ACT.Silu).then_inc(act_cs, 1)
                mod_act(act, pe_mod, act_mod)
                norm_act_sqrt(act, 0)
                norm_act_copy(act, 0, bank[0:2])
                act.wait_ge(dve_alog, 1)
                nc.scalar.activation(a_log, a_log, ACT.Exp).then_inc(act_a, 1)
                act.wait_ge(dt_chain, 2)
                nc.scalar.activation(tmp[1], tmp[1], ACT.Exp).then_inc(act_e1, 1)
                act.wait_ge(pe_ef, 1)
                nc.scalar.activation(ef.rearrange("p a b h -> p (a b h)"), bank[5][:, :], ACT.Exp).then_inc(act_ef, 1)

            @block.tensor
            def _(pe):
                pe.wait_ge(ld_const, 16)
                pe.wait_ge(ld_conv, 64)
                for k in range(TAPS):
                    nc.tensor.transpose(bank[6][:, k * CT:(k + 1) * CT], conv_w_raw[:, k, :], ident[0:CT, 0:CT])
                nc.tensor.transpose(bank[6][:, TAPS * CT:(TAPS + 1) * CT], conv_b_raw, ident[0:CT, 0:CT])
                n0 = (TAPS + 1) * CT
                nc.tensor.transpose(bank[6][:, n0:n0 + INTER // P], norm_w_raw, ident[0:INTER // P, 0:INTER // P])
                n0 += INTER // P
                for k in range(KD):
                    last = nc.tensor.transpose(bank[6][:, n0 + k * B:n0 + (k + 1) * B], c_raw[:, k * P:(k + 1) * P],
                                               ident[0:B, 0:B])
                last.then_inc(pe_cols, 1)
                pe.wait_ge(ld_mod, 16)
                mod_pe(pe, dve_csb, wmod0, csb0, pe_mod, act_mod)
                norm_pe(pe, 0, bank[0:2])
                pe.wait_ge(ld_wdt, 16)
                pe.wait_ge(norm_hT, 1 * NT // 2)
                for t in range(NT):
                    for k in range(KD):
                        last = nc.tensor.matmul(bank[4][:, t * HEADS:(t + 1) * HEADS], hT[:, k, t * P:(t + 1) * P],
                                                wdt[:, k, :], start=k == 0, stop=k == KD - 1)
                last.then_inc(pe_dt, 1)
                pe.wait_ge(dve_setup, 1)
                for b in range(B):
                    nc.tensor.matmul(bank[5][:, b * HEADS:(b + 1) * HEADS], tri_gt, la[:, 2 * b, :],
                                     start=True, stop=True)
                    last = nc.tensor.matmul(bank[5][:, (B + b) * HEADS:(B + b + 1) * HEADS], tri_le,
                                            la[:, 2 * b + 1, :], start=True, stop=True)
                last.then_inc(pe_ef, 1)

            @block.vector
            def _(dve):
                nc.vector.memset(y_acc[:, :, :], 0.0)
                dve.wait_ge(ld_row, 48)
                nc.vector.tensor_scalar(a_log, a_log, 88.0, None, ALU.min).then_inc(dve_alog, 1)
                dve.wait_ge(act_cs, 1)
                nc.vector.tensor_copy(csb0, bc(csi0.unsqueeze(3), [P, KD, B, P])).then_inc(dve_csb, 1)
                mod_dve(dve, act_mod, tmp[6].rearrange("p (u d) -> p u d", u=2), mod_chain)
                dve.wait_ge(ld_x, 16)
                norm_dve(dve, 0, 0, 1)
                dve.wait_ge(ld_row, 48)
                dve.wait_ge(pe_dt, 1)
                v3 = [t_.rearrange("p (t n) -> p t n", t=NT) for t_ in tmp]
                nc.vector.tensor_tensor(v3[0], bank[4][:, :].rearrange("p (t n) -> p t n", t=NT),
                                        bc(dt_bias.unsqueeze(1), [P, NT, HEADS]), ALU.add).then_inc(dt_chain, 1)
                dve.wait_ge(dt_chain, 1)
                nc.vector.scalar_tensor_tensor(out=tmp[1], in0=tmp[0], scalar=-1.0, in1=tmp[0],
                                               op0=ALU.mult, op1=ALU.min).then_inc(dt_chain, 1)
                nc.vector.tensor_scalar(tmp[2], tmp[0], 0.0, None, ALU.max).then_inc(dt_chain, 1)
                dve.wait_ge(act_e1, 1)
                nc.vector.tensor_scalar(tmp[3], tmp[1], 2.0, None, ALU.add).then_inc(dt_chain, 1)
                dve.wait_ge(dt_chain, 4)
                nc.vector.reciprocal(tmp[3], tmp[3]).then_inc(dt_chain, 1)
                dve.wait_ge(dt_chain, 5)
                nc.vector.tensor_tensor(tmp[4], tmp[1], tmp[3], ALU.mult).then_inc(dt_chain, 1)
                dve.wait_ge(dt_chain, 6)
                nc.vector.tensor_tensor(tmp[5], tmp[4], tmp[4], ALU.mult).then_inc(dt_chain, 1)
                dve.wait_ge(dt_chain, 7)
                nc.vector.tensor_scalar(tmp[6], tmp[5], 1.0 / 17, None, ALU.mult).then_inc(dt_chain, 1)
                n = 8
                for odd in (15, 13, 11, 9, 7, 5, 3):
                    dve.wait_ge(dt_chain, n)
                    nc.vector.scalar_tensor_tensor(out=tmp[6], in0=tmp[6], scalar=1.0 / odd, in1=tmp[5],
                                                   op0=ALU.add, op1=ALU.mult).then_inc(dt_chain, 1)
                    n += 1
                dve.wait_ge(dt_chain, n)
                nc.vector.scalar_tensor_tensor(out=tmp[6], in0=tmp[6], scalar=1.0, in1=tmp[4],
                                               op0=ALU.add, op1=ALU.mult).then_inc(dt_chain, 1)
                dve.wait_ge(dt_chain, n + 1)
                dtf = dt.rearrange("p t n -> p (t n)")
                nc.vector.scalar_tensor_tensor(out=dtf, in0=tmp[6], scalar=2.0, in1=tmp[2],
                                               op0=ALU.mult, op1=ALU.add).then_inc(dt_chain, 1)
                dve.wait_ge(dt_chain, n + 2)
                dve.wait_ge(act_a, 1)
                nc.vector.tensor_tensor(la, dt, bc(a_log.unsqueeze(1), [P, NT, HEADS]), ALU.mult).then_inc(dt_chain, 1)
                dve.wait_ge(dt_chain, n + 3)
                nc.vector.tensor_scalar(la, la, -1.0, -1.0e4, ALU.mult, ALU.max).then_inc(dve_setup, 1)
                dve.wait_ge(act_ef, 1)
                nc.vector.tensor_tensor(dte, ef[:, 0], dt.rearrange("p (b c) n -> p b c n", c=2)[:, :, 0, :],
                                        ALU.mult).then_inc(dve_setup, 1)

        names = ("pe_conv act_tap dve_chain dve_conv act_xc pe_gate act_sg pe_g dve_gm pe_xt act_xt pool_xd pool_xdd "
                 "pool_xe pool_r pe_l act_e dve_m pe_y dve_y pe_off dve_off dve_comb dve_g pe_gt act_gt act_sq "
                 "pe_out dve_out pool_w").split()
        q = {n: sem("m_" + n) for n in names}
        (pe_conv, act_tap, dve_chain, dve_conv, act_xc, pe_gate, act_sg, pe_g, dve_gm, pe_xt, act_xt, pool_xd,
         pool_xdd, pool_xe, pool_r, pe_l, act_e, dve_m, pe_y, dve_y, pe_off, dve_off, dve_comb, dve_g, pe_gt, act_gt,
         act_sq, pe_out, dve_out, pool_w) = (q[n] for n in names)
        P0, P1, L0b, L1b, T0, T1, YB, OB = bank
        STEPS = GROUPS * B
        pair_bank = [P0, P1, P0]
        gate_bank = [P1, P0]

        def conv_tile(g, m):
            return XT * g + m if m < XT else (32 + g if m == XT else 40 + g)

        with nc.Block() as block:
            @block.sync
            def _(sp):
                for g in range(2, GROUPS):
                    sp.wait_ge(pe_out, B * (g - 1))
                    load_group(sp, g)

            @block.tensor
            def _(pe):
                def conv_in(i):
                    g, b = i // B, i % B
                    if b == 0:
                        pe.wait_ge(ld_w[g % 2], 16 * NW * (g // 2 + 1))
                    for p_ in range(3):
                        if p_ == 0 and i:
                            pe.wait_ge(act_sg, 2 * i)
                        if p_ == 1 and i:
                            pe.wait_ge(act_sg, 2 * i - 1)
                        if p_ == 2:
                            pe.wait_ge(dve_conv, 3 * i + 1)
                        for m in (2 * p_, 2 * p_ + 1):
                            w = (w_x[:, g % 2, :, m * P:(m + 1) * P] if m < XT else
                                 (w_b if m == XT else w_c)[:, g % 2, :, :])
                            for k in range(KD):
                                last = nc.tensor.matmul(pair_bank[p_][:, (m % 2) * S:(m % 2 + 1) * S], w[:, k, :],
                                                        hT[:, k, b * S:(b + 1) * S], start=k == 0, stop=k == KD - 1)
                        last.then_inc(pe_conv, 1)

                def gate_in(i):
                    g, b = i // B, i % B
                    for c in range(2):
                        pe.wait_ge(dve_conv, 3 * i + 2 + c)
                        for k in range(KD):
                            last = nc.tensor.matmul(gate_bank[c][:, :], hT[:, k, (2 * b + c) * P:(2 * b + c + 1) * P],
                                                    w_z[:, g % 2, k, :], start=k == 0, stop=k == KD - 1)
                        last.then_inc(pe_gate, 1)

                conv_in(0)
                gate_in(0)
                for i in range(STEPS):
                    g, b = i // B, i % B
                    v = xc[:, i % 2]
                    pe.wait_ge(act_xc, 3 * (i + 1))
                    if i:
                        pe.wait_ge(act_gt, 2 * i - 1)
                    nc.tensor.matmul(T0[:, 0:S], v[:, 4, 0:P], v[:, 5, :], start=True, stop=True)
                    nc.tensor.matmul(T0[:, S:S + P], v[:, 4, P:S], v[:, 5, P:S], start=True, stop=True).then_inc(pe_g, 1)
                    for c in range(2):
                        if c == 0 and i:
                            pe.wait_ge(act_gt, 2 * i)
                        if c == 1:
                            pe.wait_ge(dve_gm, i + 1)
                        for m in range(XT):
                            last = nc.tensor.transpose((T1, T0)[c][:, m * P:(m + 1) * P],
                                                       v[:, m, c * P:(c + 1) * P], ident)
                        last.then_inc(pe_xt, 1)
                    for u in range(4 * i, 4 * i + 4):
                        pe.wait_ge(pool_r, u + 1)
                        if u >= 2:
                            pe.wait_ge(act_e, u - 1)
                        nc.tensor.matmul((L0b, L1b)[u % 2][:, :], tri_gt, rbuf[:, u % 2].rearrange("p a b -> p (a b)"),
                                         start=True, stop=True).then_inc(pe_l, 1)
                    if i + 1 < STEPS:
                        conv_in(i + 1)
                    for c in range(2):
                        pe.wait_ge(dve_m, 4 * i + 2 * c + 2)
                        pe.wait_ge(pool_xd, 2 * i + c + 1)
                        pe.wait_ge(dve_y, 2 * i + c)
                        for hh in range(HG):
                            last = nc.tensor.matmul(YB[:, hh * HD:(hh + 1) * HD], mbuf[:, 2 * c + hh // 4, hh % 4, :],
                                                    xd[:, c, hh * HD:(hh + 1) * HD], start=True, stop=True)
                        last.then_inc(pe_y, 1)
                    pe.wait_ge(pool_xe, i + 1)
                    pe.wait_ge(act_xt, 2 * i + 1)
                    nc.tensor.matmul(T1[:, :], gm[:, P:2 * P], xe, start=True, stop=True).then_inc(pe_off, 1)
                    if i + 1 < STEPS:
                        gate_in(i + 1)
                    for c in range(2):
                        pe.wait_ge(dve_g, 2 * i + c + 1)
                        if c == 0:
                            pe.wait_ge(act_xt, 2 * i + 2)
                        else:
                            pe.wait_ge(dve_off, i + 1)
                        for m in range(XT):
                            last = nc.tensor.transpose((T0, T1)[c][:, m * P:(m + 1) * P],
                                                       gt[:, c, m * P:(m + 1) * P], ident)
                        last.then_inc(pe_gt, 1)
                    if i:
                        pe.wait_ge(dve_out, i)
                    pe.wait_ge(pool_w, g + 1)
                    for c in range(2):
                        pe.wait_ge(act_gt, 2 * i + c + 1)
                        for m in range(XT):
                            last = nc.tensor.matmul(OB[:, c * D:(c + 1) * D], gtT[:, c, m, :], w_out[:, g % 2, m, :],
                                                    start=m == 0, stop=m == XT - 1)
                    last.then_inc(pe_out, 1)

            @block.scalar
            def _(act):
                def conv_first(i):
                    g, b = i // B, i % B

                    def tap(p_):
                        act.wait_ge(pe_conv, 3 * i + p_ + 1)
                        for m in (2 * p_, 2 * p_ + 1):
                            ct = conv_tile(g, m)
                            nc.scalar.activation(acc[:, p_, m % 2, :], pair_bank[p_][:, (m % 2) * S:(m % 2 + 1) * S],
                                                 ACT.Identity, bias=conv_b[:, ct:ct + 1],
                                                 scale=conv_w[:, ct, TAPS - 1:TAPS]).then_inc(act_tap, 1)

                    def silu(p_):
                        act.wait_ge(dve_conv, 3 * i + p_ + 1)
                        if i >= 2 and p_ == 0:
                            act.wait_ge(pe_xt, 2 * (i - 1))
                        nc.scalar.activation(xc[:, i % 2, 2 * p_:2 * p_ + 2, :], acc[:, p_], ACT.Silu).then_inc(act_xc, 1)

                    tap(0)
                    tap(1)
                    silu(0)
                    tap(2)
                    silu(1)
                    silu(2)

                def gates(i):
                    for c in range(2):
                        act.wait_ge(pe_gate, 2 * i + c + 1)
                        if i >= 2:
                            act.wait_ge(dve_g, 2 * (i - 2) + c + 1)
                        nc.scalar.activation(sg[:, i % 2, c], gate_bank[c][:, :], ACT.Silu).then_inc(act_sg, 1)

                conv_first(0)
                gates(0)
                for i in range(STEPS):
                    for c in range(2):
                        act.wait_ge(pe_xt, 2 * i + c + 1)
                        if i:
                            act.wait_ge(pool_xdd, 2 * (i - 1) + c + 1)
                        nc.scalar.copy(xtok[:, c], (T1, T0)[c][:, :]).then_inc(act_xt, 1)
                    for u in range(4 * i, 4 * i + 4):
                        act.wait_ge(pe_l, u + 1)
                        if u >= 2:
                            act.wait_ge(dve_m, u - 1)
                        nc.scalar.activation(ebuf[:, u % 2].rearrange("p a b -> p (a b)"), (L0b, L1b)[u % 2][:, :],
                                             ACT.Exp).then_inc(act_e, 1)
                    if i + 1 < STEPS:
                        conv_first(i + 1)
                        gates(i + 1)
                    for c in range(2):
                        t = 2 * (i % B) + c
                        act.wait_ge(dve_g, 2 * i + c + 1)
                        if i or c:
                            act.wait_ge(act_sq, 2 * i + c)
                        nc.scalar.activation(junk, gt[:, c], ACT.Square,
                                             accum_out=ss[:, t, i // B:i // B + 1]).then_inc(act_sq, 1)
                        act.wait_ge(pe_gt, 2 * i + c + 1)
                        if i:
                            act.wait_ge(pe_out, i)
                        nc.scalar.copy(gtT[:, c].rearrange("p a b -> p (a b)"), (T0, T1)[c][:, :]).then_inc(act_gt, 1)

            @block.gpsimd
            def _(pool):
                def decay_rows(i, c):
                    g, t = i // B, 2 * (i % B) + c
                    for hf in range(2):
                        u = 4 * i + 2 * c + hf
                        if u >= 2:
                            pool.wait_ge(pe_l, u - 1)
                        h0 = g * HG + 4 * hf
                        nc.gpsimd.tensor_tensor(rbuf[:, u % 2], bc(tri_le.unsqueeze(1), [P, 4, P]),
                                                bc(la[:, t, h0:h0 + 4].unsqueeze(2), [P, 4, P]),
                                                ALU.mult).then_inc(pool_r, 1)

                for i in range(STEPS):
                    g, b = i // B, i % B
                    hs = slice(g * HG, (g + 1) * HG)
                    decay_rows(i, 0)
                    decay_rows(i, 1)
                    if b == 0:
                        pool.wait_ge(ld_w[g % 2], 16 * NW * (g // 2 + 1))
                        nc.gpsimd.tensor_tensor(w_out[:, g % 2], w_out[:, g % 2],
                                                bc(norm_w[:, XT * g:XT * (g + 1)].unsqueeze(2), [P, XT, D]),
                                                ALU.mult).then_inc(pool_w, 1)
                    for c in range(2):
                        pool.wait_ge(act_xt, 2 * i + c + 1)
                        if i:
                            pool.wait_ge(pe_y, 2 * (i - 1) + c + 1)
                        xv = xtok[:, c].rearrange("p (h d) -> p h d", d=HD)
                        nc.gpsimd.tensor_tensor(xd[:, c].rearrange("p (h d) -> p h d", d=HD), xv,
                                                bc(dt[:, 2 * b + c, hs].unsqueeze(2), [P, HG, HD]),
                                                ALU.mult).then_inc(pool_xd, 1)
                        if c == 0:
                            if i:
                                pool.wait_ge(pe_off, i)
                            nc.gpsimd.tensor_tensor(xe.rearrange("p (h d) -> p h d", d=HD), xv,
                                                    bc(dte[:, b, hs].unsqueeze(2), [P, HG, HD]),
                                                    ALU.mult).then_inc(pool_xe, 1)
                        if i:
                            pool.wait_ge(dve_y, 2 * (i - 1) + c + 1)
                        nc.gpsimd.tensor_tensor(xdd[:, c].rearrange("p (h d) -> p h d", d=HD), xv,
                                                bc(d_skip[:, hs].unsqueeze(2), [P, HG, HD]),
                                                ALU.mult).then_inc(pool_xdd, 1)

            @block.vector
            def _(dve):
                def conv_rest(i):
                    g = i // B
                    for p_ in range(3):
                        n0 = 6 * (3 * i + p_)
                        dve.wait_ge(act_tap, 6 * i + 2 * p_ + 2)
                        for j in range(6):
                            m, sh = 2 * p_ + j % 2, j // 2 + 1
                            ct = conv_tile(g, m)
                            if j >= 2:
                                dve.wait_ge(dve_chain, n0 + j - 1)
                            ins = nc.vector.scalar_tensor_tensor(
                                out=acc[:, p_, m % 2, sh:], in0=pair_bank[p_][:, (m % 2) * S:(m % 2 + 1) * S - sh],
                                scalar=conv_w[:, ct, TAPS - 1 - sh:TAPS - sh], in1=acc[:, p_, m % 2, sh:],
                                op0=ALU.mult, op1=ALU.add)
                            ins.then_inc(dve_chain, 1)
                        dve.wait_ge(dve_chain, n0 + 6)
                        nc.vector.engine_nop().then_inc(dve_conv, 1)

                conv_rest(0)
                for i in range(STEPS):
                    g, b = i // B, i % B
                    hs = slice(g * HG, (g + 1) * HG)
                    dve.wait_ge(pe_g, i + 1)
                    if i:
                        dve.wait_ge(pe_off, i)
                    nc.vector.tensor_tensor(gm, T0[:, 0:3 * P], causal3, ALU.mult).then_inc(dve_gm, 1)
                    dve.wait_ge(dve_gm, i + 1)
                    for u in range(4):
                        c = u // 2
                        dve.wait_ge(act_e, 4 * i + u + 1)
                        if i:
                            dve.wait_ge(pe_y, 2 * (i - 1) + c + 1)
                        nc.vector.tensor_tensor(mbuf[:, u], ebuf[:, u % 2],
                                                bc(gm[:, 2 * c * P:(2 * c + 1) * P].unsqueeze(1), [P, 4, P]),
                                                ALU.mult).then_inc(dve_m, 1)
                    if i + 1 < STEPS:
                        conv_rest(i + 1)
                    n0 = 3 * i
                    for c in range(2):
                        dve.wait_ge(pe_y, 2 * i + c + 1)
                        dve.wait_ge(pool_xdd, 2 * i + c + 1)
                        if i:
                            dve.wait_ge(act_sq, 2 * (i - 1) + c + 1)
                            dve.wait_ge(pe_gt, 2 * (i - 1) + c + 1)
                        nc.vector.tensor_tensor(gt[:, c], YB[:, :], xdd[:, c], ALU.add).then_inc(dve_y, 1)
                        if c == 1:
                            dve.wait_ge(pe_off, i + 1)
                            nc.vector.tensor_tensor(off.rearrange("p (h d) -> p h d", d=HD),
                                                    T1[:, :].rearrange("p (h d) -> p h d", d=HD),
                                                    bc(ef[:, 1, b, hs].unsqueeze(2), [P, HG, HD]),
                                                    ALU.mult).then_inc(dve_off, 1)
                            dve.wait_ge(dve_off, i + 1)
                            dve.wait_ge(dve_y, 2 * i + 2)
                            nc.vector.tensor_tensor(gt[:, c], gt[:, c], off, ALU.add).then_inc(dve_comb, 1)
                            dve.wait_ge(dve_comb, i + 1)
                        dve.wait_ge(dve_y, 2 * i + c + 1)
                        dve.wait_ge(act_sg, 2 * i + c + 1)
                        nc.vector.tensor_tensor(gt[:, c], gt[:, c], sg[:, i % 2, c], ALU.mult).then_inc(dve_g, 1)
                    dve.wait_ge(pe_out, i + 1)
                    if i:
                        dve.wait_ge(dve_out, i)
                    oa = y_acc[:, 2 * b:2 * b + 2, :]
                    nc.vector.tensor_tensor(oa, OB[:, :].rearrange("p (c d) -> p c d", c=2), oa,
                                            ALU.add).then_inc(dve_out, 1)

        take = carver()
        wg = take(E0, KD, I0)
        wu = take(E0, KD, I0)
        wd = take(E0, 2, D, parts=IT)
        wsg = take(KD, IS)
        wsu = take(KD, IS)
        wsd = take(NIS, D, parts=IT)
        gate_raw = take(D, parts=E0)
        gate_t = take(KD, E0)
        slot = take(NT, 4, P)
        back_t = take(2, 4, P)
        back = take(4, NT * P)
        xe_t = take(KD, 4 * P)
        silu_g = take(2, 2 * P, parts=IT)
        act_t = take(2, 2, P, parts=IT)
        oe = take(4, D)
        sh_s = take(2, 512, parts=IT)
        sh_a = slot[0:IT, 0:4].rearrange("p t e c -> p t (e c)")
        small = [take(NT, E0) for _ in range(9)]
        r_mx, r_sum, r_rec, rms, rms_std = (take(NT) for _ in range(5))
        m8 = take(NT, 8)
        i8 = take(NT, 8).bitcast(U32)
        i8f = take(NT, 8)

        names = ("ld_gate ld_wu ld_wd ld_sh dve_ms act_ms dve_res pe_gw act_gw pe_lg dve_rt act_ex dve_sel pe_pos "
                 "dve_pos pe_sg act_sg dve_sa pe_sd act_sy dve_p dve_q pe_disp act_xe pe_q act_qt pe_up act_s dve_a "
                 "pe_dn act_oe pe_comb dve_y").split()
        f = {n: sem("f_" + n) for n in names}
        (ld_gate, ld_wu, ld_wd, ld_sh, dve_ms, act_ms, dve_res, pe_gw, act_gw, pe_lg, dve_rt, act_ex, dve_sel, pe_pos,
         dve_pos, pe_sg, act_sg, dve_sa, pe_sd, act_sy, dve_p, dve_q, pe_disp, act_xe, pe_q, act_qt, pe_up, act_s,
         dve_a, pe_dn, act_oe, pe_comb, dve_y) = (f[n] for n in names)
        NQ = E0 // 4

        def topk_select(dve, scores, k, chain, n0, eq, sel, m8, i8, i8f):
            for t in range(NT):
                nc.vector.max(m8[:, t, :], scores[:, t, :]).then_inc(chain, 1)
            for t in range(NT):
                dve.wait_ge(chain, n0 + t + 1)
                nc.vector.max_index(i8[:, t, :], m8[:, t, :], scores[:, t, :]).then_inc(chain, 1)
            dve.wait_ge(chain, n0 + 2 * NT)
            nc.vector.tensor_copy(i8f, i8).then_inc(chain, 1)
            n = n0 + 2 * NT + 1
            for r in range(k):
                dve.wait_ge(chain, n)
                nc.vector.tensor_tensor(eq if r else sel, bc(iota[:, 0:E0].unsqueeze(1), [P, NT, E0]),
                                        bc(i8f[:, :, r:r + 1], [P, NT, E0]), ALU.is_equal).then_inc(chain, 1)
                n += 1
                if r:
                    dve.wait_ge(chain, n)
                    nc.vector.tensor_tensor(sel, sel, eq, ALU.add).then_inc(chain, 1)
                    n += 1
            return n

        with nc.Block() as block:
            @block.sync
            def _(sp):
                sp.dma_start(gate_raw, A["L0_ffn_gate_w"]).then_inc(ld_gate, 16)
                sp.dma_start(wsg, A["L0_ffn_ws_gate"].rearrange("(k p) i -> p k i", p=P)).then_inc(ld_sh, 16)
                sp.dma_start(wsu, A["L0_ffn_ws_up"].rearrange("(k p) i -> p k i", p=P)).then_inc(ld_sh, 16)
                sp.dma_start(wsd, A["L0_ffn_ws_down"].rearrange("(j p) n -> p j n", p=IT)).then_inc(ld_sh, 16)
                sp.dma_start(wg, A["L0_ffn_w_gate"].rearrange("e (k p) i -> p e k i", p=P)).then_inc(ld_wu, 16)
                sp.dma_start(wu, A["L0_ffn_w_up"].rearrange("e (k p) i -> p e k i", p=P)).then_inc(ld_wu, 16)
                sp.dma_start(wd, A["L0_ffn_w_down"].rearrange("e (j p) n -> p e j n", p=IT)).then_inc(ld_wd, 16)

            @block.tensor
            def _(pe):
                pe.wait_ge(ld_gate, 16)
                for k in range(KD):
                    last = nc.tensor.transpose(bank[4][:, k * E0:(k + 1) * E0], gate_raw[:, k * P:(k + 1) * P],
                                               ident[0:E0, 0:E0])
                last.then_inc(pe_gw, 1)
                norm_pe(pe, 1, bank[0:2])
                pe.wait_ge(act_gw, 1)
                pe.wait_ge(norm_hT, 2 * NT // 2)
                for t in range(NT):
                    for k in range(KD):
                        last = nc.tensor.matmul(bank[5][:, t * E0:(t + 1) * E0], hT[:, k, t * P:(t + 1) * P],
                                                gate_t[:, k, :], start=k == 0, stop=k == KD - 1)
                last.then_inc(pe_lg, 1)
                pe.wait_ge(ld_sh, 48)
                for th in range(2):
                    for j in range(NIS):
                        u = NIS * th + j
                        if u >= 2:
                            pe.wait_ge(dve_sa, u - 1)
                        for w, bk in ((wsg, bank[u % 2]), (wsu, bank[2 + u % 2])):
                            for k in range(KD):
                                last = nc.tensor.matmul(bk[0:IT, :], w[:, k, j * IT:(j + 1) * IT],
                                                        hT[:, k, th * 512:(th + 1) * 512], start=k == 0, stop=k == KD - 1)
                        last.then_inc(pe_sg, 1)
                    for t in range(4):
                        u = 4 * th + t
                        pe.wait_ge(dve_sa, NIS * (th + 1))
                        if u >= 2:
                            pe.wait_ge(act_sy, u - 1)
                        for j in range(NIS):
                            last = nc.tensor.matmul(bank[6 + u % 2][:, 0:D], sh_a[:, j, t * P:(t + 1) * P], wsd[:, j, :],
                                                    start=j == 0, stop=j == NIS - 1)
                        last.then_inc(pe_sd, 1)
                pe.wait_ge(dve_sel, 1)
                sel = small[4]
                for t in range(NT):
                    for s_ in range(t):
                        nc.tensor.matmul(bank[5][:, P + t * E0:P + (t + 1) * E0], ones, sel[:, s_, :],
                                         start=s_ == 0, stop=False)
                    last = nc.tensor.matmul(bank[5][:, P + t * E0:P + (t + 1) * E0], tri_lt, sel[:, t, :],
                                            start=t == 0, stop=True)
                last.then_inc(pe_pos, 1)

                pe.wait_ge(dve_sa, 2 * NIS)
                pe.wait_ge(act_sy, 2 * 4)
                for eq in range(NQ):
                    for k in range(KD):
                        if eq:
                            pe.wait_ge(act_xe, 2 * eq)
                        for t in range(NT):
                            pe.wait_ge(dve_p, NT * eq + t + 1)
                            last = nc.tensor.matmul(bank[k][:, :], h[:, t, k * P:(k + 1) * P],
                                                    slot[:, t].rearrange("p e c -> p (e c)"),
                                                    start=t == 0, stop=t == NT - 1)
                        last.then_inc(pe_disp, 1)
                    for t in range(NT):
                        u = NT * eq + t
                        pe.wait_ge(dve_q, u + 1)
                        if t >= 2:
                            pe.wait_ge(act_qt, u - 1)
                        elif eq:
                            pe.wait_ge(dve_y, NT * eq - 1 + t)
                        for e in range(4):
                            last = nc.tensor.transpose(bank[2 + t % 2][:, e * P:(e + 1) * P], back_t[:, t % 2, e, :], ident)
                        last.then_inc(pe_q, 1)

                    def up(e):
                        n = 4 * eq + e
                        pe.wait_ge(act_xe, 2 * (eq + 1))
                        pe.wait_ge(ld_wu, 32)
                        if n >= 2:
                            pe.wait_ge(dve_a, n - 1)
                        if n == 1:
                            pe.wait_ge(dve_pos, 1)
                        for w, o in ((wg, 0), (wu, 2)):
                            for j in range(2):
                                for k in range(KD):
                                    last = nc.tensor.matmul(bank[4 + n % 2][0:IT, (o + j) * P:(o + j + 1) * P],
                                                            w[:, n, k, j * IT:(j + 1) * IT],
                                                            xe_t[:, k, e * P:(e + 1) * P], start=k == 0, stop=k == KD - 1)
                        last.then_inc(pe_up, 1)

                    def down(e):
                        n = 4 * eq + e
                        pe.wait_ge(dve_a, n + 1)
                        pe.wait_ge(ld_wd, 16)
                        if n >= 2:
                            pe.wait_ge(act_oe, n - 1)
                        for j in range(2):
                            last = nc.tensor.matmul(bank[6 + n % 2][:, 0:D], act_t[:, n % 2, j, :], wd[:, n, j, :],
                                                    start=j == 0, stop=j == 1)
                        last.then_inc(pe_dn, 1)

                    up(0)
                    for e in range(4):
                        if e < 3:
                            up(e + 1)
                        down(e)
                    for t in range(NT):
                        u = NT * eq + t
                        pe.wait_ge(act_oe, 4 * (eq + 1))
                        pe.wait_ge(act_qt, NT * (eq + 1))
                        if t >= 2:
                            pe.wait_ge(dve_y, u - 1)
                        for e in range(4):
                            last = nc.tensor.matmul(bank[2 + t % 2][:, 0:D], back[:, e, t * P:(t + 1) * P], oe[:, e, :],
                                                    start=e == 0, stop=e == 3)
                        last.then_inc(pe_comb, 1)

            @block.scalar
            def _(act):
                act.wait_ge(dve_ms, 2)
                nc.scalar.activation(rms_std, rms_std, ACT.Sqrt).then_inc(act_ms, 1)
                norm_act_sqrt(act, 1)
                act.wait_ge(pe_gw, 1)
                nc.scalar.copy(gate_t.rearrange("p k e -> p (k e)"), bank[4][:, 0:KD * E0]).then_inc(act_gw, 1)
                norm_act_copy(act, 1, bank[0:2])
                act.wait_ge(dve_rt, 2)
                nc.scalar.activation(small[1], small[0], ACT.Exp).then_inc(act_ex, 1)
                for th in range(2):
                    for j in range(NIS):
                        u = NIS * th + j
                        act.wait_ge(pe_sg, u + 1)
                        if u >= 2:
                            act.wait_ge(dve_sa, u - 1)
                        nc.scalar.activation(sh_s[:, u % 2], bank[u % 2][0:IT, :], ACT.Silu).then_inc(act_sg, 1)
                    for t in range(4):
                        u = 4 * th + t
                        act.wait_ge(pe_sd, u + 1)
                        nc.scalar.copy(y_acc[:, u, :], bank[6 + u % 2][:, 0:D]).then_inc(act_sy, 1)
                for eq in range(NQ):
                    for k in range(KD):
                        act.wait_ge(pe_disp, 2 * eq + k + 1)
                        if eq:
                            act.wait_ge(pe_up, 4 * eq)
                        nc.scalar.copy(xe_t[:, k], bank[k][:, :]).then_inc(act_xe, 1)
                    for t in range(NT):
                        u = NT * eq + t
                        act.wait_ge(pe_q, u + 1)
                        if eq:
                            act.wait_ge(pe_comb, NT * eq)
                        nc.scalar.copy(back[:, :, t * P:(t + 1) * P],
                                       bank[2 + t % 2][:, :].rearrange("p (e c) -> p e c", e=4)).then_inc(act_qt, 1)

                    def silu(e):
                        n = 4 * eq + e
                        act.wait_ge(pe_up, n + 1)
                        if n >= 2:
                            act.wait_ge(dve_a, n - 1)
                        nc.scalar.activation(silu_g[:, n % 2], bank[4 + n % 2][0:IT, 0:2 * P], ACT.Silu).then_inc(act_s, 1)

                    silu(0)
                    for e in range(4):
                        if e < 3:
                            silu(e + 1)
                        act.wait_ge(pe_dn, 4 * eq + e + 1)
                        if eq:
                            act.wait_ge(pe_comb, NT * eq)
                        nc.scalar.copy(oe[:, e, :], bank[6 + e % 2][:, 0:D]).then_inc(act_oe, 1)

            @block.vector
            def _(dve):
                nc.vector.tensor_reduce(rms_std, ss[:, :, :], AX, ALU.add).then_inc(dve_ms, 1)
                dve.wait_ge(dve_ms, 1)
                nc.vector.tensor_scalar(rms_std, rms_std, 1.0 / INTER, EPS, ALU.mult, ALU.add).then_inc(dve_ms, 1)
                dve.wait_ge(act_ms, 1)
                nc.vector.reciprocal(rms, rms_std).then_inc(dve_ms, 1)
                dve.wait_ge(dve_ms, 3)
                for t in range(NT):
                    nc.vector.scalar_tensor_tensor(out=y_acc[:, t, :], in0=y_acc[:, t, :], scalar=rms[:, t:t + 1],
                                                   in1=mod[:, t // 2, 2 * D:3 * D], op0=ALU.mult,
                                                   op1=ALU.mult).then_inc(dve_res, 1)
                for t in range(NT):
                    dve.wait_ge(dve_res, t + 1)
                    nc.vector.tensor_tensor(x[:, t, :], x[:, t, :], y_acc[:, t, :], ALU.add).then_inc(dve_res, 1)
                dve.wait_ge(dve_res, 2 * NT)
                norm_dve(dve, 1, 3, 4)
                lg = bank[5][:, 0:P].rearrange("p (t e) -> p t e", t=NT)
                pos = bank[5][:, P:2 * P].rearrange("p (t e) -> p t e", t=NT)
                shift, ex, prob, eqv, sel, wt, posd, qpos, qtmp = small
                dve.wait_ge(pe_lg, 1)
                nc.vector.tensor_reduce(r_mx, lg, AX, ALU.max).then_inc(dve_rt, 1)
                dve.wait_ge(dve_rt, 1)
                nc.vector.tensor_tensor(shift, lg, bc(r_mx.unsqueeze(2), [P, NT, E0]), ALU.subtract).then_inc(dve_rt, 1)
                dve.wait_ge(act_ex, 1)
                nc.vector.tensor_reduce(r_sum, ex, AX, ALU.add).then_inc(dve_rt, 1)
                dve.wait_ge(dve_rt, 3)
                nc.vector.reciprocal(r_rec, r_sum).then_inc(dve_rt, 1)
                dve.wait_ge(dve_rt, 4)
                nc.vector.tensor_tensor(prob, ex, bc(r_rec.unsqueeze(2), [P, NT, E0]), ALU.mult).then_inc(dve_rt, 1)
                dve.wait_ge(dve_rt, 5)
                n = topk_select(dve, prob, 2, dve_rt, 5, eqv, sel, m8, i8, i8f)
                dve.wait_ge(dve_rt, n)
                nc.vector.tensor_tensor(wt, prob, sel, ALU.mult).then_inc(dve_sel, 1)

                def shared(th):
                    for j in range(NIS):
                        u = NIS * th + j
                        dve.wait_ge(act_sg, u + 1)
                        if th:
                            dve.wait_ge(pe_sd, 4)
                        nc.vector.tensor_tensor(sh_a[:, j, :], bank[2 + u % 2][0:IT, :], sh_s[:, u % 2],
                                                ALU.mult).then_inc(dve_sa, 1)

                shared(0)
                shared(1)
                dve.wait_ge(pe_pos, 1)
                nc.vector.scalar_tensor_tensor(out=posd, in0=pos, scalar=1.0, in1=sel, op0=ALU.add,
                                               op1=ALU.mult).then_inc(dve_rt, 1)
                nc.vector.tensor_scalar(qtmp, pos, CAP - 1.0, 1.0, ALU.min, ALU.add).then_inc(dve_rt, 1)
                dve.wait_ge(dve_rt, n + 2)
                nc.vector.tensor_scalar(posd, posd, -1.0, None, ALU.add).then_inc(dve_rt, 1)
                nc.vector.tensor_tensor(qpos, qtmp, sel, ALU.mult).then_inc(dve_rt, 1)
                dve.wait_ge(dve_rt, n + 4)
                nc.vector.tensor_scalar(qpos, qpos, -1.0, None, ALU.add).then_inc(dve_pos, 1)
                dve.wait_ge(dve_pos, 1)
                for eq in range(NQ):
                    if eq:
                        dve.wait_ge(pe_disp, 2 * eq)
                    else:
                        dve.wait_ge(pe_sd, 2 * 4)
                    for t in range(NT):
                        for e in range(4):
                            last = nc.vector.tensor_scalar(slot[:, t, e, :], iota, posd[:, t, 4 * eq + e:4 * eq + e + 1],
                                                           None, ALU.is_equal)
                        last.then_inc(dve_p, 1)
                    for t in range(NT):
                        u = NT * eq + t
                        if u >= 2:
                            dve.wait_ge(pe_q, u - 1)
                        for e in range(4):
                            last = nc.vector.tensor_scalar(back_t[:, t % 2, e, :], iota,
                                                           qpos[:, t, 4 * eq + e:4 * eq + e + 1],
                                                           wt[:, t, 4 * eq + e:4 * eq + e + 1], ALU.is_equal, ALU.mult)
                        last.then_inc(dve_q, 1)
                    for e in range(4):
                        n = 4 * eq + e
                        dve.wait_ge(act_s, n + 1)
                        if n >= 2:
                            dve.wait_ge(pe_dn, n - 1)
                        nc.vector.tensor_tensor(act_t[:, n % 2].rearrange("p j c -> p (j c)"),
                                                bank[4 + n % 2][0:IT, 2 * P:4 * P], silu_g[:, n % 2],
                                                ALU.mult).then_inc(dve_a, 1)
                    dve.wait_ge(act_sy, 2 * 4)
                    for t in range(NT):
                        u = NT * eq + t
                        dve.wait_ge(pe_comb, u + 1)
                        if eq:
                            dve.wait_ge(dve_y, u - NT + 1)
                        nc.vector.tensor_tensor(y_acc[:, t, :], bank[2 + t % 2][:, 0:D], y_acc[:, t, :],
                                                ALU.add).then_inc(dve_y, 1)

        take = carver()
        w_raw = take(4, 2, D)
        w_t = take(4, KD, D)
        wmod1 = take(KD, 6 * D)
        csb1 = take(KD, B, P)
        c1_raw = take(D, parts=B)
        c1_t = take(KD, B)
        c1_s = take(KD, B)
        mscr = take(2, D)
        qkp = take(2, 2, AH, 32)
        r_a = take(2 * AH, DH)
        r_b = take(2 * AH, DH)
        q_t = take(4, NT * P)
        k_t = take(4, NT * P)
        v_sb = take(NT, D)
        prob_sb = wmod1.rearrange("p k n -> p (k n)")[:, 0:2048].rearrange("p (r n) -> p r n", r=4)
        prob_t = w_raw.rearrange("p a b c -> p a (b c)")
        mx = take(4, 4)
        nmx = take(4, 4)
        rs = take(NT, AH)
        rrs = take(NT, AH)
        att = take(D)
        att_t = take(KD, P)
        otmp = take(D)
        assert take(1).offset % ARENA <= ARENA - 17 * 3 * D
        late = carver()
        late(ARENA - 17 * 3 * D)
        w1_raw = late(17, 2, D)
        w1_down = late(17, 2, F1)

        names = ("ld_c ld_w ld_wm dve_res pe_wt act_wt act_cs act_csi pe_cs dve_csb pe_mod act_mod mod_chain pe_qkv "
                 "act_v dve_z dve_rope dve_ra dve_qk pe_qk act_qk pe_s dve_mask dve_mx dve_nm act_p pe_pt ev_pt_a "
                 "ev_pt_d pe_pv dve_rr dve_att pe_at act_at pe_wo dve_o dve_x").split()
        g_ = {n: sem("a_" + n) for n in names}
        (ld_c, ld_wq, ld_wm, dve_res1, pe_wt, act_wt, act_cs1, act_csi1, pe_cs, dve_csb1, pe_mod1, act_mod1, mod_chain1,
         pe_qkv, act_v, dve_z, dve_rope, dve_ra, dve_qk, pe_qk, act_qk, pe_s, dve_mask, dve_mx, dve_nm, act_p, pe_pt,
         act_pt, dve_pt, pe_pv, dve_rr, dve_att, pe_at, act_at, pe_wo, dve_o, dve_x) = (g_[n] for n in names)
        ld_w1 = sem("ld_w1")
        units = [(b, qt, js) for b in range(B) for qt, js in ((0, (0, 1, 2, 3)), (1, (0, 1)), (1, (2, 3)))]

        with nc.Block() as block:
            @block.sync
            def _(sp):
                sp.dma_start(c1_raw, A["L1_c"]).then_inc(ld_c, 16)
                sp.dma_start(wmod1, A["L1_wmod"].rearrange("(k p) n -> p k n", p=P)).then_inc(ld_wm, 16)
                for i_, nm in enumerate(("L1_attn_Wq", "L1_attn_Wk", "L1_attn_Wv", "L1_attn_Wo")):
                    sp.dma_start(w_raw[:, i_], A[nm].rearrange("(o p) d -> p o d", p=P)).then_inc(ld_wq, 16)
                sp.dma_start(w1_raw[:, 0:E1, 0, :], A["L1_ffn_expert_gate_w"].rearrange("e f h -> f e h")).then_inc(ld_w1, 16)
                sp.dma_start(w1_raw[:, 0:E1, 1, :], A["L1_ffn_expert_up_w"].rearrange("e f h -> f e h")).then_inc(ld_w1, 16)
                sp.dma_start(w1_down[:, 0:E1], A["L1_ffn_expert_down_w"].rearrange("e (o p) f -> p e o f", p=P)).then_inc(ld_w1, 16)
                sp.dma_start(w1_raw[:, E1, 0, :], A["L1_ffn_shared_gate_w"]).then_inc(ld_w1, 16)
                sp.dma_start(w1_raw[:, E1, 1, :], A["L1_ffn_shared_up_w"]).then_inc(ld_w1, 16)
                sp.dma_start(w1_down[:, E1], A["L1_ffn_shared_down_w"].rearrange("(o p) f -> p o f", p=P)).then_inc(ld_w1, 16)

            @block.tensor
            def _(pe):
                pe.wait_ge(ld_c, 16)
                for k in range(KD):
                    last = nc.tensor.transpose(bank[6][:, k * B:(k + 1) * B], c1_raw[:, k * P:(k + 1) * P], ident[0:B, 0:B])
                last.then_inc(pe_cs, 1)
                pe.wait_ge(ld_wm, 16)
                mod_pe(pe, dve_csb1, wmod1, csb1, pe_mod1, act_mod1)
                pe.wait_ge(ld_wq, 64)
                for i_ in range(4):
                    if i_ >= 2:
                        pe.wait_ge(act_wt, i_ - 1)
                    for k in range(KD):
                        for o in range(2):
                            last = nc.tensor.transpose(bank[4 + i_ % 2][:, (2 * k + o) * P:(2 * k + o + 1) * P],
                                                       w_raw[:, i_, o, k * P:(k + 1) * P], ident)
                    last.then_inc(pe_wt, 1)
                norm_pe(pe, 2, bank[0:2])
                pe.wait_ge(act_wt, 4)
                pe.wait_ge(norm_hT, 3 * NT // 2)
                pe.wait_ge(act_mod1, 3 * B)

                def qk_transposes(t):
                    pe.wait_ge(dve_qk, t + 1)
                    for s_ in range(2):
                        u = 2 * t + s_
                        if u >= 2:
                            pe.wait_ge(act_qk, u - 1)
                        for j in range(4):
                            last = nc.tensor.transpose(bank[4 + s_][:, j * P:(j + 1) * P],
                                                       qkp[:, t % 2, s_, 4 * j:4 * j + 4, :].rearrange("p a b -> p (a b)"),
                                                       ident)
                        last.then_inc(pe_qk, 1)

                for t in range(NT):
                    if t >= 2:
                        pe.wait_ge(dve_ra, 3 * (t - 1))
                        pe.wait_ge(act_v, t - 1)
                    for w, o in ((0, 0), (1, D)):
                        for k in range(KD):
                            nc.tensor.matmul(bank[t % 2][:, o:o + D], hT[:, k, t * P:(t + 1) * P], w_t[:, w, k, :],
                                             start=k == 0, stop=k == KD - 1)
                    for k in range(KD):
                        last = nc.tensor.matmul(bank[2 + t % 2][:, 0:D], hT[:, k, t * P:(t + 1) * P], w_t[:, 2, k, :],
                                                start=k == 0, stop=k == KD - 1)
                    last.then_inc(pe_qkv, 1)
                    if t:
                        qk_transposes(t - 1)
                qk_transposes(NT - 1)

                def scores(u):
                    b, qt, js = units[u]
                    nk = P * (qt + 1)
                    if u == 0:
                        pe.wait_ge(act_qk, 2 * NT)
                        pe.wait_ge(dve_ra, 3 * NT)
                        pe.wait_ge(act_v, NT)
                    for r in range(4):
                        if u:
                            pe.wait_ge(act_p, 4 * (u - 1) + r + 1)
                        for i_, j in enumerate(js):
                            last = nc.tensor.matmul(bank[r][:, i_ * nk:(i_ + 1) * nk],
                                                    q_t[32 * r:32 * r + DH, j, (2 * b + qt) * P:(2 * b + qt + 1) * P],
                                                    k_t[32 * r:32 * r + DH, j, 2 * b * P:2 * b * P + nk],
                                                    start=True, stop=True)
                        last.then_inc(pe_s, 1)

                def values(u):
                    b, qt, js = units[u]
                    for r in range(4):
                        v = 4 * u + r
                        pe.wait_ge(act_p, v + 1)
                        if r < 2:
                            if u:
                                (pe.wait_ge(act_pt, 2 * u) if r == 0 else pe.wait_ge(dve_pt, 2 * u))
                        else:
                            (pe.wait_ge(act_pt, 2 * u + 1) if r == 2 else pe.wait_ge(dve_pt, 2 * u + 1))
                        for i_ in range(4):
                            last = nc.tensor.transpose(bank[4 + r % 2][:, i_ * P:(i_ + 1) * P],
                                                       prob_sb[:, r, i_ * P:(i_ + 1) * P], ident)
                        last.then_inc(pe_pt, 1)
                    if js[0] == 0 and u:
                        pe.wait_ge(dve_att, 2 * b + qt)
                    for r in range(4):
                        if r % 2 == 0:
                            pe.wait_ge(act_pt, 2 * u + r // 2 + 1)
                        else:
                            pe.wait_ge(dve_pt, 2 * u + r // 2 + 1)
                        for i_, j in enumerate(js):
                            hd = 4 * j + r
                            for kb in range(qt + 1):
                                blk = i_ * (qt + 1) + kb
                                last = nc.tensor.matmul(bank[6][:, hd * DH:(hd + 1) * DH],
                                                        prob_t[:, r, blk * P:(blk + 1) * P],
                                                        v_sb[:, 2 * b + kb, hd * DH:(hd + 1) * DH],
                                                        start=kb == 0, stop=kb == qt)
                    last.then_inc(pe_pv, 1)

                def project(t):
                    pe.wait_ge(dve_att, t + 1)
                    if t:
                        pe.wait_ge(dve_o, t)
                    for k in range(KD):
                        last = nc.tensor.transpose(bank[7][:, k * P:(k + 1) * P], att[:, k * P:(k + 1) * P], ident)
                    last.then_inc(pe_at, 1)
                    pe.wait_ge(act_at, t + 1)
                    for k in range(KD):
                        last = nc.tensor.matmul(bank[7][:, D:2 * D], att_t[:, k, :], w_t[:, 3, k, :],
                                                start=k == 0, stop=k == KD - 1)
                    last.then_inc(pe_wo, 1)

                scores(0)
                for u in range(len(units)):
                    if u + 1 < len(units):
                        scores(u + 1)
                    values(u)
                    if units[u][2][-1] == 3:
                        project(2 * units[u][0] + units[u][1])

            @block.scalar
            def _(act):
                act.wait_ge(pe_cs, 1)
                nc.scalar.activation(c1_s.rearrange("p k b -> p (k b)"), bank[6][:, 0:KD * B], ACT.Silu).then_inc(act_cs1, 1)
                mod_act(act, pe_mod1, act_mod1)
                for i_ in range(4):
                    act.wait_ge(pe_wt, i_ + 1)
                    nc.scalar.copy(w_t[:, i_].rearrange("p k d -> p (k d)"), bank[4 + i_ % 2][:, :]).then_inc(act_wt, 1)
                norm_act_sqrt(act, 2)
                norm_act_copy(act, 2, bank[0:2])

                def qk_copies(t):
                    for s_ in range(2):
                        act.wait_ge(pe_qk, 2 * t + s_ + 1)
                        nc.scalar.copy((q_t, k_t)[s_][:, :, t * P:(t + 1) * P],
                                       bank[4 + s_][:, :].rearrange("p (j q) -> p j q", j=4)).then_inc(act_qk, 1)

                for t in range(NT):
                    act.wait_ge(pe_qkv, t + 1)
                    nc.scalar.copy(v_sb[:, t, :], bank[2 + t % 2][:, 0:D]).then_inc(act_v, 1)
                    if t:
                        qk_copies(t - 1)
                qk_copies(NT - 1)

                def exps(u):
                    b, qt, js = units[u]
                    nk = P * (qt + 1)
                    for r in range(4):
                        act.wait_ge(dve_nm, 4 * u + r + 1)
                        if u:
                            act.wait_ge(pe_pt, 4 * (u - 1) + r + 1)
                        for i_, j in enumerate(js):
                            hd = 4 * j + r
                            last = nc.scalar.activation(prob_sb[:, r, i_ * nk:(i_ + 1) * nk], bank[r][:, i_ * nk:(i_ + 1) * nk],
                                                        ACT.Exp, bias=nmx[:, r, i_:i_ + 1], scale=DH ** -0.5,
                                                        accum_out=rs[:, 2 * b + qt, hd:hd + 1])
                        last.then_inc(act_p, 1)

                exps(0)
                for u in range(len(units)):
                    for r in (0, 2):
                        act.wait_ge(pe_pt, 4 * u + r + 1)
                        if u:
                            act.wait_ge(pe_pv, u)
                        nc.scalar.copy(prob_t[:, r], bank[4][:, :]).then_inc(act_pt, 1)
                        if r == 0 and u + 1 < len(units):
                            pass
                    if u + 1 < len(units):
                        exps(u + 1)
                    if units[u][2][-1] == 3:
                        t = 2 * units[u][0] + units[u][1]
                        act.wait_ge(pe_at, t + 1)
                        if t:
                            act.wait_ge(pe_wo, t)
                        nc.scalar.copy(att_t.rearrange("p k q -> p (k q)"), bank[7][:, 0:D]).then_inc(act_at, 1)

            @block.vector
            def _(dve):
                for t in range(NT):
                    nc.vector.tensor_tensor(y_acc[:, t, :], y_acc[:, t, :], mod[:, t // 2, 5 * D:6 * D],
                                            ALU.mult).then_inc(dve_res1, 1)
                for t in range(NT):
                    dve.wait_ge(dve_res1, t + 1)
                    nc.vector.tensor_tensor(x[:, t, :], x[:, t, :], y_acc[:, t, :], ALU.add).then_inc(dve_res1, 1)
                nc.vector.memset(qkp, 0.0).then_inc(dve_z, 1)
                dve.wait_ge(act_cs1, 1)
                dve.wait_ge(dve_res1, 2 * NT)
                nc.vector.tensor_copy(csb1, bc(c1_s.unsqueeze(3), [P, KD, B, P])).then_inc(dve_csb1, 1)
                mod_dve(dve, act_mod1, mscr, mod_chain1)
                norm_dve(dve, 2, 0, 1)
                dve.wait_ge(dve_z, 1)
                for t in range(NT):
                    c = t % 2
                    qk = bank[t % 2][:, :].rearrange("p (h d) -> p h d", d=DH)
                    n = 3 * t
                    dve.wait_ge(pe_qkv, t + 1)
                    if t:
                        dve.wait_ge(dve_qk, t)
                    nc.vector.tensor_tensor(r_a, qk, bc(rope[:, 0, c].unsqueeze(1), [P, 2 * AH, DH]),
                                            ALU.mult).then_inc(dve_ra, 1)
                    for o in range(2):
                        nc.vector.tensor_tensor(r_b[:, :, o::2], qk[:, :, 1 - o::2],
                                                bc(rope[:, 1, c, o::2].unsqueeze(1), [P, 2 * AH, DH // 2]),
                                                ALU.mult).then_inc(dve_ra, 1)
                    dve.wait_ge(dve_ra, n + 3)
                    if t >= 2:
                        dve.wait_ge(pe_qk, 2 * (t - 1))
                    nc.vector.tensor_tensor(qkp[:, t % 2].rearrange("p s h d -> p (s h) d")[:, :, 0:DH], r_a, r_b,
                                            ALU.add).then_inc(dve_qk, 1)

                def maxima(u):
                    b, qt, js = units[u]
                    nj, nk = len(js), P * (qt + 1)
                    for r in range(4):
                        v = 4 * u + r
                        s3 = bank[r][:, :].rearrange("p (j k) -> p j k", j=nj)
                        dve.wait_ge(pe_s, v + 1)
                        nc.vector.tensor_tensor(s3[:, :, qt * P:nk], s3[:, :, qt * P:nk],
                                                bc(neg_mask.unsqueeze(1), [P, nj, P]), ALU.add).then_inc(dve_mask, 1)
                        dve.wait_ge(dve_mask, v + 1)
                        if v >= 4:
                            dve.wait_ge(dve_nm, v - 3)
                        nc.vector.tensor_reduce(mx[:, r, 0:nj], s3, AX, ALU.max).then_inc(dve_mx, 1)
                        dve.wait_ge(dve_mx, v + 1)
                        if u:
                            dve.wait_ge(act_p, v - 3)
                        nc.vector.tensor_scalar(nmx[:, r, 0:nj], mx[:, r, 0:nj], -DH ** -0.5, None,
                                                ALU.mult).then_inc(dve_nm, 1)

                maxima(0)
                for u in range(len(units)):
                    if u + 1 < len(units):
                        maxima(u + 1)
                    for r in (1, 3):
                        dve.wait_ge(pe_pt, 4 * u + r + 1)
                        if u:
                            dve.wait_ge(pe_pv, u)
                        nc.vector.tensor_copy(prob_t[:, r], bank[5][:, :]).then_inc(dve_pt, 1)
                    if units[u][2][-1] == 3:
                        t = 2 * units[u][0] + units[u][1]
                        nc.vector.reciprocal(rrs[:, t, :], rs[:, t, :]).then_inc(dve_rr, 1)
                        dve.wait_ge(dve_rr, t + 1)
                        dve.wait_ge(pe_pv, u + 1)
                        if t:
                            dve.wait_ge(pe_at, t)
                        nc.vector.tensor_tensor(att.rearrange("p (h d) -> p h d", d=DH),
                                                bank[6][:, 0:D].rearrange("p (h d) -> p h d", d=DH),
                                                bc(rrs[:, t, :].unsqueeze(2), [P, AH, DH]), ALU.mult).then_inc(dve_att, 1)
                        dve.wait_ge(pe_wo, t + 1)
                        if t:
                            dve.wait_ge(dve_x, t)
                        nc.vector.tensor_tensor(otmp, bank[7][:, D:2 * D], mod[:, t // 2, 2 * D:3 * D],
                                                ALU.mult).then_inc(dve_o, 1)
                        dve.wait_ge(dve_o, t + 1)
                        nc.vector.tensor_tensor(x[:, t, :], x[:, t, :], otmp, ALU.add).then_inc(dve_x, 1)

        take = carver()
        r_raw = take(D, parts=E1)
        r_t = take(KD, E1)
        bias_row = take(E1)
        gu_t = take(2, 4, F1)
        dn_t = take(2, D)
        s_sb = take(2, 512)
        a_sb = take(2, 512)
        sc1, ch1, eq1, sel1, w1, comb = (take(NT, E1) for _ in range(6))
        s1, rc1 = take(NT), take(NT)
        m8 = take(NT, 8)
        i8 = take(NT, 8).bitcast(U32)
        i8f = take(NT, 8)
        names = ("ld_r pe_rt act_rt pe_lg act_sc dve_rt dve_comb pe_wg act_wg pe_wd act_wd pe_up act_s dve_a pe_dn "
                 "out_a out_d dve_fin dve_x ld_out").split()
        g_ = {n: sem("e_" + n) for n in names}
        (ld_r, pe_rt, act_rt, pe_lg1, act_sc, dve_rt1, dve_comb1, pe_wg, act_wg, pe_wd, act_wd, pe_up1, act_s1, dve_a1,
         pe_dn1, act_y1, dve_y1, dve_fin, dve_x1, st_out) = (g_[n] for n in names)
        order = [E1] + list(range(E1))
        NE = len(order)

        with nc.Block() as block:
            @block.sync
            def _(sp):
                sp.dma_start(r_raw, A["L1_ffn_router_w"]).then_inc(ld_r, 16)
                sp.dma_start(bias_row, A["L1_ffn_router_bias"].partition_broadcast(P)).then_inc(ld_r, 16)
                ov = out.rearrange("b (c p) d -> p (b c) d", p=P)
                for t in range(NT):
                    sp.wait_ge(dve_x1, t + 1)
                    sp.dma_start(ov[:, t, :], x[:, t, :]).then_inc(st_out, 16)
                sp.wait_ge(st_out, 16 * NT)

            @block.tensor
            def _(pe):
                pe.wait_ge(ld_r, 32)
                for k in range(KD):
                    last = nc.tensor.transpose(bank[4][:, k * E1:(k + 1) * E1], r_raw[:, k * P:(k + 1) * P],
                                               ident[0:E1, 0:E1])
                last.then_inc(pe_rt, 1)
                norm_pe(pe, 3, bank[0:2])
                pe.wait_ge(act_rt, 1)
                pe.wait_ge(norm_hT, 4 * NT // 2)
                for t in range(NT):
                    for k in range(KD):
                        last = nc.tensor.matmul(bank[5][:, t * E1:(t + 1) * E1], hT[:, k, t * P:(t + 1) * P],
                                                r_t[:, k, :], start=k == 0, stop=k == KD - 1)
                last.then_inc(pe_lg1, 1)
                pe.wait_ge(ld_w1, 16 * 6)

                def weights(n):
                    e = order[n]
                    if n:
                        pe.wait_ge(act_wg, n)
                        pe.wait_ge(act_wd, n)
                    for s_ in range(2):
                        for k in range(KD):
                            last = nc.tensor.transpose(bank[0][:, (2 * s_ + k) * P:(2 * s_ + k + 1) * P],
                                                       w1_raw[:, e, s_, k * P:(k + 1) * P], ident)
                    last.then_inc(pe_wg, 1)
                    for o in range(2):
                        last = nc.tensor.transpose(bank[1][:, o * P:(o + 1) * P], w1_down[:, e, o, :], ident)
                    last.then_inc(pe_wd, 1)

                def up(n, th):
                    u = 2 * n + th
                    pe.wait_ge(act_wg, n + 1)
                    if u >= 2:
                        pe.wait_ge(dve_a1, u - 1)
                    if u == 1:
                        pe.wait_ge(act_sc, 1)
                    for s_, bk in ((0, bank[2 + th]), (1, bank[4 + th])):
                        for k in range(KD):
                            last = nc.tensor.matmul(bk[:, :], gu_t[:, n % 2, 2 * s_ + k, :],
                                                    hT[:, k, th * 512:(th + 1) * 512], start=k == 0, stop=k == KD - 1)
                    last.then_inc(pe_up1, 1)

                def down(n, th):
                    u = 2 * n + th
                    pe.wait_ge(dve_a1, u + 1)
                    pe.wait_ge(act_wd, n + 1)
                    for pr in range(2):
                        v = 2 * u + pr
                        if v >= 2:
                            w = v - 2
                            pe.wait_ge(*((act_y1, w + 1) if w < 4 else (dve_y1, 2 * (w - 4) + 2)))
                        for q_ in range(2):
                            last = nc.tensor.matmul(bank[6 + pr][:, q_ * D:(q_ + 1) * D],
                                                    a_sb[:, th, (2 * pr + q_) * P:(2 * pr + q_ + 1) * P], dn_t[:, n % 2, :],
                                                    start=True, stop=True)
                        last.then_inc(pe_dn1, 1)

                weights(0)
                up(0, 0)
                up(0, 1)
                for n in range(NE):
                    if n + 1 < NE:
                        weights(n + 1)
                    down(n, 0)
                    if n + 1 < NE:
                        up(n + 1, 0)
                    down(n, 1)
                    if n + 1 < NE:
                        up(n + 1, 1)

            @block.scalar
            def _(act):
                norm_act_sqrt(act, 3)
                act.wait_ge(pe_rt, 1)
                nc.scalar.copy(r_t.rearrange("p k e -> p (k e)"), bank[4][:, 0:KD * E1]).then_inc(act_rt, 1)
                norm_act_copy(act, 3, bank[0:2])
                act.wait_ge(pe_lg1, 1)
                nc.scalar.activation(sc1.rearrange("p t e -> p (t e)"), bank[5][:, 0:P], ACT.Sigmoid).then_inc(act_sc, 1)

                def weights(n):
                    act.wait_ge(pe_wg, n + 1)
                    if n >= 2:
                        act.wait_ge(pe_up1, 2 * (n - 1))
                    nc.scalar.copy(gu_t[:, n % 2].rearrange("p a b -> p (a b)"), bank[0][:, :]).then_inc(act_wg, 1)
                    act.wait_ge(pe_wd, n + 1)
                    if n >= 2:
                        act.wait_ge(pe_dn1, 4 * (n - 1))
                    nc.scalar.copy(dn_t[:, n % 2], bank[1][:, 0:D]).then_inc(act_wd, 1)

                weights(0)
                for n in range(NE):
                    for th in range(2):
                        u = 2 * n + th
                        act.wait_ge(pe_up1, u + 1)
                        if u >= 2:
                            act.wait_ge(dve_a1, u - 1)
                        nc.scalar.activation(s_sb[:, th], bank[2 + th][:, :], ACT.Silu).then_inc(act_s1, 1)
                        if th == 0 and n + 1 < NE:
                            weights(n + 1)
                    if n == 0:
                        for v in range(4):
                            act.wait_ge(pe_dn1, v + 1)
                            nc.scalar.copy(y_acc[:, 2 * v:2 * v + 2, :],
                                           bank[6 + v % 2][:, :].rearrange("p (a b) -> p a b", a=2)).then_inc(act_y1, 1)

            @block.vector
            def _(dve):
                norm_dve(dve, 3, 3, 4)

                def product(u):
                    th = u % 2
                    dve.wait_ge(act_s1, u + 1)
                    if u >= 2:
                        dve.wait_ge(pe_dn1, 2 * (u - 1))
                    nc.vector.tensor_tensor(a_sb[:, th], bank[4 + th][:, :], s_sb[:, th], ALU.mult).then_inc(dve_a1, 1)

                def sums(u):
                    n, th = u // 2, u % 2
                    e = order[n]
                    for pr in range(2):
                        v = 2 * u + pr
                        dve.wait_ge(pe_dn1, v + 1)
                        for q_ in range(2):
                            t = 4 * th + 2 * pr + q_
                            if n >= 2:
                                dve.wait_ge(dve_y1, NT * (n - 2) + t + 1)
                            nc.vector.scalar_tensor_tensor(out=y_acc[:, t, :], in0=bank[6 + pr][:, q_ * D:(q_ + 1) * D],
                                                           scalar=comb[:, t, e:e + 1], in1=y_acc[:, t, :],
                                                           op0=ALU.mult, op1=ALU.add).then_inc(dve_y1, 1)

                product(0)
                product(1)
                dve.wait_ge(ld_r, 32)
                dve.wait_ge(act_sc, 1)
                nc.vector.tensor_tensor(ch1, sc1, bc(bias_row.unsqueeze(1), [P, NT, E1]), ALU.add).then_inc(dve_rt1, 1)
                dve.wait_ge(dve_rt1, 1)
                n = topk_select(dve, ch1, K1, dve_rt1, 1, eq1, sel1, m8, i8, i8f)
                dve.wait_ge(dve_rt1, n)
                nc.vector.tensor_tensor(w1, sc1, sel1, ALU.mult).then_inc(dve_rt1, 1)
                dve.wait_ge(dve_rt1, n + 1)
                nc.vector.tensor_reduce(s1, w1, AX, ALU.add).then_inc(dve_rt1, 1)
                dve.wait_ge(dve_rt1, n + 2)
                nc.vector.tensor_scalar(s1, s1, 1e-20, None, ALU.add).then_inc(dve_rt1, 1)
                dve.wait_ge(dve_rt1, n + 3)
                nc.vector.reciprocal(rc1, s1).then_inc(dve_rt1, 1)
                dve.wait_ge(dve_rt1, n + 4)
                nc.vector.tensor_tensor(comb, w1, bc(rc1.unsqueeze(2), [P, NT, E1]), ALU.mult).then_inc(dve_comb1, 1)
                dve.wait_ge(dve_comb1, 1)
                dve.wait_ge(act_y1, 4)
                for u in range(2, 2 * NE):
                    product(u)
                    if u >= 3:
                        sums(u - 1)
                sums(2 * NE - 1)
                for t in range(NT):
                    dve.wait_ge(dve_y1, NT * (NE - 2) + t + 1)
                    nc.vector.tensor_tensor(y_acc[:, t, :], y_acc[:, t, :], mod[:, t // 2, 5 * D:6 * D],
                                            ALU.mult).then_inc(dve_fin, 1)
                for t in range(NT):
                    dve.wait_ge(dve_fin, t + 1)
                    nc.vector.tensor_tensor(x[:, t, :], x[:, t, :], y_acc[:, t, :], ALU.add).then_inc(dve_x1, 1)


_INS = ['L0_attn_hidden_states', 'L0_attn_Wz', 'L0_attn_Wx', 'L0_attn_WB', 'L0_attn_WC', 'L0_attn_Wdt',
        'L0_attn_conv_w', 'L0_attn_conv_b', 'L0_attn_dt_bias', 'L0_attn_A_log', 'L0_attn_D', 'L0_attn_norm_w',
        'L0_attn_Wout', 'L0_ffn_gate_w', 'L0_ffn_w_gate', 'L0_ffn_w_up', 'L0_ffn_w_down', 'L0_ffn_ws_gate',
        'L0_ffn_ws_up', 'L0_ffn_ws_down', 'L0_c', 'L0_wmod', 'L1_attn_Wq', 'L1_attn_Wk', 'L1_attn_Wv', 'L1_attn_Wo',
        'L1_ffn_router_w', 'L1_ffn_router_bias', 'L1_ffn_expert_gate_w', 'L1_ffn_expert_up_w',
        'L1_ffn_expert_down_w', 'L1_ffn_shared_gate_w', 'L1_ffn_shared_up_w', 'L1_ffn_shared_down_w', 'L1_c',
        'L1_wmod']


def constants():
    import numpy as np
    k = np.arange(P)[:, None]
    j = np.arange(P)[None, :]
    c = np.zeros((P, C_ALL), np.float32)
    c[:, C_ID:C_ID + P] = k == j
    c[:, C_GT:C_GT + P] = k > j
    c[:, C_LE:C_LE + P] = k <= j
    c[:, C_ONE:C_ONE + P] = 1.0
    c[:, C_LE2:C_LE2 + P] = k <= j
    c[:, C_LT:C_LT + P] = k < j
    c[:, C_NEG:C_NEG + P] = np.where(j > k, -1e30, 0.0)
    c[:, C_IOTA:C_IOTA + P] = np.broadcast_to(j, (P, P))
    theta = (np.float32(10000.0) ** (np.float32(-2.0) * np.arange(DH // 2, dtype=np.float32) / np.float32(DH)))
    ang = np.arange(S, dtype=np.float32)[:, None] * theta.astype(np.float32)[None, :]
    cos, sin = np.cos(ang).astype(np.float32), np.sin(ang).astype(np.float32)
    tab = np.zeros((2, S, DH), np.float32)
    tab[0, :, 0::2] = cos
    tab[0, :, 1::2] = cos
    tab[1, :, 0::2] = -sin
    tab[1, :, 1::2] = sin
    c[:, C_ROPE:] = tab.reshape(2, 2, P, DH).transpose(2, 0, 1, 3).reshape(P, -1)
    return c


def kernel(**inputs):
    import numpy as _np
    import concourse.bacc as _bacc
    from concourse import mybir as _mybir
    from concourse.bass_utils import run_bass_kernel_spmd as _run

    nc = _bacc.Bacc("TRN2", target_bir_lowering=False, num_devices=1)
    arrays, aps = {}, {}
    for name in _INS:
        a = _np.ascontiguousarray(inputs[name])
        arrays[f"in_{name}"] = a
        aps[name] = nc.dram_tensor(f"in_{name}", a.shape, _mybir.dt.from_np(a.dtype), kind="ExternalInput").ap()
    arrays["const_in"] = constants()
    aps["const"] = nc.dram_tensor("const_in", arrays["const_in"].shape, F32, kind="ExternalInput").ap()
    out = nc.dram_tensor("out_0", (B, S, D), F32, kind="ExternalOutput").ap()
    build(nc, aps, out)
    r = _run(nc, [arrays], core_ids=[0])
    return r.results[0]["out_0"]
```

```python
from contextlib import ExitStack

import concourse.bass as bass
from concourse import mybir

F32 = mybir.dt.float32
F32R = mybir.dt.float32r
U32 = mybir.dt.uint32
ALU = mybir.AluOpType
ACT = mybir.ActivationFunctionType
AX = mybir.AxisListType.X

P = 128
B, S, D = 4, 256, 256
NT = B * S // P
KD = D // P
HEADS, HD, GROUPS, NST = 64, 64, 8, 128
HG = HEADS // GROUPS
GC = HG * HD
XT = GC // P
TAPS = 4
INTER = HEADS * HD
E0, I0, CAP, IT = 16, 176, 128, 88
IS = 352
NIS = IS // IT
E1, F1, K1 = 16, 128, 4
AH, DH = 16, 16
EPS = 1e-5
CT = (INTER + 2 * GROUPS * NST) // P
COLS = (TAPS + 1) * CT + 2 * (INTER // P) + 2 * KD * B
C_ID, C_GT, C_LE, C_ONE, C_LE2, C_LT, C_NEG, C_IOTA, C_ROPE = [P * i for i in range(9)]
C_ALL = C_ROPE + 2 * 2 * DH
ARENA = 23610
HALVES = 14340


def bc(ap, shape):
    return ap.broadcast_to(shape)


def build(nc, A, out):
    with ExitStack() as ctx:
        def sb(name, shape, dt=F32):
            return ctx.enter_context(nc.sbuf_tensor(name, shape, dt))

        def sem(name):
            return ctx.enter_context(nc.semaphore(name))

        bank = [ctx.enter_context(nc.psum_tensor(f"bank{i}", [P, 512], F32)) for i in range(8)]
        const = sb("const", [P, C_ALL])
        ident = const[:, C_ID:C_ID + P]
        tri_gt = const[:, C_GT:C_GT + P]
        tri_le = const[:, C_LE:C_LE + P]
        ones = const[:, C_ONE:C_ONE + P]
        causal3 = const[:, C_LE:C_LE + 3 * P]
        tri_lt = const[:, C_LT:C_LT + P]
        neg_mask = const[:, C_NEG:C_NEG + P]
        iota = const[:, C_IOTA:C_IOTA + P]
        rope = const[:, C_ROPE:C_ALL].rearrange("p (s c d) -> p s c d", s=2, c=2)
        x = sb("x", [P, NT, D])
        h = sb("h", [P, NT, D])
        hT_hi = sb("hT_hi", [P, KD, NT * P], F32R)
        hT_lo = sb("hT_lo", [P, KD, NT * P], F32R)
        tri_gt_r = sb("tri_gt_r", [P, P], F32R)
        cs = sb("cs", [P, 2 * KD * B])
        mod = sb("mod", [P, B, 3 * D])
        stats = sb("stats", [P, NT, 6])
        mv = sb("mv", [P, NT, 2])
        rstd = sb("rstd", [P, NT])
        std = sb("std", [P, NT])
        nmr = sb("nmr", [P, NT])
        y_acc = sb("y_acc", [P, NT, D])
        ss = sb("ss", [P, NT, GROUPS])
        arena = sb("arena", [P, ARENA])
        halves = sb("halves", [P, HALVES], F32R)

        def carver(arena=arena, size=ARENA):
            at = [0]

            def take(*shape, parts=P):
                n = 1
                for s in shape:
                    n *= s
                assert at[0] + n <= size, at[0] + n
                v = arena[0:parts, at[0]:at[0] + n]
                at[0] += n
                if len(shape) == 1:
                    return v
                names = "abcd"[:len(shape)]
                return v.rearrange("p (" + " ".join(names) + ") -> p " + " ".join(names),
                                   **{c: s for c, s in zip(names, shape)})
            return take

        norm_chain = sem("norm_chain")
        norm_std = sem("norm_std")
        norm_x = sem("norm_x")
        norm_h = sem("norm_h")
        norm_tr = sem("norm_tr")
        norm_hi = sem("norm_hi")
        norm_hT = sem("norm_hT")
        ld_ss, ld_gt = sem("ld_ss"), sem("ld_gt")

        NC = 3 * NT + 3

        def norm_stats(n, t):
            nc.vector.bn_stats(stats[:, t, :], x[:, t, :]).then_inc(norm_chain, 1)

        def norm_dve(dve, n):
            n0 = n * NC
            for t in range(NT):
                dve.wait_ge(norm_chain, n0 + t + 1)
                nc.vector.bn_aggr(mv[:, t, :], stats[:, t, :]).then_inc(norm_chain, 1)
            dve.wait_ge(norm_chain, n0 + 2 * NT)
            nc.vector.tensor_scalar(std[:, :], mv[:, :, 1], EPS, None, ALU.add).then_inc(norm_chain, 1)
            dve.wait_ge(norm_std, n + 1)
            nc.vector.reciprocal(rstd[:, :], std[:, :]).then_inc(norm_chain, 1)
            dve.wait_ge(norm_chain, n0 + 2 * NT + 2)
            nc.vector.scalar_tensor_tensor(out=nmr[:, :], in0=mv[:, :, 0], scalar=-1.0, in1=rstd[:, :],
                                           op0=ALU.mult, op1=ALU.mult).then_inc(norm_chain, 1)
            dve.wait_ge(ld_ss, 16 * (n + 1))
            for t in range(NT):
                dve.wait_ge(norm_x, n * NT + t + 1)
                nc.vector.tensor_tensor(h[:, t, :], h[:, t, :], mod[:, t // 2, D:2 * D], ALU.mult).then_inc(norm_chain, 1)

        def norm_pool(pool, n):
            pool.wait_ge(ld_ss, 16 * (n + 1))
            for t in range(NT):
                pool.wait_ge(norm_chain, n * NC + 2 * NT + 3 + t + 1)
                nc.gpsimd.tensor_tensor(h[:, t, :], h[:, t, :], mod[:, t // 2, 0:D], ALU.add).then_inc(norm_h, 1)

        def norm_dve_lo(dve, n, banks):
            for j in range(NT // 2):
                dve.wait_ge(norm_hi, n * NT // 2 + j + 1)
                cols = slice(2 * j * P, (2 * j + 2) * P)
                nc.vector.tensor_tensor(hT_lo[:, :, cols], banks[j % 2][:, :].rearrange("p (k t) -> p k t", k=KD),
                                        hT_hi[:, :, cols].bitcast(F32), ALU.subtract).then_inc(norm_hT, 1)

        def norm_act(act, n):
            act.wait_ge(norm_chain, n * NC + 2 * NT + 1)
            nc.scalar.activation(std[:, :], std[:, :], ACT.Sqrt).then_inc(norm_std, 1)
            act.wait_ge(norm_chain, n * NC + 2 * NT + 3)
            for t in range(NT):
                nc.scalar.activation(h[:, t, :], x[:, t, :], ACT.Identity, bias=nmr[:, t:t + 1],
                                     scale=rstd[:, t:t + 1]).then_inc(norm_x, 1)

        def norm_pe(pe, n, banks):
            for j in range(NT // 2):
                pe.wait_ge(norm_h, n * NT + 2 * j + 2)
                if j >= 2:
                    pe.wait_ge(norm_hT, n * NT // 2 + j - 1)
                for k in range(KD):
                    for q in range(2):
                        last = nc.tensor.transpose(banks[j % 2][:, (2 * k + q) * P:(2 * k + q + 1) * P],
                                                   h[:, 2 * j + q, k * P:(k + 1) * P], ident)
                last.then_inc(norm_tr, 1)

        def norm_act_copy(act, n, banks):
            for j in range(NT // 2):
                act.wait_ge(norm_tr, n * NT // 2 + j + 1)
                nc.scalar.copy(hT_hi[:, :, 2 * j * P:(2 * j + 2) * P],
                               banks[j % 2][:, :].rearrange("p (k t) -> p k t", k=KD)).then_inc(norm_hi, 1)

        def mm3(out, left, right, first, last):
            nc.tensor.matmul(out, left[0], right[0], start=first, stop=False)
            nc.tensor.matmul(out, left[0], right[1], start=False, stop=False)
            return nc.tensor.matmul(out, left[1], right[0], start=False, stop=last)

        rows = A["mod_rows"]
        pe_mod, mod_chain, st_mod, ld_mod1 = sem("pe_mod"), sem("mod_chain"), sem("st_mod"), sem("ld_mod1")
        MC = 9

        def load_shift_scale(eng, m):
            eng.dma_start(mod[:, :, 0:2 * D], rows[m // 2, :, m % 2 * 3 * D:(m % 2 * 3 + 2) * D]
                          .partition_broadcast(P)).then_inc(ld_ss, 16)

        def load_gate(eng, m):
            eng.dma_start(mod[:, :, 2 * D:3 * D], rows[m // 2, :, (m % 2 * 3 + 2) * D:(m % 2 * 3 + 3) * D]
                          .partition_broadcast(P)).then_inc(ld_gt, 16)

        take = carver()
        raw_x = take(KD, GC)
        raw_b = take(KD, NST)
        raw_c = take(KD, NST)
        raw_z = take(KD, GC)
        w_out = take(2, XT, D)
        cols = take(COLS)
        conv_w = cols[:, 0:TAPS * CT].rearrange("p (k t) -> p t k", k=TAPS)
        conv_b = cols[:, TAPS * CT:(TAPS + 1) * CT]
        norm_w = cols[:, (TAPS + 1) * CT:(TAPS + 1) * CT + INTER // P]
        d_col = cols[:, COLS - 2 * KD * B - INTER // P:COLS - 2 * KD * B]
        c_t = cols[:, COLS - 2 * KD * B:COLS]
        a_log = take(HEADS)
        dt_bias = take(HEADS)
        dt = take(NT, HEADS)
        la = take(2, NT, HEADS)
        dte = take(B, HEADS)
        ef = take(B, HEADS)
        base = take(1).offset % ARENA
        xc = take(2, 6, S)
        acc = take(3, 2, S)
        ebuf = take(2, 4, P)
        mbuf = take(2, 4, 4, P)
        xtok = take(2, GC)
        xd = take(2, GC)
        xe = take(GC)
        gm = take(2, 3 * P)
        gt = take(2, XT, S)
        la_wide = take(GC)
        sg = h[:, :, :].rearrange("p (i m) d -> p i m d", i=2)
        sq = mod[:, :, 0:S]
        ef_t = mod[:, :, S:S + P]
        off = mod[:, :, S + P:S + 2 * P]
        takeh = carver(halves, HALVES)
        w_x = takeh(2, 2, KD, GC)
        w_b = takeh(2, 2, KD, NST)
        w_c = takeh(2, 2, KD, NST)
        w_z = takeh(2, 2, KD, GC)
        rbuf = takeh(2, 4, 4, P)
        take_t = carver()
        take_t(base)
        wmod = take_t(2, KD, 6 * D)
        mrow = take_t(2, 6 * D, parts=B)
        wdt = take_t(KD, HEADS)
        tmp = [take_t(NT * HEADS) for _ in range(7)]
        conv_raw = take_t(P * TAPS, parts=CT)
        conv_w_raw = conv_raw.rearrange("t (p k) -> t k p", k=TAPS)
        conv_b_raw = take_t(P, parts=CT)
        norm_w_raw = take_t(P, parts=INTER // P)
        d_raw = take_t(HG // XT, parts=INTER // P)
        d_wide = take_t(P, parts=INTER // P)
        c_raw = take_t(2, D, parts=B)
        mscr = take_t(2, D, parts=B)
        la_r = sb("la_r", [P, NT, HEADS], F32R)
        wdt_r = rbuf[:, 0, 0, :].rearrange("p s (k n) -> p s k n", k=KD)

        (ld_x, ld_const, ld_mod, ld_row, ld_conv, act_cs, dt_chain, act_exp, pe_dt, pe_ef, act_ef,
         dve_setup, pe_cols, act_cols, dve_alog, act_wdt, dve_wdt, ld_a, act_whi, pool_wlo, dve_dw) = (
            sem(n) for n in "ld_x ld_const ld_mod ld_row ld_conv act_cs dt_chain act_exp pe_dt pe_ef act_ef "
            "dve_setup pe_cols act_cols dve_alog act_wdt dve_wdt ld_a act_whi pool_wlo dve_dw".split())

        x_in = A["L0_attn_hidden_states"].rearrange("b (c p) d -> p (b c) d", p=P)
        ld_o = [sem("ld_o_even"), sem("ld_o_odd")]
        NW = 4
        parts = ((raw_x, w_x), (raw_b, w_b), (raw_c, w_c), (raw_z, w_z))

        def load_group(eng, g):
            for raw, nm, n in ((raw_x, "L0_attn_Wx", GC), (raw_b, "L0_attn_WB", NST), (raw_c, "L0_attn_WC", NST),
                               (raw_z, "L0_attn_Wz", GC)):
                eng.dma_start(raw, A[nm][:, g * n:(g + 1) * n].rearrange("(k p) n -> p k n", p=P)).then_inc(ld_a, 16)

        def load_out(eng, g):
            eng.dma_start(w_out[:, g % 2], A["L0_attn_Wout"][g * GC:(g + 1) * GC, :]
                          .rearrange("(k p) n -> p k n", p=P)).then_inc(ld_o[g % 2], 16)

        def split_hi(act, g):
            act.wait_ge(ld_a, 16 * NW * (g + 1))
            for raw, w in parts:
                nc.scalar.copy(w[:, g % 2, 0], raw).then_inc(act_whi, 1)

        def split_lo(pool, g):
            for i_, (raw, w) in enumerate(parts):
                pool.wait_ge(act_whi, NW * g + i_ + 1)
                nc.gpsimd.tensor_tensor(w[:, g % 2, 1], raw, w[:, g % 2, 0].bitcast(F32),
                                        ALU.subtract).then_inc(pool_wlo, 1)

        mod_bank = (bank[2], bank[3], bank[7])

        def mod_final(dve, layer):
            b0, b1, b2 = mod_bank
            row = mrow[:, layer]
            dve.wait_ge(pe_mod, layer + 1)
            nc.vector.tensor_copy(row[:, 0:D], b0[0:B, 0:D]).then_inc(mod_chain, 1)
            nc.vector.tensor_scalar(row[:, D:2 * D], b0[0:B, D:2 * D], 1.0, None, ALU.add).then_inc(mod_chain, 1)
            nc.vector.tensor_copy(row[:, 2 * D:4 * D], b1[0:B, :]).then_inc(mod_chain, 1)
            nc.vector.tensor_scalar(row[:, 4 * D:5 * D], b2[0:B, 0:D], 1.0, None, ALU.add).then_inc(mod_chain, 1)
            nc.vector.tensor_copy(row[:, 5 * D:6 * D], b2[0:B, D:2 * D]).then_inc(mod_chain, 1)
            g = row.rearrange("b (s r d) -> b s r d", s=2, r=3)[:, :, 2, :]
            n0 = MC * layer
            dve.wait_ge(mod_chain, n0 + 5)
            nc.vector.tensor_scalar(mscr, g, 0.0, 2.0, ALU.is_ge, ALU.mult).then_inc(mod_chain, 1)
            dve.wait_ge(mod_chain, n0 + 6)
            nc.vector.tensor_scalar(mscr, mscr, -1.0, None, ALU.add).then_inc(mod_chain, 1)
            dve.wait_ge(mod_chain, n0 + 7)
            nc.vector.tensor_tensor(g, g, mscr, ALU.mult).then_inc(mod_chain, 1)
            dve.wait_ge(mod_chain, n0 + 8)
            nc.vector.scalar_tensor_tensor(out=g, in0=g, scalar=0.25, in1=mscr,
                                           op0=ALU.max, op1=ALU.mult).then_inc(mod_chain, 1)

        with nc.Block() as block:
            @block.sync
            def _(sp):
                sp.dma_start(c_raw[:, 0], A["L0_c"]).then_inc(ld_conv, 16)
                sp.dma_start(c_raw[:, 1], A["L1_c"]).then_inc(ld_conv, 16)
                sp.dma_start(conv_raw, A["L0_attn_conv_w"].rearrange("(t p) k -> t (p k)", p=P)).then_inc(ld_conv, 16)
                sp.dma_start(conv_b_raw, A["L0_attn_conv_b"].rearrange("(t p) -> t p", p=P)).then_inc(ld_conv, 16)
                sp.dma_start(norm_w_raw, A["L0_attn_norm_w"].rearrange("(t p) -> t p", p=P)).then_inc(ld_conv, 16)
                sp.dma_start(d_raw, A["L0_attn_D"].rearrange("(t a) -> t a", a=HG // XT)).then_inc(ld_conv, 16)
                sp.dma_start(const[:, :], A["const"]).then_inc(ld_const, 16)
                sp.dma_start(wmod[:, 0], A["L0_wmod"].rearrange("(k p) n -> p k n", p=P)).then_inc(ld_mod, 16)
                sp.dma_start(x[:, :, :], x_in).then_inc(ld_x, 16)
                sp.dma_start(wdt, A["L0_attn_Wdt"].rearrange("(k p) n -> p k n", p=P)).then_inc(ld_row, 16)
                sp.dma_start(a_log, A["L0_attn_A_log"].partition_broadcast(P)).then_inc(ld_row, 16)
                sp.dma_start(dt_bias, A["L0_attn_dt_bias"].partition_broadcast(P)).then_inc(ld_row, 16)
                load_group(sp, 0)
                sp.dma_start(wmod[:, 1], A["L1_wmod"].rearrange("(k p) n -> p k n", p=P)).then_inc(ld_mod1, 16)
                load_out(sp, 0)
                load_out(sp, 1)
                for layer in range(2):
                    sp.wait_ge(mod_chain, MC * (layer + 1))
                    sp.dma_start(rows[layer], mrow[:, layer]).then_inc(st_mod, 16)
                    if layer == 0:
                        sp.wait_ge(st_mod, 16)
                        load_shift_scale(sp, 0)
                        load_gate(sp, 0)
                sp.wait_ge(st_mod, 32)

            @block.scalar
            def _(act):
                act.wait_ge(pe_cols, 1)
                nc.scalar.copy(cols, bank[6][:, 0:COLS]).then_inc(act_cols, 1)
                act.wait_ge(act_cols, 1)
                nc.scalar.activation(cs[:, :], c_t, ACT.Silu).then_inc(act_cs, 1)
                norm_act(act, 0)
                act.wait_ge(ld_row, 48)
                nc.scalar.copy(wdt_r[:, 0], wdt).then_inc(act_wdt, 1)
                norm_act_copy(act, 0, bank[0:2])
                act.wait_ge(dve_alog, 1)
                nc.scalar.activation(a_log, a_log, ACT.Exp).then_inc(act_exp, 1)
                split_hi(act, 0)
                act.wait_ge(dt_chain, 2)
                nc.scalar.activation(tmp[1], tmp[1], ACT.Exp).then_inc(act_exp, 1)
                act.wait_ge(pe_ef, 1)
                nc.scalar.activation(ef.rearrange("p b h -> p (b h)"), bank[5][:, 0:B * HEADS], ACT.Exp).then_inc(act_ef, 1)

            @block.gpsimd
            def _(pool):
                norm_pool(pool, 0)
                split_lo(pool, 0)

            @block.tensor
            def _(pe):
                pe.wait_ge(ld_const, 16)
                pe.wait_ge(ld_conv, 96)
                for k in range(TAPS):
                    nc.tensor.transpose(bank[6][:, k * CT:(k + 1) * CT], conv_w_raw[:, k, :], ident[0:CT, 0:CT])
                nc.tensor.transpose(bank[6][:, TAPS * CT:(TAPS + 1) * CT], conv_b_raw, ident[0:CT, 0:CT])
                n0 = (TAPS + 1) * CT
                nc.tensor.transpose(bank[6][:, n0:n0 + INTER // P], norm_w_raw, ident[0:INTER // P, 0:INTER // P])
                n0 += INTER // P
                pe.wait_ge(dve_dw, 1)
                nc.tensor.transpose(bank[6][:, n0:n0 + INTER // P], d_wide, ident[0:INTER // P, 0:INTER // P])
                n0 += INTER // P
                for k in range(2 * KD):
                    last = nc.tensor.transpose(bank[6][:, n0 + k * B:n0 + (k + 1) * B],
                                               c_raw[:, k // KD, k % KD * P:(k % KD + 1) * P], ident[0:B, 0:B])
                last.then_inc(pe_cols, 1)
                pe.wait_ge(ld_mod, 16)
                pe.wait_ge(act_cs, 1)

                def mod_products(layer):
                    for n in range(3):
                        for k in range(KD):
                            c0 = (layer * KD + k) * B
                            last = nc.tensor.matmul(mod_bank[n][0:B, :], cs[:, c0:c0 + B],
                                                    wmod[:, layer, k, n * 512:(n + 1) * 512], start=k == 0, stop=k == KD - 1)
                    last.then_inc(pe_mod, 1)

                mod_products(0)
                norm_pe(pe, 0, bank[0:2])
                pe.wait_ge(dve_wdt, 1)
                pe.wait_ge(norm_hT, NT // 2)
                for t in range(NT):
                    for k in range(KD):
                        ts = slice(t * P, (t + 1) * P)
                        last = mm3(bank[4][:, t * HEADS:(t + 1) * HEADS], (hT_hi[:, k, ts], hT_lo[:, k, ts]),
                                   (wdt_r[:, 0, k, :], wdt_r[:, 1, k, :]), k == 0, k == KD - 1)
                last.then_inc(pe_dt, 1)
                pe.wait_ge(ld_mod1, 16)
                pe.wait_ge(mod_chain, MC)
                mod_products(1)
                pe.wait_ge(dve_setup, 1)
                for b in range(B):
                    last = nc.tensor.matmul(bank[5][:, b * HEADS:(b + 1) * HEADS], tri_gt, la[:, 0, 2 * b, :],
                                            start=True, stop=True)
                last.then_inc(pe_ef, 1)

            @block.vector
            def _(dve):
                dve.wait_ge(ld_conv, 96)
                nc.vector.tensor_copy(d_wide.rearrange("t (a d) -> t a d", d=HD),
                                      bc(d_raw.unsqueeze(2), [INTER // P, HG // XT, HD])).then_inc(dve_dw, 1)
                nc.vector.memset(y_acc[:, :, :], 0.0)
                dve.wait_ge(ld_const, 16)
                nc.vector.tensor_copy(tri_gt_r[:, :], tri_gt)
                dve.wait_ge(ld_row, 48)
                nc.vector.tensor_scalar(a_log, a_log, 88.0, None, ALU.min).then_inc(dve_alog, 1)
                dve.wait_ge(ld_x, 16)
                for t in range(NT):
                    norm_stats(0, t)
                mod_final(dve, 0)
                norm_dve(dve, 0)
                dve.wait_ge(act_wdt, 1)
                nc.vector.tensor_tensor(wdt_r[:, 1], wdt, wdt_r[:, 0].bitcast(F32), ALU.subtract).then_inc(dve_wdt, 1)
                norm_dve_lo(dve, 0, bank[0:2])
                mod_final(dve, 1)
                dve.wait_ge(pe_dt, 1)
                v3 = [t_.rearrange("p (t n) -> p t n", t=NT) for t_ in tmp]
                nc.vector.tensor_tensor(v3[0], bank[4][:, :].rearrange("p (t n) -> p t n", t=NT),
                                        bc(dt_bias.unsqueeze(1), [P, NT, HEADS]), ALU.add).then_inc(dt_chain, 1)
                dve.wait_ge(dt_chain, 1)
                nc.vector.scalar_tensor_tensor(out=tmp[1], in0=tmp[0], scalar=-1.0, in1=tmp[0],
                                               op0=ALU.mult, op1=ALU.min).then_inc(dt_chain, 1)
                nc.vector.tensor_scalar(tmp[2], tmp[0], 0.0, None, ALU.max).then_inc(dt_chain, 1)
                dve.wait_ge(act_exp, 2)
                nc.vector.tensor_scalar(tmp[3], tmp[1], 2.0, None, ALU.add).then_inc(dt_chain, 1)
                dve.wait_ge(dt_chain, 4)
                nc.vector.reciprocal(tmp[3], tmp[3]).then_inc(dt_chain, 1)
                dve.wait_ge(dt_chain, 5)
                nc.vector.tensor_tensor(tmp[4], tmp[1], tmp[3], ALU.mult).then_inc(dt_chain, 1)
                dve.wait_ge(dt_chain, 6)
                nc.vector.tensor_tensor(tmp[5], tmp[4], tmp[4], ALU.mult).then_inc(dt_chain, 1)
                dve.wait_ge(dt_chain, 7)
                nc.vector.tensor_scalar(tmp[6], tmp[5], 1.0 / 17, None, ALU.mult).then_inc(dt_chain, 1)
                n = 8
                for odd in (15, 13, 11, 9, 7, 5, 3):
                    dve.wait_ge(dt_chain, n)
                    nc.vector.scalar_tensor_tensor(out=tmp[6], in0=tmp[6], scalar=1.0 / odd, in1=tmp[5],
                                                   op0=ALU.add, op1=ALU.mult).then_inc(dt_chain, 1)
                    n += 1
                dve.wait_ge(dt_chain, n)
                nc.vector.scalar_tensor_tensor(out=tmp[6], in0=tmp[6], scalar=1.0, in1=tmp[4],
                                               op0=ALU.add, op1=ALU.mult).then_inc(dt_chain, 1)
                dve.wait_ge(dt_chain, n + 1)
                dtf = dt.rearrange("p t n -> p (t n)")
                nc.vector.scalar_tensor_tensor(out=dtf, in0=tmp[6], scalar=2.0, in1=tmp[2],
                                               op0=ALU.mult, op1=ALU.add).then_inc(dt_chain, 1)
                dve.wait_ge(dt_chain, n + 2)
                nc.vector.tensor_tensor(la[:, 0], dt, bc(a_log.unsqueeze(1), [P, NT, HEADS]), ALU.mult).then_inc(dt_chain, 1)
                dve.wait_ge(dt_chain, n + 3)
                nc.vector.tensor_scalar(la[:, 0], la[:, 0], -1.0, -1.0e4, ALU.mult, ALU.max).then_inc(dve_setup, 1)
                dve.wait_ge(dve_setup, 1)
                nc.vector.tensor_copy(la_r[:, :, :], la[:, 0]).then_inc(dve_setup, 1)
                dve.wait_ge(dve_setup, 2)
                nc.vector.tensor_tensor(la[:, 1], la[:, 0], la_r[:, :, :].bitcast(F32), ALU.subtract).then_inc(dve_setup, 1)
                dve.wait_ge(act_ef, 1)
                nc.vector.tensor_tensor(dte, ef, dt.rearrange("p (b c) n -> p b c n", c=2)[:, :, 0, :],
                                        ALU.mult).then_inc(dve_setup, 1)

        names = ("pe_conv act_tap dve_chain dve_conv act_xc pe_gate act_sg pe_g dve_gm pe_xt act_xt pool_xd "
                 "pool_xe pool_r pe_l act_e dve_m pe_y dve_y pe_off dve_off dve_g pool_g pe_ef act_ef act_law act_sq "
                 "pe_out dve_out pool_w").split()
        q = {n: sem("m_" + n) for n in names}
        (pe_conv, act_tap, dve_chain, dve_conv, act_xc, pe_gate, act_sg, pe_g, dve_gm, pe_xt, act_xt, pool_xd,
         pool_xe, pool_r, pe_l, act_e, dve_m, pe_y, dve_y, pe_off, dve_off, dve_g, pool_g, pe_eft, act_eft, act_law, act_sq,
         pe_out, dve_out, pool_w) = (q[n] for n in names)
        P0, P1, W0, W1, TB, Y0, Y1, OB = bank
        STEPS = GROUPS * B
        proj = (P0, P1)
        work = (W0, W1)
        U_X, U_EF, U_L, U_OFF = 0, 2, 3, 7

        def conv_tile(g, m):
            return XT * g + m if m < XT else (32 + g if m == XT else 40 + g)

        def pair_of(i, k):
            return proj[(5 * i + k) % 2]

        def tiles(ap):
            return ap.rearrange("p (m t) -> p m t", m=XT)

        with nc.Block() as block:
            @block.sync
            def _(sp):
                for g in range(1, GROUPS):
                    sp.wait_ge(pool_wlo, NW * g)
                    load_group(sp, g)
                    if g >= 2:
                        sp.wait_ge(pe_out, B * (g - 1))
                        load_out(sp, g)

            @block.tensor
            def _(pe):
                def project(i, k_):
                    g, b = i // B, i % B
                    if b == 0 and k_ == 0:
                        pe.wait_ge(pool_wlo, NW * (g + 1))
                    if k_ < 2:
                        if i:
                            pe.wait_ge(act_sg, 2 * (i - 1) + k_ + 1)
                    else:
                        pe.wait_ge(dve_conv, 3 * i + k_ - 1)
                    tok = slice(b * S, (b + 1) * S)
                    for half in range(2):
                        m = 2 * k_ + half if k_ < 3 else 2 * (k_ - 3) + half
                        w_ = (w_x if m < XT else w_b if m == XT else w_c) if k_ < 3 else w_z
                        w = w_[:, g % 2, :, :, m * P:(m + 1) * P] if m < XT else w_[:, g % 2]
                        for k in range(KD):
                            last = mm3(pair_of(i, k_)[:, half * S:(half + 1) * S], (w[:, 0, k, :], w[:, 1, k, :]),
                                       (hT_hi[:, k, tok], hT_lo[:, k, tok]), k == 0, k == KD - 1)
                    last.then_inc(pe_conv if k_ < 3 else pe_gate, 1)

                def x_rows(i, c):
                    if i and c == 0:
                        pe.wait_ge(act_e, 4 * i)
                    if i and c == 1:
                        pe.wait_ge(dve_off, i)
                    for m in range(XT):
                        last = nc.tensor.transpose(work[c][:, m * P:(m + 1) * P], xc[:, i % 2, m, c * P:(c + 1) * P],
                                                   ident)
                    last.then_inc(pe_xt, 1)

                def half_decay(i):
                    pe.wait_ge(act_xt, 2 * i + 1)
                    pe.wait_ge(act_law, i + 1)
                    for m in range(XT):
                        last = nc.tensor.matmul(W0[:, m * P:(m + 1) * P], la_wide[:, m * P:(m + 1) * P],
                                                tri_le, start=True, stop=True)
                    last.then_inc(pe_eft, 1)

                def decays(u):
                    i, k = u // 4, u % 4
                    pe.wait_ge(pool_r, u + 1)
                    if k == 0:
                        pe.wait_ge(act_xt, 2 * i + 2)
                    elif k == 1:
                        pe.wait_ge(act_eft, i + 1)
                    else:
                        pe.wait_ge(act_e, u - 1)
                    for s_ in range(2):
                        last = nc.tensor.matmul(work[(U_L + k) % 2][:, :], tri_gt_r[:, :],
                                                rbuf[:, s_, u % 4].rearrange("p a b -> p (a b)"),
                                                start=s_ == 0, stop=s_ == 1)
                    last.then_inc(pe_l, 1)

                def out_proj(i):
                    g = i // B
                    if i:
                        pe.wait_ge(dve_out, 2 * i)
                    pe.wait_ge(pool_w, g + 1)
                    pe.wait_ge(pool_g, i + 1)
                    for c in range(2):
                        for m in range(XT):
                            nc.tensor.matmul(OB[:, c * D:(c + 1) * D], gt[:, i % 2, m, c * P:(c + 1) * P],
                                             w_out[:, g % 2, m, :], start=m == 0, stop=m == XT - 1)
                    pe.wait_ge(act_sq, i + 1)
                    pe.wait_ge(dve_gm, min(i + 2, STEPS))
                    for c in range(2):
                        for m in range(XT):
                            last = nc.tensor.matmul(TB[:, 3 * P + c:3 * P + c + 1], sq[:, m, c * P:(c + 1) * P],
                                                    ones[:, 0:1], start=m == 0, stop=m == XT - 1)
                    last.then_inc(pe_out, 1)

                for k_ in range(5):
                    project(0, k_)
                for i in range(STEPS):
                    more = i + 1 < STEPS
                    v = xc[:, i % 2]
                    if more:
                        project(i + 1, 0)
                    pe.wait_ge(act_xc, 3 * (i + 1))
                    if i >= 2:
                        pe.wait_ge(dve_out, 2 * (i - 1))
                    if i:
                        pe.wait_ge(dve_gm, i)
                    nc.tensor.matmul(TB[:, 0:S], v[:, 4, 0:P], v[:, 5, :], start=True, stop=True)
                    nc.tensor.matmul(TB[:, S:S + P], v[:, 4, P:S], v[:, 5, P:S], start=True, stop=True).then_inc(pe_g, 1)
                    x_rows(i, 0)
                    x_rows(i, 1)
                    if more:
                        project(i + 1, 1)
                    half_decay(i)
                    decays(4 * i)
                    decays(4 * i + 1)
                    if more:
                        project(i + 1, 2)
                    decays(4 * i + 2)
                    decays(4 * i + 3)
                    if i:
                        out_proj(i - 1)
                    if more:
                        project(i + 1, 3)
                    pe.wait_ge(pool_xe, i + 1)
                    pe.wait_ge(act_e, 4 * i + 3)
                    pe.wait_ge(dve_gm, i + 1)
                    for m in range(XT):
                        last = nc.tensor.matmul(W1[:, m * P:(m + 1) * P], xe[:, m * P:(m + 1) * P],
                                                gm[:, i % 2, P:2 * P], start=True, stop=True)
                    last.then_inc(pe_off, 1)
                    if more:
                        project(i + 1, 4)
                    if i:
                        pe.wait_ge(dve_y, XT * i)
                    for c in range(2):
                        pe.wait_ge(dve_m, 4 * i + 2 * c + 2)
                        pe.wait_ge(pool_xd, 2 * i + c + 1)
                        for hh in range(HG):
                            m, r0 = hh // 2, HD * (hh % 2)
                            last = nc.tensor.matmul((Y0, Y1)[m // 2][r0:r0 + HD,
                                                                     m % 2 * S + c * P:m % 2 * S + (c + 1) * P],
                                                    xd[:, c, hh * HD:(hh + 1) * HD],
                                                    mbuf[:, i % 2, 2 * c + hh // 4, hh % 4, :], start=True, stop=True)
                        last.then_inc(pe_y, 1)
                out_proj(STEPS - 1)

            @block.scalar
            def _(act):
                def tap(i, p_):
                    act.wait_ge(pe_conv, 3 * i + p_ + 1)
                    if i:
                        act.wait_ge(act_xc, 3 * (i - 1) + p_ + 1)
                    for m in (2 * p_, 2 * p_ + 1):
                        ct = conv_tile(i // B, m)
                        nc.scalar.activation(acc[:, p_, m % 2, :], pair_of(i, p_)[:, (m % 2) * S:(m % 2 + 1) * S],
                                             ACT.Identity, bias=conv_b[:, ct:ct + 1],
                                             scale=conv_w[:, ct, TAPS - 1:TAPS]).then_inc(act_tap, 1)

                def silu(i, p_):
                    act.wait_ge(dve_conv, 3 * i + p_ + 1)
                    if i >= 2 and p_ == 0:
                        act.wait_ge(pe_xt, 2 * (i - 1))
                        act.wait_ge(dve_y, XT * (i - 1))
                    nc.scalar.activation(xc[:, i % 2, 2 * p_:2 * p_ + 2, :], acc[:, p_], ACT.Silu).then_inc(act_xc, 1)

                def gate(i, k):
                    act.wait_ge(pe_gate, 2 * i + k + 1)
                    if i >= 2:
                        act.wait_ge(pool_g, i - 1)
                    nc.scalar.activation(sg[:, i % 2, 2 * k:2 * k + 2, :].rearrange("p m t -> p (m t)"),
                                         pair_of(i, 3 + k)[:, :], ACT.Silu).then_inc(act_sg, 1)

                def exps(u):
                    k = u % 4
                    act.wait_ge(pe_l, u + 1)
                    if u >= 2:
                        act.wait_ge(dve_m, u - 1)
                    nc.scalar.activation(ebuf[:, u % 2].rearrange("p a b -> p (a b)"), work[(U_L + k) % 2][:, :],
                                         ACT.Exp).then_inc(act_e, 1)

                def squares(i):
                    act.wait_ge(pool_g, i + 1)
                    if i:
                        act.wait_ge(pe_out, i)
                    nc.scalar.activation(sq, gt[:, i % 2], ACT.Square).then_inc(act_sq, 1)

                def widen(i):
                    g, b = i // B, i % B
                    if i:
                        act.wait_ge(pe_eft, i)
                    nc.scalar.copy(la_wide.rearrange("p (h d) -> p h d", d=HD),
                                   bc(la[:, 0, 2 * b + 1, g * HG:(g + 1) * HG].unsqueeze(2),
                                      [P, HG, HD])).then_inc(act_law, 1)

                widen(0)
                for p_ in range(3):
                    tap(0, p_)
                    silu(0, p_)
                gate(0, 0)
                gate(0, 1)
                for i in range(STEPS):
                    more = i + 1 < STEPS
                    if more:
                        tap(i + 1, 0)
                    for c in range(2):
                        act.wait_ge(pe_xt, 2 * i + c + 1)
                        if i:
                            act.wait_ge(pool_xd, 2 * i)
                            act.wait_ge(pool_xe, i)
                        nc.scalar.copy(xtok[:, c], work[c][:, :]).then_inc(act_xt, 1)
                    act.wait_ge(pe_eft, i + 1)
                    if i:
                        act.wait_ge(dve_off, i)
                    nc.scalar.activation(ef_t, tiles(W0[:, :]), ACT.Exp).then_inc(act_eft, 1)
                    exps(4 * i)
                    exps(4 * i + 1)
                    if more:
                        tap(i + 1, 1)
                    if i:
                        squares(i - 1)
                    exps(4 * i + 2)
                    exps(4 * i + 3)
                    if more:
                        tap(i + 1, 2)
                        silu(i + 1, 0)
                        silu(i + 1, 1)
                        gate(i + 1, 0)
                        silu(i + 1, 2)
                        gate(i + 1, 1)
                        widen(i + 1)
                    if i % B == 0 and i // B + 1 < GROUPS:
                        split_hi(act, i // B + 1)
                squares(STEPS - 1)

            @block.gpsimd
            def _(pool):
                def decay_rows(u):
                    i, c, hf = u // 4, u // 2 % 2, u % 2
                    t, h0 = 2 * (i % B) + c, i // B * HG + 4 * hf
                    if u >= 4:
                        pool.wait_ge(pe_l, u - 3)
                    for s_, a in ((0, la_r[:, t, h0:h0 + 4].bitcast(F32)), (1, la[:, 1, t, h0:h0 + 4])):
                        last = nc.gpsimd.tensor_tensor(rbuf[:, s_, u % 4], bc(tri_le.unsqueeze(1), [P, 4, P]),
                                                       bc(a.unsqueeze(2), [P, 4, P]), ALU.mult)
                    last.then_inc(pool_r, 1)

                def scaled(i):
                    g, b = i // B, i % B
                    hs = slice(g * HG, (g + 1) * HG)

                    def times(dst, c, a):
                        return nc.gpsimd.tensor_tensor(dst.rearrange("p (h d) -> p h d", d=HD),
                                                       xtok[:, c].rearrange("p (h d) -> p h d", d=HD),
                                                       bc(a.unsqueeze(2), [P, HG, HD]), ALU.mult)
                    for c in range(2):
                        pool.wait_ge(act_xt, 2 * i + c + 1)
                        if i:
                            pool.wait_ge(pe_y, 2 * (i - 1) + c + 1)
                        times(xd[:, c], c, dt[:, 2 * b + c, hs]).then_inc(pool_xd, 1)
                        if c == 0:
                            if i:
                                pool.wait_ge(pe_off, i)
                            times(xe, 0, dte[:, b, hs]).then_inc(pool_xe, 1)

                def gated(i):
                    pool.wait_ge(dve_g, i + 1)
                    pool.wait_ge(act_sg, 2 * i + 2)
                    nc.gpsimd.tensor_tensor(gt[:, i % 2], gt[:, i % 2], sg[:, i % 2], ALU.mult).then_inc(pool_g, 1)

                for u in range(4):
                    decay_rows(u)
                for i in range(STEPS):
                    g = i // B
                    if i:
                        gated(i - 1)
                    scaled(i)
                    if i + 1 < STEPS:
                        decay_rows(4 * i + 4)
                        decay_rows(4 * i + 5)
                    if i % B == 0:
                        pool.wait_ge(ld_o[g % 2], 16 * (g // 2 + 1))
                        nc.gpsimd.tensor_tensor(w_out[:, g % 2], w_out[:, g % 2],
                                                bc(norm_w[:, XT * g:XT * (g + 1)].unsqueeze(2), [P, XT, D]),
                                                ALU.mult).then_inc(pool_w, 1)
                    if i % B == 1 and g + 1 < GROUPS:
                        split_lo(pool, g + 1)
                    if i + 1 < STEPS:
                        decay_rows(4 * i + 6)
                        decay_rows(4 * i + 7)
                gated(STEPS - 1)

            @block.vector
            def _(dve):
                def conv_rest(i, p_):
                    n0 = 6 * (3 * i + p_)
                    dve.wait_ge(act_tap, 6 * i + 2 * p_ + 2)
                    for j in range(6):
                        m, sh = 2 * p_ + j % 2, j // 2 + 1
                        ct = conv_tile(i // B, m)
                        if j >= 2:
                            dve.wait_ge(dve_chain, n0 + j - 1)
                        nc.vector.scalar_tensor_tensor(
                            out=acc[:, p_, m % 2, sh:], in0=pair_of(i, p_)[:, (m % 2) * S:(m % 2 + 1) * S - sh],
                            scalar=conv_w[:, ct, TAPS - 1 - sh:TAPS - sh], in1=acc[:, p_, m % 2, sh:],
                            op0=ALU.mult, op1=ALU.add).then_inc(dve_chain, 1)
                    dve.wait_ge(dve_chain, n0 + 6)
                    nc.vector.engine_nop().then_inc(dve_conv, 1)

                def masked(u):
                    i, c = u // 4, u // 2 % 2
                    dve.wait_ge(act_e, u + 1)
                    if i >= 2:
                        dve.wait_ge(pe_y, 2 * (i - 2) + c + 1)
                    nc.vector.tensor_tensor(mbuf[:, i % 2, u % 4], ebuf[:, u % 2],
                                            bc(gm[:, i % 2, 2 * c * P:(2 * c + 1) * P].unsqueeze(1), [P, 4, P]),
                                            ALU.mult).then_inc(dve_m, 1)

                def scan_out(i):
                    dve.wait_ge(pe_y, 2 * i + 2)
                    if i >= 2:
                        dve.wait_ge(pe_out, i - 1)
                    for m in range(XT):
                        ct = XT * (i // B) + m
                        nc.vector.scalar_tensor_tensor(
                            out=gt[:, i % 2, m, :], in0=xc[:, i % 2, m, :], scalar=d_col[:, ct:ct + 1],
                            in1=(Y0, Y1)[m // 2][:, (m % 2) * S:(m % 2 + 1) * S], op0=ALU.mult,
                            op1=ALU.add).then_inc(dve_y, 1)
                    dve.wait_ge(dve_y, XT * (i + 1))
                    dve.wait_ge(dve_off, i + 1)
                    nc.vector.tensor_tensor(gt[:, i % 2, :, P:S], gt[:, i % 2, :, P:S], off, ALU.add).then_inc(dve_g, 1)

                def out_sum(i):
                    b = i % B
                    dve.wait_ge(pe_out, i + 1)
                    nc.vector.tensor_copy(ss[:, 2 * b:2 * b + 2, i // B], TB[:, 3 * P:3 * P + 2]).then_inc(dve_out, 1)
                    if i >= B:
                        dve.wait_ge(dve_out, 2 * (i - B) + 2)
                    ya = y_acc[:, 2 * b:2 * b + 2, :]
                    nc.vector.tensor_tensor(ya, OB[:, :].rearrange("p (c d) -> p c d", c=2), ya,
                                            ALU.add).then_inc(dve_out, 1)

                for p_ in range(3):
                    conv_rest(0, p_)
                for i in range(STEPS):
                    more = i + 1 < STEPS
                    if i:
                        scan_out(i - 1)
                    dve.wait_ge(pe_g, i + 1)
                    if i >= 2:
                        dve.wait_ge(pe_off, i - 1)
                    nc.vector.tensor_tensor(gm[:, i % 2], TB[:, 0:3 * P], causal3, ALU.mult).then_inc(dve_gm, 1)
                    if more:
                        conv_rest(i + 1, 0)
                    dve.wait_ge(dve_gm, i + 1)
                    masked(4 * i)
                    masked(4 * i + 1)
                    if more:
                        conv_rest(i + 1, 1)
                    masked(4 * i + 2)
                    masked(4 * i + 3)
                    if more:
                        conv_rest(i + 1, 2)
                    dve.wait_ge(pe_off, i + 1)
                    dve.wait_ge(act_eft, i + 1)
                    if i:
                        dve.wait_ge(dve_g, i)
                    nc.vector.tensor_tensor(off, tiles(W1[:, :]), ef_t, ALU.mult).then_inc(dve_off, 1)
                    if i:
                        out_sum(i - 1)
                scan_out(STEPS - 1)
                out_sum(STEPS - 1)

        take = carver()
        wg = take(2, 4, KD, I0)
        wu = take(2, 4, KD, I0)
        wd = take(2, 4, 2, D, parts=IT)
        wsg = take(KD, IS)
        wsu = take(KD, IS)
        wsd = take(NIS, D, parts=IT)
        gate_raw = take(D, parts=E0)
        back_t = take(2, 4, P)
        back = take(4, NT * P)
        sh_a = back[0:IT].rearrange("p e (a n) -> p (e a) n", a=2)[:, 0:NIS, :]
        xe_t = take(KD, 4 * P)
        silu_g = take(2, 2 * P, parts=IT)
        act_t = take(2, 2, P, parts=IT)
        oe = take(4, D)
        sh_s = take(2, 512, parts=IT)
        small = [take(NT, E0) for _ in range(9)]
        r_mx, r_sum, r_rec, rms, rms_std = (take(NT) for _ in range(5))
        m8 = take(NT, 8)
        i8 = take(NT, 8).bitcast(U32)
        i8f = take(NT, 8)
        takeh = carver(halves, HALVES)
        slot = takeh(NT, 4, P)
        h_r = takeh(2, NT, D)
        wsg_r = takeh(2, KD, IS)
        wsu_r = takeh(2, KD, IS)
        gate_t = takeh(2, KD, E0)
        ld_wu = [sem("ld_wu_even"), sem("ld_wu_odd")]
        act_sh, pool_sh, act_h, pool_h, dve_gw = (sem(n) for n in (
            "act_sh", "pool_sh", "act_h", "pool_h", "dve_gw"))
        pool_res = sem("pool_res")

        names = ("ld_gate ld_sh dve_ms act_ms dve_res pe_gw act_gw pe_lg dve_rt act_ex dve_sel pe_pos "
                 "dve_pos pe_sg act_sg dve_sa pe_sd act_sy dve_p dve_q pe_disp act_xe pe_q act_qt pe_up act_s dve_a "
                 "pe_dn act_oe pe_comb dve_y").split()
        f = {n: sem("f_" + n) for n in names}
        (ld_gate, ld_sh, dve_ms, act_ms, dve_res, pe_gw, act_gw, pe_lg, dve_rt, act_ex, dve_sel, pe_pos,
         dve_pos, pe_sg, act_sg, dve_sa, pe_sd, act_sy, dve_p, dve_q, pe_disp, act_xe, pe_q, act_qt, pe_up, act_s,
         dve_a, pe_dn, act_oe, pe_comb, dve_y) = (f[n] for n in names)
        NQ = E0 // 4

        def topk_select(dve, scores, k, chain, n0, eq, sel, m8, i8, i8f):
            for t in range(NT):
                nc.vector.max(m8[:, t, :], scores[:, t, :]).then_inc(chain, 1)
            for t in range(NT):
                dve.wait_ge(chain, n0 + t + 1)
                nc.vector.max_index(i8[:, t, :], m8[:, t, :], scores[:, t, :]).then_inc(chain, 1)
            dve.wait_ge(chain, n0 + 2 * NT)
            nc.vector.tensor_copy(i8f, i8).then_inc(chain, 1)
            n = n0 + 2 * NT + 1
            for r in range(k):
                dve.wait_ge(chain, n)
                nc.vector.tensor_tensor(eq if r else sel, bc(iota[:, 0:E0].unsqueeze(1), [P, NT, E0]),
                                        bc(i8f[:, :, r:r + 1], [P, NT, E0]), ALU.is_equal).then_inc(chain, 1)
                n += 1
                if r:
                    dve.wait_ge(chain, n)
                    nc.vector.tensor_tensor(sel, sel, eq, ALU.add).then_inc(chain, 1)
                    n += 1
            return n

        with nc.Block() as block:
            @block.sync
            def _(sp):
                sp.dma_start(gate_raw, A["L0_ffn_gate_w"]).then_inc(ld_gate, 16)
                load_shift_scale(sp, 1)
                sp.dma_start(wsg, A["L0_ffn_ws_gate"].rearrange("(k p) i -> p k i", p=P)).then_inc(ld_sh, 16)
                sp.dma_start(wsu, A["L0_ffn_ws_up"].rearrange("(k p) i -> p k i", p=P)).then_inc(ld_sh, 16)
                sp.dma_start(wsd, A["L0_ffn_ws_down"].rearrange("(j p) n -> p j n", p=IT)).then_inc(ld_sh, 16)
                for eq in range(NQ):
                    if eq == 2:
                        sp.wait_ge(dve_res, NT)
                        load_gate(sp, 1)
                        sp.wait_ge(norm_h, 2 * NT)
                        load_shift_scale(sp, 2)
                    if eq >= 2:
                        sp.wait_ge(pe_dn, 4 * (eq - 1))
                    e4, r_ = slice(4 * eq, 4 * eq + 4), eq % 2
                    sp.dma_start(wg[:, r_], A["L0_ffn_w_gate"][e4].rearrange("e (k p) i -> p e k i", p=P)).then_inc(ld_wu[r_], 16)
                    sp.dma_start(wu[:, r_], A["L0_ffn_w_up"][e4].rearrange("e (k p) i -> p e k i", p=P)).then_inc(ld_wu[r_], 16)
                    sp.dma_start(wd[:, r_], A["L0_ffn_w_down"][e4].rearrange("e (j p) n -> p e j n", p=IT)).then_inc(ld_wu[r_], 16)

            @block.tensor
            def _(pe):
                pe.wait_ge(ld_gate, 16)
                for k in range(KD):
                    last = nc.tensor.transpose(bank[4][:, k * E0:(k + 1) * E0], gate_raw[:, k * P:(k + 1) * P],
                                               ident[0:E0, 0:E0])
                last.then_inc(pe_gw, 1)
                norm_pe(pe, 1, bank[0:2])
                pe.wait_ge(dve_gw, 1)
                pe.wait_ge(norm_hT, 2 * NT // 2)
                for t in range(NT):
                    for k in range(KD):
                        ts = slice(t * P, (t + 1) * P)
                        last = mm3(bank[5][:, t * E0:(t + 1) * E0], (hT_hi[:, k, ts], hT_lo[:, k, ts]),
                                   (gate_t[:, 0, k, :], gate_t[:, 1, k, :]), k == 0, k == KD - 1)
                last.then_inc(pe_lg, 1)
                pe.wait_ge(pool_sh, 2)
                pe.wait_ge(ld_sh, 48)
                for th in range(2):
                    for j in range(NIS):
                        u = NIS * th + j
                        if u >= 2:
                            pe.wait_ge(dve_sa, u - 1)
                        tok, ij = slice(th * 512, (th + 1) * 512), slice(j * IT, (j + 1) * IT)
                        for w, bk in ((wsg_r, bank[u % 2]), (wsu_r, bank[2 + u % 2])):
                            for k in range(KD):
                                last = mm3(bk[0:IT, :], (w[:, 0, k, ij], w[:, 1, k, ij]),
                                           (hT_hi[:, k, tok], hT_lo[:, k, tok]), k == 0, k == KD - 1)
                        last.then_inc(pe_sg, 1)
                    for t in range(4):
                        u = 4 * th + t
                        pe.wait_ge(dve_sa, NIS * (th + 1))
                        if u >= 2:
                            pe.wait_ge(act_sy, u - 1)
                        for j in range(NIS):
                            last = nc.tensor.matmul(bank[6 + u % 2][:, 0:D], sh_a[:, j, t * P:(t + 1) * P], wsd[:, j, :],
                                                    start=j == 0, stop=j == NIS - 1)
                        last.then_inc(pe_sd, 1)
                pe.wait_ge(dve_sel, 1)
                sel = small[4]
                for t in range(NT):
                    for s_ in range(t):
                        nc.tensor.matmul(bank[5][:, P + t * E0:P + (t + 1) * E0], ones, sel[:, s_, :],
                                         start=s_ == 0, stop=False)
                    last = nc.tensor.matmul(bank[5][:, P + t * E0:P + (t + 1) * E0], tri_lt, sel[:, t, :],
                                            start=t == 0, stop=True)
                last.then_inc(pe_pos, 1)

                pe.wait_ge(dve_sa, 2 * NIS)
                pe.wait_ge(act_sy, 2 * 4)
                pe.wait_ge(pool_h, 1)
                for eq in range(NQ):
                    for k in range(KD):
                        if eq:
                            pe.wait_ge(act_xe, 2 * eq)
                        for t in range(NT):
                            pe.wait_ge(dve_p, NT * eq + t + 1)
                            for s_ in range(2):
                                last = nc.tensor.matmul(bank[k][:, :], h_r[:, s_, t, k * P:(k + 1) * P],
                                                        slot[:, t].rearrange("p e c -> p (e c)"),
                                                        start=t + s_ == 0, stop=t == NT - 1 and s_ == 1)
                        last.then_inc(pe_disp, 1)
                    for t in range(NT):
                        u = NT * eq + t
                        pe.wait_ge(dve_q, u + 1)
                        if t >= 2:
                            pe.wait_ge(act_qt, u - 1)
                        elif eq:
                            pe.wait_ge(dve_y, NT * eq - 1 + t)
                        for e in range(4):
                            last = nc.tensor.transpose(bank[2 + t % 2][:, e * P:(e + 1) * P], back_t[:, t % 2, e, :], ident)
                        last.then_inc(pe_q, 1)

                    def up(e):
                        n = 4 * eq + e
                        pe.wait_ge(act_xe, 2 * (eq + 1))
                        pe.wait_ge(ld_wu[eq % 2], 48 * (eq // 2 + 1))
                        if n >= 2:
                            pe.wait_ge(dve_a, n - 1)
                        if n == 1:
                            pe.wait_ge(dve_pos, 1)
                        for w, o in ((wg, 0), (wu, 2)):
                            for j in range(2):
                                for k in range(KD):
                                    last = nc.tensor.matmul(bank[4 + n % 2][0:IT, (o + j) * P:(o + j + 1) * P],
                                                            w[:, eq % 2, e, k, j * IT:(j + 1) * IT],
                                                            xe_t[:, k, e * P:(e + 1) * P], start=k == 0, stop=k == KD - 1)
                        last.then_inc(pe_up, 1)

                    def down(e):
                        n = 4 * eq + e
                        pe.wait_ge(dve_a, n + 1)
                        if n >= 2:
                            pe.wait_ge(act_oe, n - 1)
                        for j in range(2):
                            last = nc.tensor.matmul(bank[6 + n % 2][:, 0:D], act_t[:, n % 2, j, :], wd[:, eq % 2, e, j, :],
                                                    start=j == 0, stop=j == 1)
                        last.then_inc(pe_dn, 1)

                    up(0)
                    for e in range(4):
                        if e < 3:
                            up(e + 1)
                        down(e)
                    for t in range(NT):
                        u = NT * eq + t
                        pe.wait_ge(act_oe, 4 * (eq + 1))
                        pe.wait_ge(act_qt, NT * (eq + 1))
                        if t >= 2:
                            pe.wait_ge(dve_y, u - 1)
                        for e in range(4):
                            last = nc.tensor.matmul(bank[2 + t % 2][:, 0:D], back[:, e, t * P:(t + 1) * P], oe[:, e, :],
                                                    start=e == 0, stop=e == 3)
                        last.then_inc(pe_comb, 1)

            @block.scalar
            def _(act):
                act.wait_ge(dve_ms, 2)
                nc.scalar.activation(rms_std, rms_std, ACT.Sqrt).then_inc(act_ms, 1)
                act.wait_ge(ld_sh, 48)
                nc.scalar.copy(wsg_r[:, 0], wsg).then_inc(act_sh, 1)
                nc.scalar.copy(wsu_r[:, 0], wsu).then_inc(act_sh, 1)
                act.wait_ge(pe_gw, 1)
                nc.scalar.copy(gate_t[:, 0].rearrange("p k e -> p (k e)"), bank[4][:, 0:KD * E0]).then_inc(act_gw, 1)
                norm_act(act, 1)
                norm_act_copy(act, 1, bank[0:2])
                act.wait_ge(dve_rt, 2)
                nc.scalar.activation(small[1], small[0], ACT.Exp).then_inc(act_ex, 1)
                nc.scalar.copy(h_r[:, 0], h[:, :, :]).then_inc(act_h, 1)
                for th in range(2):
                    for j in range(NIS):
                        u = NIS * th + j
                        act.wait_ge(pe_sg, u + 1)
                        if u >= 2:
                            act.wait_ge(dve_sa, u - 1)
                        nc.scalar.activation(sh_s[:, u % 2], bank[u % 2][0:IT, :], ACT.Silu).then_inc(act_sg, 1)
                    for t in range(4):
                        u = 4 * th + t
                        act.wait_ge(pe_sd, u + 1)
                        nc.scalar.copy(y_acc[:, u, :], bank[6 + u % 2][:, 0:D]).then_inc(act_sy, 1)
                for eq in range(NQ):
                    for k in range(KD):
                        act.wait_ge(pe_disp, 2 * eq + k + 1)
                        if eq:
                            act.wait_ge(pe_up, 4 * eq)
                        nc.scalar.copy(xe_t[:, k], bank[k][:, :]).then_inc(act_xe, 1)
                    for t in range(NT):
                        u = NT * eq + t
                        act.wait_ge(pe_q, u + 1)
                        if eq:
                            act.wait_ge(pe_comb, NT * eq)
                        else:
                            act.wait_ge(pe_sd, 2 * 4)
                        nc.scalar.copy(back[:, :, t * P:(t + 1) * P],
                                       bank[2 + t % 2][:, :].rearrange("p (e c) -> p e c", e=4)).then_inc(act_qt, 1)

                    def silu(e):
                        n = 4 * eq + e
                        act.wait_ge(pe_up, n + 1)
                        if n >= 2:
                            act.wait_ge(dve_a, n - 1)
                        nc.scalar.activation(silu_g[:, n % 2], bank[4 + n % 2][0:IT, 0:2 * P], ACT.Silu).then_inc(act_s, 1)

                    silu(0)
                    for e in range(4):
                        if e < 3:
                            silu(e + 1)
                        act.wait_ge(pe_dn, 4 * eq + e + 1)
                        if eq:
                            act.wait_ge(pe_comb, NT * eq)
                        nc.scalar.copy(oe[:, e, :], bank[6 + e % 2][:, 0:D]).then_inc(act_oe, 1)

            @block.gpsimd
            def _(pool):
                for t in range(NT):
                    pool.wait_ge(dve_res, t + 1)
                    nc.gpsimd.tensor_tensor(x[:, t, :], x[:, t, :], y_acc[:, t, :], ALU.add).then_inc(pool_res, 1)
                norm_pool(pool, 1)
                for i_, (w, wr) in enumerate(((wsg, wsg_r), (wsu, wsu_r))):
                    pool.wait_ge(act_sh, i_ + 1)
                    nc.gpsimd.tensor_tensor(wr[:, 1], w, wr[:, 0].bitcast(F32), ALU.subtract).then_inc(pool_sh, 1)
                pool.wait_ge(act_h, 1)
                nc.gpsimd.tensor_tensor(h_r[:, 1], h[:, :, :], h_r[:, 0].bitcast(F32), ALU.subtract).then_inc(pool_h, 1)

            @block.vector
            def _(dve):
                nc.vector.tensor_reduce(rms_std, ss[:, :, :], AX, ALU.add).then_inc(dve_ms, 1)
                dve.wait_ge(dve_ms, 1)
                nc.vector.tensor_scalar(rms_std, rms_std, 1.0 / INTER, EPS, ALU.mult, ALU.add).then_inc(dve_ms, 1)
                dve.wait_ge(act_ms, 1)
                nc.vector.reciprocal(rms, rms_std).then_inc(dve_ms, 1)
                dve.wait_ge(dve_ms, 3)
                for t in range(NT):
                    nc.vector.scalar_tensor_tensor(out=y_acc[:, t, :], in0=y_acc[:, t, :], scalar=rms[:, t:t + 1],
                                                   in1=mod[:, t // 2, 2 * D:3 * D], op0=ALU.mult,
                                                   op1=ALU.mult).then_inc(dve_res, 1)
                for t in range(NT):
                    dve.wait_ge(pool_res, t + 1)
                    norm_stats(1, t)
                norm_dve(dve, 1)
                dve.wait_ge(act_gw, 1)
                nc.vector.tensor_tensor(gate_t[:, 1].rearrange("p k e -> p (k e)"), bank[4][:, 0:KD * E0],
                                        gate_t[:, 0].rearrange("p k e -> p (k e)").bitcast(F32),
                                        ALU.subtract).then_inc(dve_gw, 1)
                norm_dve_lo(dve, 1, bank[0:2])
                lg = bank[5][:, 0:P].rearrange("p (t e) -> p t e", t=NT)
                pos = bank[5][:, P:2 * P].rearrange("p (t e) -> p t e", t=NT)
                shift, ex, prob, eqv, sel, wt, posd, qpos, qtmp = small
                dve.wait_ge(pe_lg, 1)
                nc.vector.tensor_reduce(r_mx, lg, AX, ALU.max).then_inc(dve_rt, 1)
                dve.wait_ge(dve_rt, 1)
                nc.vector.tensor_tensor(shift, lg, bc(r_mx.unsqueeze(2), [P, NT, E0]), ALU.subtract).then_inc(dve_rt, 1)
                dve.wait_ge(act_ex, 1)
                nc.vector.tensor_reduce(r_sum, ex, AX, ALU.add).then_inc(dve_rt, 1)
                dve.wait_ge(dve_rt, 3)
                nc.vector.reciprocal(r_rec, r_sum).then_inc(dve_rt, 1)
                dve.wait_ge(dve_rt, 4)
                nc.vector.tensor_tensor(prob, ex, bc(r_rec.unsqueeze(2), [P, NT, E0]), ALU.mult).then_inc(dve_rt, 1)
                dve.wait_ge(dve_rt, 5)
                n = topk_select(dve, prob, 2, dve_rt, 5, eqv, sel, m8, i8, i8f)
                dve.wait_ge(dve_rt, n)
                nc.vector.tensor_tensor(wt, prob, sel, ALU.mult).then_inc(dve_sel, 1)

                def shared(th):
                    for j in range(NIS):
                        u = NIS * th + j
                        dve.wait_ge(act_sg, u + 1)
                        if th:
                            dve.wait_ge(pe_sd, 4)
                        nc.vector.tensor_tensor(sh_a[:, j, :], bank[2 + u % 2][0:IT, :], sh_s[:, u % 2],
                                                ALU.mult).then_inc(dve_sa, 1)

                shared(0)
                shared(1)
                dve.wait_ge(pe_pos, 1)
                nc.vector.scalar_tensor_tensor(out=posd, in0=pos, scalar=1.0, in1=sel, op0=ALU.add,
                                               op1=ALU.mult).then_inc(dve_rt, 1)
                nc.vector.tensor_scalar(qtmp, pos, CAP - 1.0, 1.0, ALU.min, ALU.add).then_inc(dve_rt, 1)
                dve.wait_ge(dve_rt, n + 2)
                nc.vector.tensor_scalar(posd, posd, -1.0, None, ALU.add).then_inc(dve_rt, 1)
                nc.vector.tensor_tensor(qpos, qtmp, sel, ALU.mult).then_inc(dve_rt, 1)
                dve.wait_ge(dve_rt, n + 4)
                nc.vector.tensor_scalar(qpos, qpos, -1.0, None, ALU.add).then_inc(dve_pos, 1)
                dve.wait_ge(dve_pos, 1)
                for eq in range(NQ):
                    if eq:
                        dve.wait_ge(pe_disp, 2 * eq)
                    for t in range(NT):
                        for e in range(4):
                            last = nc.vector.tensor_scalar(slot[:, t, e, :], iota, posd[:, t, 4 * eq + e:4 * eq + e + 1],
                                                           None, ALU.is_equal)
                        last.then_inc(dve_p, 1)
                    for t in range(NT):
                        u = NT * eq + t
                        if u >= 2:
                            dve.wait_ge(pe_q, u - 1)
                        for e in range(4):
                            last = nc.vector.tensor_scalar(back_t[:, t % 2, e, :], iota,
                                                           qpos[:, t, 4 * eq + e:4 * eq + e + 1],
                                                           wt[:, t, 4 * eq + e:4 * eq + e + 1], ALU.is_equal, ALU.mult)
                        last.then_inc(dve_q, 1)
                    for e in range(4):
                        n = 4 * eq + e
                        dve.wait_ge(act_s, n + 1)
                        if n >= 2:
                            dve.wait_ge(pe_dn, n - 1)
                        nc.vector.tensor_tensor(act_t[:, n % 2].rearrange("p j c -> p (j c)"),
                                                bank[4 + n % 2][0:IT, 2 * P:4 * P], silu_g[:, n % 2],
                                                ALU.mult).then_inc(dve_a, 1)
                    dve.wait_ge(act_sy, 2 * 4)
                    for t in range(NT):
                        u = NT * eq + t
                        dve.wait_ge(pe_comb, u + 1)
                        if eq:
                            dve.wait_ge(dve_y, u - NT + 1)
                        nc.vector.tensor_tensor(y_acc[:, t, :], bank[2 + t % 2][:, 0:D], y_acc[:, t, :],
                                                ALU.add).then_inc(dve_y, 1)

        take = carver()
        w_raw = take(4, 2, D)
        wide = take(2048)
        takeh = carver(halves, HALVES)
        w_t = takeh(4, 2, KD, D)
        att_t = takeh(2, KD, P)
        qkp = take(2, 2, AH, 32)
        r_a = take(2 * AH, DH)
        r_b = take(2 * AH, DH)
        q_t = take(4, NT * P)
        k_t = take(4, NT * P)
        v_sb = take(NT, D)
        prob_sb = wide[:, 0:2048].rearrange("p (r n) -> p r n", r=4)
        prob_t = w_raw.rearrange("p a b c -> p a (b c)")
        mx = take(4, 4)
        nmx = take(4, 4)
        rs = take(NT, AH)
        rrs = take(NT, AH)
        att = take(D)
        otmp = take(D)
        W1 = 3 * D
        late = carver()
        late(ARENA - (E1 + 1) * W1)
        w1_raw = late(E1 + 1, 3, D)
        EARLY = 13
        assert take(1).offset % ARENA <= ARENA - (E1 + 1 - EARLY) * W1

        def load_experts(eng, e0, e1):
            e = slice(e0, e1)
            eng.dma_start(w1_raw[:, e, 0, :], A["L1_ffn_expert_gate_w"][e].rearrange("e f h -> f e h")).then_inc(ld_w1, 16)
            eng.dma_start(w1_raw[:, e, 1, :], A["L1_ffn_expert_up_w"][e].rearrange("e f h -> f e h")).then_inc(ld_w1, 16)
            for e_ in range(e0, e1):
                eng.dma_start(w1_raw[:, e_, 2, :].rearrange("p (o f) -> p o f", o=2),
                              A["L1_ffn_expert_down_w"][e_].rearrange("(o p) f -> p o f", p=P)).then_inc(ld_w1, 16)

        names = ("ld_w dve_res pe_wt act_wt pe_qkv "
                 "act_v dve_ra dve_qk pe_qk act_qk pe_s dve_mask dve_mx dve_nm act_p pe_pt ev_pt_a "
                 "ev_pt_d pe_pv dve_rr dve_att pe_at act_at pe_wo dve_o dve_x dve_wt dve_at").split()
        g_ = {n: sem("a_" + n) for n in names}
        (ld_wq, dve_res1, pe_wt, act_wt, pe_qkv, act_v, dve_ra, dve_qk, pe_qk, act_qk, pe_s, dve_mask, dve_mx, dve_nm, act_p, pe_pt,
         act_pt, dve_pt, pe_pv, dve_rr, dve_att, pe_at, act_at, pe_wo, dve_o, dve_x, dve_wt, dve_at) = (g_[n] for n in names)
        ld_w1 = sem("ld_w1")
        units = [(b, qt, js) for b in range(B) for qt, js in ((0, (0, 1, 2, 3)), (1, (0, 1)), (1, (2, 3)))]

        with nc.Block() as block:
            @block.sync
            def _(sp):
                for i_, nm in enumerate(("L1_attn_Wq", "L1_attn_Wk", "L1_attn_Wv", "L1_attn_Wo")):
                    sp.dma_start(w_raw[:, i_], A[nm].rearrange("(o p) d -> p o d", p=P)).then_inc(ld_wq, 16)
                sp.dma_start(w1_raw[:, E1, 0, :], A["L1_ffn_shared_gate_w"]).then_inc(ld_w1, 16)
                sp.dma_start(w1_raw[:, E1, 1, :], A["L1_ffn_shared_up_w"]).then_inc(ld_w1, 16)
                sp.dma_start(w1_raw[:, E1, 2, :].rearrange("p (o f) -> p o f", o=2),
                             A["L1_ffn_shared_down_w"].rearrange("(o p) f -> p o f", p=P)).then_inc(ld_w1, 16)
                load_experts(sp, EARLY, E1)
                sp.wait_ge(pool_res, 2 * NT)
                load_gate(sp, 2)
                sp.wait_ge(norm_h, 3 * NT)
                load_shift_scale(sp, 3)

            @block.tensor
            def _(pe):
                pe.wait_ge(ld_wq, 64)
                for i_ in range(4):
                    for k in range(KD):
                        for o in range(2):
                            last = nc.tensor.transpose(bank[4 + i_][:, (2 * k + o) * P:(2 * k + o + 1) * P],
                                                       w_raw[:, i_, o, k * P:(k + 1) * P], ident)
                    last.then_inc(pe_wt, 1)
                norm_pe(pe, 2, bank[0:2])
                pe.wait_ge(dve_wt, 4)
                pe.wait_ge(norm_hT, 3 * NT // 2)

                def qk_transposes(t):
                    pe.wait_ge(dve_qk, t + 1)
                    for s_ in range(2):
                        u = 2 * t + s_
                        if u >= 2:
                            pe.wait_ge(act_qk, u - 1)
                        for j in range(4):
                            last = nc.tensor.transpose(bank[4 + s_][:, j * P:(j + 1) * P],
                                                       qkp[:, t % 2, s_, 4 * j:4 * j + 4, :].rearrange("p a b -> p (a b)"),
                                                       ident)
                        last.then_inc(pe_qk, 1)

                for t in range(NT):
                    if t >= 2:
                        pe.wait_ge(dve_ra, 3 * (t - 1))
                        pe.wait_ge(act_v, t - 1)
                    ts = slice(t * P, (t + 1) * P)
                    for w, dst in ((0, bank[t % 2][:, 0:D]), (1, bank[t % 2][:, D:2 * D]), (2, bank[2 + t % 2][:, 0:D])):
                        for k in range(KD):
                            last = mm3(dst, (hT_hi[:, k, ts], hT_lo[:, k, ts]), (w_t[:, w, 0, k, :], w_t[:, w, 1, k, :]),
                                       k == 0, k == KD - 1)
                    last.then_inc(pe_qkv, 1)
                    if t:
                        qk_transposes(t - 1)
                qk_transposes(NT - 1)

                def scores(u):
                    b, qt, js = units[u]
                    nk = P * (qt + 1)
                    if u == 0:
                        pe.wait_ge(act_qk, 2 * NT)
                        pe.wait_ge(dve_ra, 3 * NT)
                        pe.wait_ge(act_v, NT)
                    for r in range(4):
                        if u:
                            pe.wait_ge(act_p, 4 * (u - 1) + r + 1)
                        for i_, j in enumerate(js):
                            last = nc.tensor.matmul(bank[r][:, i_ * nk:(i_ + 1) * nk],
                                                    q_t[32 * r:32 * r + DH, j, (2 * b + qt) * P:(2 * b + qt + 1) * P],
                                                    k_t[32 * r:32 * r + DH, j, 2 * b * P:2 * b * P + nk],
                                                    start=True, stop=True)
                        last.then_inc(pe_s, 1)

                def values(u):
                    b, qt, js = units[u]
                    for r in range(4):
                        v = 4 * u + r
                        pe.wait_ge(act_p, v + 1)
                        if r < 2:
                            if u:
                                (pe.wait_ge(act_pt, 2 * u) if r == 0 else pe.wait_ge(dve_pt, 2 * u))
                        else:
                            (pe.wait_ge(act_pt, 2 * u + 1) if r == 2 else pe.wait_ge(dve_pt, 2 * u + 1))
                        for i_ in range(4):
                            last = nc.tensor.transpose(bank[4 + r % 2][:, i_ * P:(i_ + 1) * P],
                                                       prob_sb[:, r, i_ * P:(i_ + 1) * P], ident)
                        last.then_inc(pe_pt, 1)
                    if js[0] == 0 and u:
                        pe.wait_ge(dve_att, 2 * b + qt)
                    for r in range(4):
                        if r % 2 == 0:
                            pe.wait_ge(act_pt, 2 * u + r // 2 + 1)
                        else:
                            pe.wait_ge(dve_pt, 2 * u + r // 2 + 1)
                        for i_, j in enumerate(js):
                            hd = 4 * j + r
                            for kb in range(qt + 1):
                                blk = i_ * (qt + 1) + kb
                                last = nc.tensor.matmul(bank[6][:, hd * DH:(hd + 1) * DH],
                                                        prob_t[:, r, blk * P:(blk + 1) * P],
                                                        v_sb[:, 2 * b + kb, hd * DH:(hd + 1) * DH],
                                                        start=kb == 0, stop=kb == qt)
                    last.then_inc(pe_pv, 1)

                def project(t):
                    pe.wait_ge(dve_att, t + 1)
                    if t:
                        pe.wait_ge(dve_o, t)
                    for k in range(KD):
                        last = nc.tensor.transpose(bank[7][:, k * P:(k + 1) * P], att[:, k * P:(k + 1) * P], ident)
                    last.then_inc(pe_at, 1)
                    pe.wait_ge(dve_at, t + 1)
                    for k in range(KD):
                        last = mm3(bank[7][:, D:2 * D], (att_t[:, 0, k, :], att_t[:, 1, k, :]),
                                   (w_t[:, 3, 0, k, :], w_t[:, 3, 1, k, :]), k == 0, k == KD - 1)
                    last.then_inc(pe_wo, 1)

                scores(0)
                for u in range(len(units)):
                    if u + 1 < len(units):
                        scores(u + 1)
                    values(u)
                    if units[u][2][-1] == 3:
                        project(2 * units[u][0] + units[u][1])

            @block.gpsimd
            def _(pool):
                pool.wait_ge(ld_gt, 32)
                for t in range(NT):
                    nc.gpsimd.tensor_tensor(y_acc[:, t, :], y_acc[:, t, :], mod[:, t // 2, 2 * D:3 * D],
                                            ALU.mult).then_inc(pool_res, 1)
                nc.gpsimd.memset(qkp, 0.0).then_inc(pool_res, 1)
                norm_pool(pool, 2)

            @block.scalar
            def _(act):
                for i_ in range(4):
                    act.wait_ge(pe_wt, i_ + 1)
                    nc.scalar.copy(w_t[:, i_, 0].rearrange("p k d -> p (k d)"), bank[4 + i_][:, :]).then_inc(act_wt, 1)
                norm_act(act, 2)
                norm_act_copy(act, 2, bank[0:2])

                def qk_copies(t):
                    for s_ in range(2):
                        act.wait_ge(pe_qk, 2 * t + s_ + 1)
                        nc.scalar.copy((q_t, k_t)[s_][:, :, t * P:(t + 1) * P],
                                       bank[4 + s_][:, :].rearrange("p (j q) -> p j q", j=4)).then_inc(act_qk, 1)

                for t in range(NT):
                    act.wait_ge(pe_qkv, t + 1)
                    nc.scalar.copy(v_sb[:, t, :], bank[2 + t % 2][:, 0:D]).then_inc(act_v, 1)
                    if t:
                        qk_copies(t - 1)
                qk_copies(NT - 1)

                def exps(u):
                    b, qt, js = units[u]
                    nk = P * (qt + 1)
                    for r in range(4):
                        act.wait_ge(dve_nm, 4 * u + r + 1)
                        if u:
                            act.wait_ge(pe_pt, 4 * (u - 1) + r + 1)
                        for i_, j in enumerate(js):
                            hd = 4 * j + r
                            last = nc.scalar.activation(prob_sb[:, r, i_ * nk:(i_ + 1) * nk], bank[r][:, i_ * nk:(i_ + 1) * nk],
                                                        ACT.Exp, bias=nmx[:, r, i_:i_ + 1], scale=DH ** -0.5,
                                                        accum_out=rs[:, 2 * b + qt, hd:hd + 1])
                        last.then_inc(act_p, 1)

                exps(0)
                for u in range(len(units)):
                    for r in (0, 2):
                        act.wait_ge(pe_pt, 4 * u + r + 1)
                        if u:
                            act.wait_ge(pe_pv, u)
                        nc.scalar.copy(prob_t[:, r], bank[4][:, :]).then_inc(act_pt, 1)
                    if u + 1 < len(units):
                        exps(u + 1)
                    if units[u][2][-1] == 3:
                        t = 2 * units[u][0] + units[u][1]
                        act.wait_ge(pe_at, t + 1)
                        if t:
                            act.wait_ge(pe_wo, t)
                        nc.scalar.copy(att_t[:, 0].rearrange("p k q -> p (k q)"), bank[7][:, 0:D]).then_inc(act_at, 1)

            @block.vector
            def _(dve):
                for t in range(NT):
                    dve.wait_ge(pool_res, NT + t + 1)
                    nc.vector.tensor_tensor(x[:, t, :], x[:, t, :], y_acc[:, t, :], ALU.add).then_inc(dve_res1, 1)
                    dve.wait_ge(dve_res1, t + 1)
                    norm_stats(2, t)
                norm_dve(dve, 2)
                for i_ in range(4):
                    dve.wait_ge(act_wt, i_ + 1)
                    nc.vector.tensor_tensor(w_t[:, i_, 1].rearrange("p k d -> p (k d)"), bank[4 + i_][:, :],
                                            w_t[:, i_, 0].rearrange("p k d -> p (k d)").bitcast(F32),
                                            ALU.subtract).then_inc(dve_wt, 1)
                norm_dve_lo(dve, 2, bank[0:2])
                dve.wait_ge(ld_gt, 48)
                dve.wait_ge(pool_res, 2 * NT + 1)
                for t in range(NT):
                    c = t % 2
                    qk = bank[t % 2][:, :].rearrange("p (h d) -> p h d", d=DH)
                    n = 3 * t
                    dve.wait_ge(pe_qkv, t + 1)
                    if t:
                        dve.wait_ge(dve_qk, t)
                    nc.vector.tensor_tensor(r_a, qk, bc(rope[:, 0, c].unsqueeze(1), [P, 2 * AH, DH]),
                                            ALU.mult).then_inc(dve_ra, 1)
                    for o in range(2):
                        nc.vector.tensor_tensor(r_b[:, :, o::2], qk[:, :, 1 - o::2],
                                                bc(rope[:, 1, c, o::2].unsqueeze(1), [P, 2 * AH, DH // 2]),
                                                ALU.mult).then_inc(dve_ra, 1)
                    dve.wait_ge(dve_ra, n + 3)
                    if t >= 2:
                        dve.wait_ge(pe_qk, 2 * (t - 1))
                    nc.vector.tensor_tensor(qkp[:, t % 2].rearrange("p s h d -> p (s h) d")[:, :, 0:DH], r_a, r_b,
                                            ALU.add).then_inc(dve_qk, 1)

                def maxima(u):
                    b, qt, js = units[u]
                    nj, nk = len(js), P * (qt + 1)
                    for r in range(4):
                        v = 4 * u + r
                        s3 = bank[r][:, :].rearrange("p (j k) -> p j k", j=nj)
                        dve.wait_ge(pe_s, v + 1)
                        nc.vector.tensor_tensor(s3[:, :, qt * P:nk], s3[:, :, qt * P:nk],
                                                bc(neg_mask.unsqueeze(1), [P, nj, P]), ALU.add).then_inc(dve_mask, 1)
                        dve.wait_ge(dve_mask, v + 1)
                        if v >= 4:
                            dve.wait_ge(dve_nm, v - 3)
                        nc.vector.tensor_reduce(mx[:, r, 0:nj], s3, AX, ALU.max).then_inc(dve_mx, 1)
                        dve.wait_ge(dve_mx, v + 1)
                        if u:
                            dve.wait_ge(act_p, v - 3)
                        nc.vector.tensor_scalar(nmx[:, r, 0:nj], mx[:, r, 0:nj], -DH ** -0.5, None,
                                                ALU.mult).then_inc(dve_nm, 1)

                maxima(0)
                for u in range(len(units)):
                    if u + 1 < len(units):
                        maxima(u + 1)
                    for r in (1, 3):
                        dve.wait_ge(pe_pt, 4 * u + r + 1)
                        if u:
                            dve.wait_ge(pe_pv, u)
                        nc.vector.tensor_copy(prob_t[:, r], bank[5][:, :]).then_inc(dve_pt, 1)
                    if units[u][2][-1] == 3:
                        t = 2 * units[u][0] + units[u][1]
                        nc.vector.reciprocal(rrs[:, t, :], rs[:, t, :]).then_inc(dve_rr, 1)
                        dve.wait_ge(dve_rr, t + 1)
                        dve.wait_ge(pe_pv, u + 1)
                        if t:
                            dve.wait_ge(pe_at, t)
                        nc.vector.tensor_tensor(att.rearrange("p (h d) -> p h d", d=DH),
                                                bank[6][:, 0:D].rearrange("p (h d) -> p h d", d=DH),
                                                bc(rrs[:, t, :].unsqueeze(2), [P, AH, DH]), ALU.mult).then_inc(dve_att, 1)
                        dve.wait_ge(act_at, t + 1)
                        if t:
                            dve.wait_ge(pe_wo, t)
                        nc.vector.tensor_tensor(att_t[:, 1].rearrange("p k q -> p (k q)"), bank[7][:, 0:D],
                                                att_t[:, 0].rearrange("p k q -> p (k q)").bitcast(F32),
                                                ALU.subtract).then_inc(dve_at, 1)
                        dve.wait_ge(pe_wo, t + 1)
                        if t:
                            dve.wait_ge(dve_x, t)
                        nc.vector.tensor_tensor(otmp, bank[7][:, D:2 * D], mod[:, t // 2, 2 * D:3 * D],
                                                ALU.mult).then_inc(dve_o, 1)
                        dve.wait_ge(dve_o, t + 1)
                        nc.vector.tensor_tensor(x[:, t, :], x[:, t, :], otmp, ALU.add).then_inc(dve_x, 1)

        take = carver()
        r_raw = take(D, parts=E1)
        bias_row = take(E1)
        assert take(1).offset % ARENA <= 8000
        takeh = carver(halves, HALVES)
        r_t = takeh(2, KD, E1)
        gu_t = takeh(2, 2, 4, F1)
        dn_t = take(2, D)
        s_sb = take(2, 512)
        a_sb = take(2, 512)
        sc1, ch1, eq1, sel1, w1, comb = (take(NT, E1) for _ in range(6))
        s1, rc1 = take(NT), take(NT)
        m8 = take(NT, 8)
        i8 = take(NT, 8).bitcast(U32)
        i8f = take(NT, 8)
        names = ("ld_r pe_rt act_rt pe_lg act_sc dve_rt dve_comb pe_wg act_wg pe_wd act_wd pe_up act_s dve_a pe_dn "
                 "out_a out_d dve_fin dve_x ld_out dve_r dve_wg").split()
        g_ = {n: sem("e_" + n) for n in names}
        (ld_r, pe_rt, act_rt, pe_lg1, act_sc, dve_rt1, dve_comb1, pe_wg, act_wg, pe_wd, act_wd, pe_up1, act_s1, dve_a1,
         pe_dn1, act_y1, dve_y1, dve_fin, dve_x1, st_out, dve_r, dve_wg) = (g_[n] for n in names)
        order = [E1] + list(range(EARLY, E1)) + list(range(EARLY))
        NE = len(order)

        with nc.Block() as block:
            @block.sync
            def _(sp):
                load_gate(sp, 3)
                sp.dma_start(r_raw, A["L1_ffn_router_w"]).then_inc(ld_r, 16)
                sp.dma_start(bias_row, A["L1_ffn_router_bias"].partition_broadcast(P)).then_inc(ld_r, 16)
                load_experts(sp, 0, EARLY)
                ov = out.rearrange("b (c p) d -> p (b c) d", p=P)
                for t in range(NT):
                    sp.wait_ge(dve_x1, t + 1)
                    sp.dma_start(ov[:, t, :], x[:, t, :]).then_inc(st_out, 16)
                sp.wait_ge(st_out, 16 * NT)

            @block.tensor
            def _(pe):
                pe.wait_ge(ld_r, 32)
                for k in range(KD):
                    last = nc.tensor.transpose(bank[4][:, k * E1:(k + 1) * E1], r_raw[:, k * P:(k + 1) * P],
                                               ident[0:E1, 0:E1])
                last.then_inc(pe_rt, 1)
                norm_pe(pe, 3, bank[0:2])
                pe.wait_ge(dve_r, 1)
                pe.wait_ge(norm_hT, 4 * NT // 2)
                for t in range(NT):
                    for k in range(KD):
                        ts = slice(t * P, (t + 1) * P)
                        last = mm3(bank[5][:, t * E1:(t + 1) * E1], (hT_hi[:, k, ts], hT_lo[:, k, ts]),
                                   (r_t[:, 0, k, :], r_t[:, 1, k, :]), k == 0, k == KD - 1)
                last.then_inc(pe_lg1, 1)
                early = 16 * (3 + 2 + E1 - EARLY)
                late_all = early + 16 * (2 + EARLY)

                def weights(n):
                    e = order[n]
                    pe.wait_ge(ld_w1, late_all if e < EARLY else early)
                    if n:
                        pe.wait_ge(dve_wg, n)
                        pe.wait_ge(act_wd, n)
                    for s_ in range(2):
                        for k in range(KD):
                            last = nc.tensor.transpose(bank[0][:, (2 * s_ + k) * P:(2 * s_ + k + 1) * P],
                                                       w1_raw[:, e, s_, k * P:(k + 1) * P], ident)
                    last.then_inc(pe_wg, 1)
                    for o in range(2):
                        last = nc.tensor.transpose(bank[1][:, o * P:(o + 1) * P], w1_raw[:, e, 2, o * P:(o + 1) * P], ident)
                    last.then_inc(pe_wd, 1)

                def up(n, th):
                    u = 2 * n + th
                    pe.wait_ge(dve_wg, n + 1)
                    if u >= 2:
                        pe.wait_ge(dve_a1, u - 1)
                    if u == 1:
                        pe.wait_ge(act_sc, 1)
                    for s_, bk in ((0, bank[2 + th]), (1, bank[4 + th])):
                        for k in range(KD):
                            tok = slice(th * 512, (th + 1) * 512)
                            last = mm3(bk[:, :], (gu_t[:, n % 2, 0, 2 * s_ + k, :], gu_t[:, n % 2, 1, 2 * s_ + k, :]),
                                       (hT_hi[:, k, tok], hT_lo[:, k, tok]), k == 0, k == KD - 1)
                    last.then_inc(pe_up1, 1)

                def down(n, th):
                    u = 2 * n + th
                    pe.wait_ge(dve_a1, u + 1)
                    pe.wait_ge(act_wd, n + 1)
                    for pr in range(2):
                        v = 2 * u + pr
                        if v >= 2:
                            w = v - 2
                            pe.wait_ge(*((act_y1, w + 1) if w < 4 else (dve_y1, 2 * (w - 4) + 2)))
                        for q_ in range(2):
                            last = nc.tensor.matmul(bank[6 + pr][:, q_ * D:(q_ + 1) * D],
                                                    a_sb[:, th, (2 * pr + q_) * P:(2 * pr + q_ + 1) * P], dn_t[:, n % 2, :],
                                                    start=True, stop=True)
                        last.then_inc(pe_dn1, 1)

                weights(0)
                up(0, 0)
                up(0, 1)
                for n in range(NE):
                    if n + 1 < NE:
                        weights(n + 1)
                    down(n, 0)
                    if n + 1 < NE:
                        up(n + 1, 0)
                    down(n, 1)
                    if n + 1 < NE:
                        up(n + 1, 1)

            @block.gpsimd
            def _(pool):
                norm_pool(pool, 3)

            @block.scalar
            def _(act):
                act.wait_ge(pe_rt, 1)
                nc.scalar.copy(r_t[:, 0].rearrange("p k e -> p (k e)"), bank[4][:, 0:KD * E1]).then_inc(act_rt, 1)
                norm_act(act, 3)
                norm_act_copy(act, 3, bank[0:2])
                act.wait_ge(pe_lg1, 1)
                nc.scalar.activation(sc1.rearrange("p t e -> p (t e)"), bank[5][:, 0:P], ACT.Sigmoid).then_inc(act_sc, 1)

                def weights(n):
                    act.wait_ge(pe_wg, n + 1)
                    if n >= 2:
                        act.wait_ge(pe_up1, 2 * (n - 1))
                    nc.scalar.copy(gu_t[:, n % 2, 0].rearrange("p a b -> p (a b)"), bank[0][:, :]).then_inc(act_wg, 1)
                    act.wait_ge(pe_wd, n + 1)
                    if n >= 2:
                        act.wait_ge(pe_dn1, 4 * (n - 1))
                    nc.scalar.copy(dn_t[:, n % 2], bank[1][:, 0:D]).then_inc(act_wd, 1)

                weights(0)
                for n in range(NE):
                    for th in range(2):
                        u = 2 * n + th
                        act.wait_ge(pe_up1, u + 1)
                        if u >= 2:
                            act.wait_ge(dve_a1, u - 1)
                        nc.scalar.activation(s_sb[:, th], bank[2 + th][:, :], ACT.Silu).then_inc(act_s1, 1)
                        if th == 0 and n + 1 < NE:
                            weights(n + 1)
                    if n == 0:
                        for v in range(4):
                            act.wait_ge(pe_dn1, v + 1)
                            nc.scalar.copy(y_acc[:, 2 * v:2 * v + 2, :],
                                           bank[6 + v % 2][:, :].rearrange("p (a b) -> p a b", a=2)).then_inc(act_y1, 1)

            @block.vector
            def _(dve):
                for t in range(NT):
                    norm_stats(3, t)
                norm_dve(dve, 3)
                dve.wait_ge(act_rt, 1)
                nc.vector.tensor_tensor(r_t[:, 1].rearrange("p k e -> p (k e)"), bank[4][:, 0:KD * E1],
                                        r_t[:, 0].rearrange("p k e -> p (k e)").bitcast(F32),
                                        ALU.subtract).then_inc(dve_r, 1)
                norm_dve_lo(dve, 3, bank[0:2])

                def weights_lo(n):
                    dve.wait_ge(act_wg, n + 1)
                    if n >= 2:
                        dve.wait_ge(pe_up1, 2 * (n - 1))
                    nc.vector.tensor_tensor(gu_t[:, n % 2, 1].rearrange("p a b -> p (a b)"), bank[0][:, :],
                                            gu_t[:, n % 2, 0].rearrange("p a b -> p (a b)").bitcast(F32),
                                            ALU.subtract).then_inc(dve_wg, 1)

                def product(u):
                    th = u % 2
                    dve.wait_ge(act_s1, u + 1)
                    if u >= 2:
                        dve.wait_ge(pe_dn1, 2 * (u - 1))
                    nc.vector.tensor_tensor(a_sb[:, th], bank[4 + th][:, :], s_sb[:, th], ALU.mult).then_inc(dve_a1, 1)

                def sums(u):
                    n, th = u // 2, u % 2
                    e = order[n]
                    for pr in range(2):
                        v = 2 * u + pr
                        dve.wait_ge(pe_dn1, v + 1)
                        for q_ in range(2):
                            t = 4 * th + 2 * pr + q_
                            if n >= 2:
                                dve.wait_ge(dve_y1, NT * (n - 2) + t + 1)
                            nc.vector.scalar_tensor_tensor(out=y_acc[:, t, :], in0=bank[6 + pr][:, q_ * D:(q_ + 1) * D],
                                                           scalar=comb[:, t, e:e + 1], in1=y_acc[:, t, :],
                                                           op0=ALU.mult, op1=ALU.add).then_inc(dve_y1, 1)

                weights_lo(0)
                product(0)
                weights_lo(1)
                product(1)
                dve.wait_ge(ld_r, 32)
                dve.wait_ge(act_sc, 1)
                nc.vector.tensor_tensor(ch1, sc1, bc(bias_row.unsqueeze(1), [P, NT, E1]), ALU.add).then_inc(dve_rt1, 1)
                dve.wait_ge(dve_rt1, 1)
                n = topk_select(dve, ch1, K1, dve_rt1, 1, eq1, sel1, m8, i8, i8f)
                dve.wait_ge(dve_rt1, n)
                nc.vector.tensor_tensor(w1, sc1, sel1, ALU.mult).then_inc(dve_rt1, 1)
                dve.wait_ge(dve_rt1, n + 1)
                nc.vector.tensor_reduce(s1, w1, AX, ALU.add).then_inc(dve_rt1, 1)
                dve.wait_ge(dve_rt1, n + 2)
                nc.vector.tensor_scalar(s1, s1, 1e-20, None, ALU.add).then_inc(dve_rt1, 1)
                dve.wait_ge(dve_rt1, n + 3)
                nc.vector.reciprocal(rc1, s1).then_inc(dve_rt1, 1)
                dve.wait_ge(dve_rt1, n + 4)
                nc.vector.tensor_tensor(comb, w1, bc(rc1.unsqueeze(2), [P, NT, E1]), ALU.mult).then_inc(dve_comb1, 1)
                dve.wait_ge(dve_comb1, 1)
                dve.wait_ge(act_y1, 4)
                for u in range(2, 2 * NE):
                    product(u)
                    if u % 2 == 0 and u // 2 + 1 < NE:
                        weights_lo(u // 2 + 1)
                    if u >= 3:
                        sums(u - 1)
                sums(2 * NE - 1)
                dve.wait_ge(ld_gt, 64)
                for t in range(NT):
                    dve.wait_ge(dve_y1, NT * (NE - 2) + t + 1)
                    nc.vector.tensor_tensor(y_acc[:, t, :], y_acc[:, t, :], mod[:, t // 2, 2 * D:3 * D],
                                            ALU.mult).then_inc(dve_fin, 1)
                for t in range(NT):
                    dve.wait_ge(dve_fin, t + 1)
                    nc.vector.tensor_tensor(x[:, t, :], x[:, t, :], y_acc[:, t, :], ALU.add).then_inc(dve_x1, 1)


_INS = ['L0_attn_hidden_states', 'L0_attn_Wz', 'L0_attn_Wx', 'L0_attn_WB', 'L0_attn_WC', 'L0_attn_Wdt',
        'L0_attn_conv_w', 'L0_attn_conv_b', 'L0_attn_dt_bias', 'L0_attn_A_log', 'L0_attn_D', 'L0_attn_norm_w',
        'L0_attn_Wout', 'L0_ffn_gate_w', 'L0_ffn_w_gate', 'L0_ffn_w_up', 'L0_ffn_w_down', 'L0_ffn_ws_gate',
        'L0_ffn_ws_up', 'L0_ffn_ws_down', 'L0_c', 'L0_wmod', 'L1_attn_Wq', 'L1_attn_Wk', 'L1_attn_Wv', 'L1_attn_Wo',
        'L1_ffn_router_w', 'L1_ffn_router_bias', 'L1_ffn_expert_gate_w', 'L1_ffn_expert_up_w',
        'L1_ffn_expert_down_w', 'L1_ffn_shared_gate_w', 'L1_ffn_shared_up_w', 'L1_ffn_shared_down_w', 'L1_c',
        'L1_wmod']


def constants():
    import numpy as np
    k = np.arange(P)[:, None]
    j = np.arange(P)[None, :]
    c = np.zeros((P, C_ALL), np.float32)
    c[:, C_ID:C_ID + P] = k == j
    c[:, C_GT:C_GT + P] = k > j
    c[:, C_LE:C_LE + P] = k <= j
    c[:, C_ONE:C_ONE + P] = 1.0
    c[:, C_LE2:C_LE2 + P] = k <= j
    c[:, C_LT:C_LT + P] = k < j
    c[:, C_NEG:C_NEG + P] = np.where(j > k, -1e30, 0.0)
    c[:, C_IOTA:C_IOTA + P] = np.broadcast_to(j, (P, P))
    theta = (np.float32(10000.0) ** (np.float32(-2.0) * np.arange(DH // 2, dtype=np.float32) / np.float32(DH)))
    ang = np.arange(S, dtype=np.float32)[:, None] * theta.astype(np.float32)[None, :]
    cos, sin = np.cos(ang).astype(np.float32), np.sin(ang).astype(np.float32)
    tab = np.zeros((2, S, DH), np.float32)
    tab[0, :, 0::2] = cos
    tab[0, :, 1::2] = cos
    tab[1, :, 0::2] = -sin
    tab[1, :, 1::2] = sin
    c[:, C_ROPE:] = tab.reshape(2, 2, P, DH).transpose(2, 0, 1, 3).reshape(P, -1)
    return c


def kernel(**inputs):
    import numpy as _np
    import concourse.bacc as _bacc
    from concourse import mybir as _mybir
    from concourse.bass_utils import run_bass_kernel_spmd as _run

    nc = _bacc.Bacc("TRN2", target_bir_lowering=False, num_devices=1)
    arrays, aps = {}, {}
    for name in _INS:
        a = _np.ascontiguousarray(inputs[name])
        arrays[f"in_{name}"] = a
        aps[name] = nc.dram_tensor(f"in_{name}", a.shape, _mybir.dt.from_np(a.dtype), kind="ExternalInput").ap()
    arrays["const_in"] = constants()
    aps["const"] = nc.dram_tensor("const_in", arrays["const_in"].shape, F32, kind="ExternalInput").ap()
    aps["mod_rows"] = nc.dram_tensor("mod_rows", (2, B, 6 * D), F32, kind="Internal").ap()
    out = nc.dram_tensor("out_0", (B, S, D), F32, kind="ExternalOutput").ap()
    build(nc, aps, out)
    r = _run(nc, [arrays], core_ids=[0])
    return r.results[0]["out_0"]
```

```python
from contextlib import ExitStack

import concourse.bass as bass
from concourse import mybir

F32 = mybir.dt.float32
F32R = mybir.dt.float32r
U32 = mybir.dt.uint32
ALU = mybir.AluOpType
ACT = mybir.ActivationFunctionType
AX = mybir.AxisListType.X

P = 128
B, S, D = 4, 256, 256
NT = B * S // P
KD = D // P
HEADS, HD, GROUPS, NST = 64, 64, 8, 128
HG = HEADS // GROUPS
GC = HG * HD
XT = GC // P
TAPS = 4
INTER = HEADS * HD
E0, I0, CAP, IT = 16, 176, 128, 88
IS = 352
NIS = IS // IT
E1, F1, K1 = 16, 128, 4
AH, DH = 16, 16
EPS = 1e-5
CT = (INTER + 2 * GROUPS * NST) // P
COLS = (TAPS + 1) * CT + 2 * (INTER // P) + 2 * KD * B
C_ID, C_GT, C_LE, C_ONE, C_LE2, C_LT, C_NEG, C_IOTA, C_ROPE = [P * i for i in range(9)]
C_ALL = C_ROPE + 2 * 2 * DH
ARENA = 23610
HALVES = 14340


def bc(ap, shape):
    return ap.broadcast_to(shape)


def build(nc, A, out):
    with ExitStack() as ctx:
        def sb(name, shape, dt=F32):
            return ctx.enter_context(nc.sbuf_tensor(name, shape, dt))

        def sem(name):
            return ctx.enter_context(nc.semaphore(name))

        bank = [ctx.enter_context(nc.psum_tensor(f"bank{i}", [P, 512], F32)) for i in range(8)]
        const = sb("const", [P, C_ALL])
        ident = const[:, C_ID:C_ID + P]
        tri_gt = const[:, C_GT:C_GT + P]
        tri_le = const[:, C_LE:C_LE + P]
        ones = const[:, C_ONE:C_ONE + P]
        causal3 = const[:, C_LE:C_LE + 3 * P]
        tri_lt = const[:, C_LT:C_LT + P]
        neg_mask = const[:, C_NEG:C_NEG + P]
        iota = const[:, C_IOTA:C_IOTA + P]
        rope = const[:, C_ROPE:C_ALL].rearrange("p (s c d) -> p s c d", s=2, c=2)
        x = sb("x", [P, NT, D])
        h = sb("h", [P, NT, D])
        hT_hi = sb("hT_hi", [P, KD, NT * P], F32R)
        hT_lo = sb("hT_lo", [P, KD, NT * P], F32R)
        tri_gt_r = sb("tri_gt_r", [P, P], F32R)
        cs = sb("cs", [P, 2 * KD * B])
        mod = sb("mod", [P, B, 3 * D])
        stats = sb("stats", [P, NT, 6])
        mv = sb("mv", [P, NT, 2])
        rstd = sb("rstd", [P, NT])
        std = sb("std", [P, NT])
        nmr = sb("nmr", [P, NT])
        y_acc = sb("y_acc", [P, NT, D])
        ss = sb("ss", [P, NT, GROUPS])
        arena = sb("arena", [P, ARENA])
        halves = sb("halves", [P, HALVES], F32R)

        def carver(arena=arena, size=ARENA):
            at = [0]

            def take(*shape, parts=P):
                n = 1
                for s in shape:
                    n *= s
                assert at[0] + n <= size, at[0] + n
                v = arena[0:parts, at[0]:at[0] + n]
                at[0] += n
                if len(shape) == 1:
                    return v
                names = "abcd"[:len(shape)]
                return v.rearrange("p (" + " ".join(names) + ") -> p " + " ".join(names),
                                   **{c: s for c, s in zip(names, shape)})
            return take

        norm_chain = sem("norm_chain")
        norm_std = sem("norm_std")
        norm_x = sem("norm_x")
        norm_h = sem("norm_h")
        norm_tr = sem("norm_tr")
        norm_hi = sem("norm_hi")
        norm_hT = sem("norm_hT")
        ld_ss, ld_gt = sem("ld_ss"), sem("ld_gt")

        NC = 3 * NT + 3

        def norm_stats(n, t):
            nc.vector.bn_stats(stats[:, t, :], x[:, t, :]).then_inc(norm_chain, 1)

        def norm_dve(dve, n, meanwhile=None):
            n0 = n * NC
            for t in range(NT):
                dve.wait_ge(norm_chain, n0 + t + 1)
                nc.vector.bn_aggr(mv[:, t, :], stats[:, t, :]).then_inc(norm_chain, 1)
            dve.wait_ge(norm_chain, n0 + 2 * NT)
            nc.vector.tensor_scalar(std[:, :], mv[:, :, 1], EPS, None, ALU.add).then_inc(norm_chain, 1)
            if meanwhile:
                meanwhile()
            dve.wait_ge(norm_std, n + 1)
            nc.vector.reciprocal(rstd[:, :], std[:, :]).then_inc(norm_chain, 1)
            dve.wait_ge(norm_chain, n0 + 2 * NT + 2)
            nc.vector.scalar_tensor_tensor(out=nmr[:, :], in0=mv[:, :, 0], scalar=-1.0, in1=rstd[:, :],
                                           op0=ALU.mult, op1=ALU.mult).then_inc(norm_chain, 1)
            dve.wait_ge(ld_ss, 16 * (n + 1))
            for t in range(NT):
                dve.wait_ge(norm_x, n * NT + t + 1)
                nc.vector.tensor_tensor(h[:, t, :], h[:, t, :], mod[:, t // 2, D:2 * D], ALU.mult).then_inc(norm_chain, 1)

        def norm_pool(pool, n):
            pool.wait_ge(ld_ss, 16 * (n + 1))
            for t in range(NT):
                pool.wait_ge(norm_chain, n * NC + 2 * NT + 3 + t + 1)
                nc.gpsimd.tensor_tensor(h[:, t, :], h[:, t, :], mod[:, t // 2, 0:D], ALU.add).then_inc(norm_h, 1)

        def norm_dve_lo(dve, n, banks):
            for j in range(NT // 2):
                dve.wait_ge(norm_hi, n * NT // 2 + j + 1)
                cols = slice(2 * j * P, (2 * j + 2) * P)
                nc.vector.tensor_tensor(hT_lo[:, :, cols], banks[j % 2][:, :].rearrange("p (k t) -> p k t", k=KD),
                                        hT_hi[:, :, cols].bitcast(F32), ALU.subtract).then_inc(norm_hT, 1)

        def norm_act(act, n):
            act.wait_ge(norm_chain, n * NC + 2 * NT + 1)
            nc.scalar.activation(std[:, :], std[:, :], ACT.Sqrt).then_inc(norm_std, 1)
            act.wait_ge(norm_chain, n * NC + 2 * NT + 3)
            for t in range(NT):
                nc.scalar.activation(h[:, t, :], x[:, t, :], ACT.Identity, bias=nmr[:, t:t + 1],
                                     scale=rstd[:, t:t + 1]).then_inc(norm_x, 1)

        def norm_pe(pe, n, banks):
            for j in range(NT // 2):
                pe.wait_ge(norm_h, n * NT + 2 * j + 2)
                if j >= 2:
                    pe.wait_ge(norm_hT, n * NT // 2 + j - 1)
                for k in range(KD):
                    for q in range(2):
                        last = nc.tensor.transpose(banks[j % 2][:, (2 * k + q) * P:(2 * k + q + 1) * P],
                                                   h[:, 2 * j + q, k * P:(k + 1) * P], ident)
                last.then_inc(norm_tr, 1)

        def norm_act_copy(act, n, banks):
            for j in range(NT // 2):
                act.wait_ge(norm_tr, n * NT // 2 + j + 1)
                nc.scalar.copy(hT_hi[:, :, 2 * j * P:(2 * j + 2) * P],
                               banks[j % 2][:, :].rearrange("p (k t) -> p k t", k=KD)).then_inc(norm_hi, 1)

        def mm3(out, left, right, first, last):
            nc.tensor.matmul(out, left[0], right[0], start=first, stop=False)
            nc.tensor.matmul(out, left[0], right[1], start=False, stop=False)
            return nc.tensor.matmul(out, left[1], right[0], start=False, stop=last)

        rows = A["mod_rows"]
        pe_mod, mod_chain, st_mod, ld_mod1 = sem("pe_mod"), sem("mod_chain"), sem("st_mod"), sem("ld_mod1")
        MC = 9

        def load_shift_scale(eng, m):
            eng.dma_start(mod[:, :, 0:2 * D], rows[m // 2, :, m % 2 * 3 * D:(m % 2 * 3 + 2) * D]
                          .partition_broadcast(P)).then_inc(ld_ss, 16)

        def load_gate(eng, m):
            eng.dma_start(mod[:, :, 2 * D:3 * D], rows[m // 2, :, (m % 2 * 3 + 2) * D:(m % 2 * 3 + 3) * D]
                          .partition_broadcast(P)).then_inc(ld_gt, 16)

        take = carver()
        raw_x = take(KD, GC)
        raw_b = take(KD, NST)
        raw_c = take(KD, NST)
        raw_z = take(KD, GC)
        w_out = take(2, XT, D)
        cols = take(COLS)
        conv_w = cols[:, 0:TAPS * CT].rearrange("p (k t) -> p t k", k=TAPS)
        conv_b = cols[:, TAPS * CT:(TAPS + 1) * CT]
        norm_w = cols[:, (TAPS + 1) * CT:(TAPS + 1) * CT + INTER // P]
        d_col = cols[:, COLS - 2 * KD * B - INTER // P:COLS - 2 * KD * B]
        c_t = cols[:, COLS - 2 * KD * B:COLS]
        a_log = take(HEADS)
        dt_bias = take(HEADS)
        dt = take(NT, HEADS)
        la = take(2, NT, HEADS)
        dte = take(B, HEADS)
        ef = take(2, B, HEADS)
        base = take(1).offset % ARENA
        xc = take(2, 6, S)
        acc = take(3, 2, S)
        ebuf = take(2, 4, P)
        mbuf = take(2, 4, 4, P)
        xtok = take(2, GC)
        xd = take(2, GC)
        xe = take(GC)
        gm = take(2, 3 * P)
        gt = take(2, XT, S)
        ef_wide = take(GC)
        sg = h[:, :, :].rearrange("p (i m) d -> p i m d", i=2)
        sq = mod[:, :, 0:S]
        ef_t = mod[:, :, S:S + P]
        off = mod[:, :, S + P:S + 2 * P]
        takeh = carver(halves, HALVES)
        w_x = takeh(2, 2, KD, GC)
        w_b = takeh(2, 2, KD, NST)
        w_c = takeh(2, 2, KD, NST)
        w_z = takeh(2, 2, KD, GC)
        rbuf = takeh(2, 4, 4, P)
        take_t = carver()
        take_t(base)
        wmod = take_t(2, KD, 6 * D)
        mrow = take_t(2, 6 * D, parts=B)
        wdt = take_t(KD, HEADS)
        tmp = [take_t(NT * HEADS) for _ in range(7)]
        dt_t = take_t(NT * P, parts=HEADS)
        conv_raw = take_t(P * TAPS, parts=CT)
        conv_w_raw = conv_raw.rearrange("t (p k) -> t k p", k=TAPS)
        conv_b_raw = take_t(P, parts=CT)
        norm_w_raw = take_t(P, parts=INTER // P)
        d_raw = take_t(HG // XT, parts=INTER // P)
        d_wide = take_t(P, parts=INTER // P)
        c_raw = take_t(2, D, parts=B)
        mscr = take_t(2, D, parts=B)
        la_r = sb("la_r", [P, NT, HEADS], F32R)
        wdt_r = rbuf[:, 0, 0, :].rearrange("p s (k n) -> p s k n", k=KD)

        (ld_x, ld_const, ld_mod, ld_row, ld_conv, act_cs, dt_chain, act_exp, pe_dt, pe_ef, act_ef,
         dve_setup, pe_cols, act_cols, dve_alog, act_wdt, dve_wdt, ld_a, act_whi, pool_wlo, dve_dw) = (
            sem(n) for n in "ld_x ld_const ld_mod ld_row ld_conv act_cs dt_chain act_exp pe_dt pe_ef act_ef "
            "dve_setup pe_cols act_cols dve_alog act_wdt dve_wdt ld_a act_whi pool_wlo dve_dw".split())

        x_in = A["L0_attn_hidden_states"].rearrange("b (c p) d -> p (b c) d", p=P)
        ld_o = [sem("ld_o_even"), sem("ld_o_odd")]
        NW = 4
        parts = ((raw_x, w_x), (raw_b, w_b), (raw_c, w_c), (raw_z, w_z))

        def load_group(eng, g):
            for raw, nm, n in ((raw_x, "L0_attn_Wx", GC), (raw_b, "L0_attn_WB", NST), (raw_c, "L0_attn_WC", NST),
                               (raw_z, "L0_attn_Wz", GC)):
                eng.dma_start(raw, A[nm][:, g * n:(g + 1) * n].rearrange("(k p) n -> p k n", p=P)).then_inc(ld_a, 16)

        def load_out(eng, g):
            eng.dma_start(w_out[:, g % 2], A["L0_attn_Wout"][g * GC:(g + 1) * GC, :]
                          .rearrange("(k p) n -> p k n", p=P)).then_inc(ld_o[g % 2], 16)

        def split_hi(act, g):
            act.wait_ge(ld_a, 16 * NW * (g + 1))
            for raw, w in parts:
                nc.scalar.copy(w[:, g % 2, 0], raw).then_inc(act_whi, 1)

        def split_lo(pool, g):
            for i_, (raw, w) in enumerate(parts):
                pool.wait_ge(act_whi, NW * g + i_ + 1)
                nc.gpsimd.tensor_tensor(w[:, g % 2, 1], raw, w[:, g % 2, 0].bitcast(F32),
                                        ALU.subtract).then_inc(pool_wlo, 1)

        mod_bank = (bank[2], bank[3], bank[7])
        dt_bank = (bank[4], bank[6])

        def mod_final(dve, layer):
            b0, b1, b2 = mod_bank
            row = mrow[:, layer]
            dve.wait_ge(pe_mod, layer + 1)
            nc.vector.tensor_copy(row[:, 0:D], b0[0:B, 0:D]).then_inc(mod_chain, 1)
            nc.vector.tensor_scalar(row[:, D:2 * D], b0[0:B, D:2 * D], 1.0, None, ALU.add).then_inc(mod_chain, 1)
            nc.vector.tensor_copy(row[:, 2 * D:4 * D], b1[0:B, :]).then_inc(mod_chain, 1)
            nc.vector.tensor_scalar(row[:, 4 * D:5 * D], b2[0:B, 0:D], 1.0, None, ALU.add).then_inc(mod_chain, 1)
            nc.vector.tensor_copy(row[:, 5 * D:6 * D], b2[0:B, D:2 * D]).then_inc(mod_chain, 1)
            g = row.rearrange("b (s r d) -> b s r d", s=2, r=3)[:, :, 2, :]
            n0 = MC * layer
            dve.wait_ge(mod_chain, n0 + 5)
            nc.vector.tensor_scalar(mscr, g, 0.0, 2.0, ALU.is_ge, ALU.mult).then_inc(mod_chain, 1)
            dve.wait_ge(mod_chain, n0 + 6)
            nc.vector.tensor_scalar(mscr, mscr, -1.0, None, ALU.add).then_inc(mod_chain, 1)
            dve.wait_ge(mod_chain, n0 + 7)
            nc.vector.tensor_tensor(g, g, mscr, ALU.mult).then_inc(mod_chain, 1)
            dve.wait_ge(mod_chain, n0 + 8)
            nc.vector.scalar_tensor_tensor(out=g, in0=g, scalar=0.25, in1=mscr,
                                           op0=ALU.max, op1=ALU.mult).then_inc(mod_chain, 1)

        with nc.Block() as block:
            @block.sync
            def _(sp):
                sp.dma_start(c_raw[:, 0], A["L0_c"]).then_inc(ld_conv, 16)
                sp.dma_start(c_raw[:, 1], A["L1_c"]).then_inc(ld_conv, 16)
                sp.dma_start(conv_raw, A["L0_attn_conv_w"].rearrange("(t p) k -> t (p k)", p=P)).then_inc(ld_conv, 16)
                sp.dma_start(conv_b_raw, A["L0_attn_conv_b"].rearrange("(t p) -> t p", p=P)).then_inc(ld_conv, 16)
                sp.dma_start(norm_w_raw, A["L0_attn_norm_w"].rearrange("(t p) -> t p", p=P)).then_inc(ld_conv, 16)
                sp.dma_start(d_raw, A["L0_attn_D"].rearrange("(t a) -> t a", a=HG // XT)).then_inc(ld_conv, 16)
                sp.dma_start(const[:, :], A["const"]).then_inc(ld_const, 16)
                sp.dma_start(wmod[:, 0], A["L0_wmod"].rearrange("(k p) n -> p k n", p=P)).then_inc(ld_mod, 16)
                sp.dma_start(x[:, :, :], x_in).then_inc(ld_x, 16)
                sp.dma_start(wmod[:, 1], A["L1_wmod"].rearrange("(k p) n -> p k n", p=P)).then_inc(ld_mod1, 16)
                sp.dma_start(wdt, A["L0_attn_Wdt"].rearrange("(k p) n -> p k n", p=P)).then_inc(ld_row, 16)
                sp.dma_start(a_log, A["L0_attn_A_log"].partition_broadcast(P)).then_inc(ld_row, 16)
                sp.dma_start(dt_bias, A["L0_attn_dt_bias"].partition_broadcast(P)).then_inc(ld_row, 16)
                load_group(sp, 0)
                load_out(sp, 0)
                load_out(sp, 1)
                for layer in range(2):
                    sp.wait_ge(mod_chain, MC * (layer + 1))
                    sp.dma_start(rows[layer], mrow[:, layer]).then_inc(st_mod, 16)
                    if layer == 0:
                        sp.wait_ge(st_mod, 16)
                        load_shift_scale(sp, 0)
                        load_gate(sp, 0)
                sp.wait_ge(st_mod, 32)

            @block.scalar
            def _(act):
                act.wait_ge(pe_cols, 1)
                nc.scalar.copy(cols, bank[6][:, 0:COLS]).then_inc(act_cols, 1)
                act.wait_ge(act_cols, 1)
                nc.scalar.activation(cs[:, :], c_t, ACT.Silu).then_inc(act_cs, 1)
                norm_act(act, 0)
                act.wait_ge(ld_row, 48)
                nc.scalar.copy(wdt_r[:, 0], wdt).then_inc(act_wdt, 1)
                norm_act_copy(act, 0, bank[0:2])
                for th in range(2):
                    act.wait_ge(pe_dt, th + 1)
                    nc.scalar.copy(dt_t[:, th * 512:(th + 1) * 512], dt_bank[th][0:HEADS, :]).then_inc(act_wdt, 1)
                act.wait_ge(dve_alog, 1)
                nc.scalar.activation(a_log, a_log, ACT.Exp).then_inc(act_exp, 1)
                act.wait_ge(dt_chain, 2)
                nc.scalar.activation(tmp[1], tmp[1], ACT.Exp).then_inc(act_exp, 1)
                split_hi(act, 0)
                act.wait_ge(pe_ef, 1)
                nc.scalar.activation(ef.rearrange("p a b h -> p (a b h)"), bank[4][:, :], ACT.Exp).then_inc(act_ef, 1)

            @block.gpsimd
            def _(pool):
                norm_pool(pool, 0)
                split_lo(pool, 0)

            @block.tensor
            def _(pe):
                pe.wait_ge(ld_const, 16)
                pe.wait_ge(ld_conv, 96)
                for k in range(TAPS):
                    nc.tensor.transpose(bank[6][:, k * CT:(k + 1) * CT], conv_w_raw[:, k, :], ident[0:CT, 0:CT])
                nc.tensor.transpose(bank[6][:, TAPS * CT:(TAPS + 1) * CT], conv_b_raw, ident[0:CT, 0:CT])
                n0 = (TAPS + 1) * CT
                nc.tensor.transpose(bank[6][:, n0:n0 + INTER // P], norm_w_raw, ident[0:INTER // P, 0:INTER // P])
                n0 += INTER // P
                pe.wait_ge(dve_dw, 1)
                nc.tensor.transpose(bank[6][:, n0:n0 + INTER // P], d_wide, ident[0:INTER // P, 0:INTER // P])
                n0 += INTER // P
                for k in range(2 * KD):
                    last = nc.tensor.transpose(bank[6][:, n0 + k * B:n0 + (k + 1) * B],
                                               c_raw[:, k // KD, k % KD * P:(k % KD + 1) * P], ident[0:B, 0:B])
                last.then_inc(pe_cols, 1)
                pe.wait_ge(ld_mod, 16)
                pe.wait_ge(act_cs, 1)

                def mod_products(layer):
                    for n in range(3):
                        for k in range(KD):
                            c0 = (layer * KD + k) * B
                            last = nc.tensor.matmul(mod_bank[n][0:B, :], cs[:, c0:c0 + B],
                                                    wmod[:, layer, k, n * 512:(n + 1) * 512], start=k == 0, stop=k == KD - 1)
                    last.then_inc(pe_mod, 1)

                mod_products(0)
                pe.wait_ge(ld_mod1, 16)
                pe.wait_ge(mod_chain, 5)
                mod_products(1)
                norm_pe(pe, 0, bank[0:2])
                pe.wait_ge(dve_wdt, 1)
                for th in range(2):
                    pe.wait_ge(norm_hT, NT // 4 * (th + 1))
                    tok = slice(th * 512, (th + 1) * 512)
                    for k in range(KD):
                        last = mm3(dt_bank[th][0:HEADS, :], (wdt_r[:, 0, k, :], wdt_r[:, 1, k, :]),
                                   (hT_hi[:, k, tok], hT_lo[:, k, tok]), k == 0, k == KD - 1)
                    last.then_inc(pe_dt, 1)
                pe.wait_ge(act_wdt, 3)
                for t in range(NT):
                    last = nc.tensor.transpose(bank[5][:, t * HEADS:(t + 1) * HEADS], dt_t[:, t * P:(t + 1) * P],
                                               ident[0:HEADS, 0:HEADS])
                last.then_inc(pe_dt, 1)
                pe.wait_ge(dve_setup, 1)
                for b in range(B):
                    nc.tensor.matmul(bank[4][:, b * HEADS:(b + 1) * HEADS], tri_gt, la[:, 0, 2 * b, :],
                                     start=True, stop=True)
                    last = nc.tensor.matmul(bank[4][:, (B + b) * HEADS:(B + b + 1) * HEADS], tri_le,
                                            la[:, 0, 2 * b + 1, :], start=True, stop=True)
                last.then_inc(pe_ef, 1)

            @block.vector
            def _(dve):
                dve.wait_ge(ld_conv, 96)
                nc.vector.tensor_copy(d_wide.rearrange("t (a d) -> t a d", d=HD),
                                      bc(d_raw.unsqueeze(2), [INTER // P, HG // XT, HD])).then_inc(dve_dw, 1)
                nc.vector.memset(y_acc[:, :, :], 0.0)
                dve.wait_ge(ld_const, 16)
                nc.vector.tensor_copy(tri_gt_r[:, :], tri_gt)
                dve.wait_ge(ld_row, 48)
                nc.vector.tensor_scalar(a_log, a_log, 88.0, None, ALU.min).then_inc(dve_alog, 1)
                mod_final(dve, 0)
                dve.wait_ge(ld_x, 16)
                for t in range(NT):
                    norm_stats(0, t)
                norm_dve(dve, 0)
                dve.wait_ge(act_wdt, 1)
                nc.vector.tensor_tensor(wdt_r[:, 1], wdt, wdt_r[:, 0].bitcast(F32), ALU.subtract).then_inc(dve_wdt, 1)
                norm_dve_lo(dve, 0, bank[0:2])
                mod_final(dve, 1)
                dve.wait_ge(pe_dt, 3)
                v3 = [t_.rearrange("p (t n) -> p t n", t=NT) for t_ in tmp]
                nc.vector.tensor_tensor(v3[0], bank[5][:, :].rearrange("p (t n) -> p t n", t=NT),
                                        bc(dt_bias.unsqueeze(1), [P, NT, HEADS]), ALU.add).then_inc(dt_chain, 1)
                dve.wait_ge(dt_chain, 1)
                nc.vector.scalar_tensor_tensor(out=tmp[1], in0=tmp[0], scalar=-1.0, in1=tmp[0],
                                               op0=ALU.mult, op1=ALU.min).then_inc(dt_chain, 1)
                nc.vector.tensor_scalar(tmp[2], tmp[0], 0.0, None, ALU.max).then_inc(dt_chain, 1)
                dve.wait_ge(act_exp, 2)
                nc.vector.tensor_scalar(tmp[3], tmp[1], 2.0, None, ALU.add).then_inc(dt_chain, 1)
                dve.wait_ge(dt_chain, 4)
                nc.vector.reciprocal(tmp[3], tmp[3]).then_inc(dt_chain, 1)
                dve.wait_ge(dt_chain, 5)
                nc.vector.tensor_tensor(tmp[4], tmp[1], tmp[3], ALU.mult).then_inc(dt_chain, 1)
                dve.wait_ge(dt_chain, 6)
                nc.vector.tensor_tensor(tmp[5], tmp[4], tmp[4], ALU.mult).then_inc(dt_chain, 1)
                dve.wait_ge(dt_chain, 7)
                nc.vector.tensor_scalar(tmp[6], tmp[5], 1.0 / 13, None, ALU.mult).then_inc(dt_chain, 1)
                n = 8
                for odd in (11, 9, 7, 5, 3):
                    dve.wait_ge(dt_chain, n)
                    nc.vector.scalar_tensor_tensor(out=tmp[6], in0=tmp[6], scalar=1.0 / odd, in1=tmp[5],
                                                   op0=ALU.add, op1=ALU.mult).then_inc(dt_chain, 1)
                    n += 1
                dve.wait_ge(dt_chain, n)
                nc.vector.scalar_tensor_tensor(out=tmp[6], in0=tmp[6], scalar=1.0, in1=tmp[4],
                                               op0=ALU.add, op1=ALU.mult).then_inc(dt_chain, 1)
                dve.wait_ge(dt_chain, n + 1)
                dtf = dt.rearrange("p t n -> p (t n)")
                nc.vector.scalar_tensor_tensor(out=dtf, in0=tmp[6], scalar=2.0, in1=tmp[2],
                                               op0=ALU.mult, op1=ALU.add).then_inc(dt_chain, 1)
                dve.wait_ge(dt_chain, n + 2)
                nc.vector.tensor_tensor(la[:, 0], dt, bc(a_log.unsqueeze(1), [P, NT, HEADS]), ALU.mult).then_inc(dt_chain, 1)
                dve.wait_ge(dt_chain, n + 3)
                nc.vector.tensor_scalar(la[:, 0], la[:, 0], -1.0, -1.0e4, ALU.mult, ALU.max).then_inc(dve_setup, 1)
                dve.wait_ge(dve_setup, 1)
                nc.vector.tensor_copy(la_r[:, :, :], la[:, 0]).then_inc(dve_setup, 1)
                dve.wait_ge(dve_setup, 2)
                nc.vector.tensor_tensor(la[:, 1], la[:, 0], la_r[:, :, :].bitcast(F32), ALU.subtract).then_inc(dve_setup, 1)
                dve.wait_ge(act_ef, 1)
                nc.vector.tensor_tensor(dte, ef[:, 0], dt.rearrange("p (b c) n -> p b c n", c=2)[:, :, 0, :],
                                        ALU.mult).then_inc(dve_setup, 1)

        names = ("pe_conv act_tap dve_chain dve_conv act_xc pe_gate act_sg pe_g dve_gm pe_xt act_xt pool_xd "
                 "pool_xe pool_r pe_l act_e dve_m pe_y dve_y pe_off dve_off dve_g pool_g pe_ef act_ef act_efw act_sq pool_sq "
                 "pe_out dve_out pool_w").split()
        q = {n: sem("m_" + n) for n in names}
        (pe_conv, act_tap, dve_chain, dve_conv, act_xc, pe_gate, act_sg, pe_g, dve_gm, pe_xt, act_xt, pool_xd,
         pool_xe, pool_r, pe_l, act_e, dve_m, pe_y, dve_y, pe_off, dve_off, dve_g, pool_g, pe_eft, act_eft, act_efw, act_sq, pool_sq,
         pe_out, dve_out, pool_w) = (q[n] for n in names)
        P0, P1, W0, W1, TB, Y0, Y1, OB = bank
        STEPS = GROUPS * B
        proj = (P0, P1)
        work = (W0, W1)
        FIRST_L = 3

        def conv_tile(g, m):
            return XT * g + m if m < XT else (32 + g if m == XT else 40 + g)

        def pair_of(i, k):
            return proj[(5 * i + k) % 2]

        def tiles(ap):
            return ap.rearrange("p (m t) -> p m t", m=XT)

        with nc.Block() as block:
            @block.sync
            def _(sp):
                for g in range(1, GROUPS):
                    sp.wait_ge(pool_wlo, NW * g)
                    load_group(sp, g)
                    if g >= 2:
                        sp.wait_ge(pe_out, B * (g - 1))
                        load_out(sp, g)

            @block.tensor
            def _(pe):
                def project(i, k_):
                    g, b = i // B, i % B
                    if b == 0 and k_ == 0:
                        pe.wait_ge(pool_wlo, NW * (g + 1))
                    if k_ < 2:
                        if i:
                            pe.wait_ge(act_sg, 2 * (i - 1) + k_ + 1)
                    else:
                        pe.wait_ge(dve_conv, 3 * i + k_ - 1)
                    tok = slice(b * S, (b + 1) * S)
                    for half in range(2):
                        m = 2 * k_ + half if k_ < 3 else 2 * (k_ - 3) + half
                        w_ = (w_x if m < XT else w_b if m == XT else w_c) if k_ < 3 else w_z
                        w = w_[:, g % 2, :, :, m * P:(m + 1) * P] if m < XT else w_[:, g % 2]
                        for k in range(KD):
                            last = mm3(pair_of(i, k_)[:, half * S:(half + 1) * S], (w[:, 0, k, :], w[:, 1, k, :]),
                                       (hT_hi[:, k, tok], hT_lo[:, k, tok]), k == 0, k == KD - 1)
                    last.then_inc(pe_conv if k_ < 3 else pe_gate, 1)

                def x_rows(i, c):
                    if i and c == 0:
                        pe.wait_ge(act_e, 4 * i)
                    if i and c == 1:
                        pe.wait_ge(dve_off, i)
                    for m in range(XT):
                        last = nc.tensor.transpose(work[c][:, m * P:(m + 1) * P], xc[:, i % 2, m, c * P:(c + 1) * P],
                                                   ident)
                    last.then_inc(pe_xt, 1)

                def half_decay(i):
                    pe.wait_ge(act_xt, 2 * i + 1)
                    pe.wait_ge(act_efw, i + 1)
                    for m in range(XT):
                        last = nc.tensor.transpose(W0[:, m * P:(m + 1) * P], ef_wide[:, m * P:(m + 1) * P], ident)
                    last.then_inc(pe_eft, 1)

                def decays(u):
                    i, k = u // 4, u % 4
                    pe.wait_ge(pool_r, u + 1)
                    if k == 0:
                        pe.wait_ge(act_xt, 2 * i + 2)
                    elif k == 1:
                        pe.wait_ge(act_eft, i + 1)
                    else:
                        pe.wait_ge(act_e, u - 1)
                    for s_ in range(2):
                        last = nc.tensor.matmul(work[(FIRST_L + k) % 2][:, :], tri_gt_r[:, :],
                                                rbuf[:, s_, u % 4].rearrange("p a b -> p (a b)"),
                                                start=s_ == 0, stop=s_ == 1)
                    last.then_inc(pe_l, 1)

                def out_proj(i):
                    g = i // B
                    if i:
                        pe.wait_ge(dve_out, 2 * i)
                    pe.wait_ge(pool_w, g + 1)
                    pe.wait_ge(pool_g, i + 1)
                    for c in range(2):
                        for m in range(XT):
                            nc.tensor.matmul(OB[:, c * D:(c + 1) * D], gt[:, i % 2, m, c * P:(c + 1) * P],
                                             w_out[:, g % 2, m, :], start=m == 0, stop=m == XT - 1)

                def square_rows(i):
                    pe.wait_ge(pool_sq, 2 * (i + 1))
                    pe.wait_ge(dve_gm, min(i + 2, STEPS))
                    for c in range(2):
                        last = nc.tensor.matmul(TB[:, 3 * P + c:3 * P + c + 1], sq[:, 0, c * P:(c + 1) * P],
                                                ones[:, 0:1], start=True, stop=True)
                    last.then_inc(pe_out, 1)

                for k_ in range(5):
                    project(0, k_)
                for i in range(STEPS):
                    more = i + 1 < STEPS
                    v = xc[:, i % 2]
                    if more:
                        project(i + 1, 0)
                    pe.wait_ge(act_xc, 3 * i + 2)
                    x_rows(i, 0)
                    x_rows(i, 1)
                    if more:
                        project(i + 1, 1)
                    pe.wait_ge(act_xc, 3 * (i + 1))
                    if i >= 2:
                        pe.wait_ge(dve_out, 2 * (i - 1))
                    if i:
                        pe.wait_ge(dve_gm, i)
                    nc.tensor.matmul(TB[:, 0:S], v[:, 4, 0:P], v[:, 5, :], start=True, stop=True)
                    nc.tensor.matmul(TB[:, S:S + P], v[:, 4, P:S], v[:, 5, P:S], start=True, stop=True).then_inc(pe_g, 1)
                    half_decay(i)
                    decays(4 * i)
                    decays(4 * i + 1)
                    if more:
                        project(i + 1, 2)
                    decays(4 * i + 2)
                    decays(4 * i + 3)
                    if i:
                        out_proj(i - 1)
                    if more:
                        project(i + 1, 3)
                    pe.wait_ge(pool_xe, i + 1)
                    pe.wait_ge(act_e, 4 * i + 3)
                    pe.wait_ge(dve_gm, i + 1)
                    for m in range(XT):
                        last = nc.tensor.matmul(W1[:, m * P:(m + 1) * P], xe[:, m * P:(m + 1) * P],
                                                gm[:, i % 2, P:2 * P], start=True, stop=True)
                    last.then_inc(pe_off, 1)
                    if more:
                        project(i + 1, 4)
                    if i:
                        pe.wait_ge(dve_y, XT * i)
                    for c in range(2):
                        pe.wait_ge(dve_m, 4 * i + 2 * c + 2)
                        pe.wait_ge(pool_xd, 2 * i + c + 1)
                        for hh in range(HG):
                            m, r0 = hh // 2, HD * (hh % 2)
                            last = nc.tensor.matmul((Y0, Y1)[m // 2][r0:r0 + HD,
                                                                     m % 2 * S + c * P:m % 2 * S + (c + 1) * P],
                                                    xd[:, c, hh * HD:(hh + 1) * HD],
                                                    mbuf[:, i % 2, 2 * c + hh // 4, hh % 4, :], start=True, stop=True)
                        last.then_inc(pe_y, 1)
                    if i:
                        square_rows(i - 1)
                out_proj(STEPS - 1)
                square_rows(STEPS - 1)

            @block.scalar
            def _(act):
                def tap(i, p_):
                    act.wait_ge(pe_conv, 3 * i + p_ + 1)
                    if i:
                        act.wait_ge(act_xc, 3 * (i - 1) + p_ + 1)
                    for m in (2 * p_, 2 * p_ + 1):
                        ct = conv_tile(i // B, m)
                        nc.scalar.activation(acc[:, p_, m % 2, :], pair_of(i, p_)[:, (m % 2) * S:(m % 2 + 1) * S],
                                             ACT.Identity, bias=conv_b[:, ct:ct + 1],
                                             scale=conv_w[:, ct, TAPS - 1:TAPS]).then_inc(act_tap, 1)

                def silu(i, p_):
                    act.wait_ge(dve_conv, 3 * i + p_ + 1)
                    if i >= 2 and p_ == 0:
                        act.wait_ge(pe_xt, 2 * (i - 1))
                        act.wait_ge(dve_y, XT * (i - 1))
                    nc.scalar.activation(xc[:, i % 2, 2 * p_:2 * p_ + 2, :], acc[:, p_], ACT.Silu).then_inc(act_xc, 1)

                def gate(i, k):
                    act.wait_ge(pe_gate, 2 * i + k + 1)
                    if i >= 2:
                        act.wait_ge(pool_g, i - 1)
                    nc.scalar.activation(sg[:, i % 2, 2 * k:2 * k + 2, :].rearrange("p m t -> p (m t)"),
                                         pair_of(i, 3 + k)[:, :], ACT.Silu).then_inc(act_sg, 1)

                def exps(u):
                    k = u % 4
                    act.wait_ge(pe_l, u + 1)
                    if u >= 2:
                        act.wait_ge(dve_m, u - 1)
                    nc.scalar.activation(ebuf[:, u % 2].rearrange("p a b -> p (a b)"), work[(FIRST_L + k) % 2][:, :],
                                         ACT.Exp).then_inc(act_e, 1)

                def squares(i):
                    act.wait_ge(pool_g, i + 1)
                    if i:
                        act.wait_ge(pe_out, i)
                    nc.scalar.activation(sq, gt[:, i % 2], ACT.Square).then_inc(act_sq, 1)

                def widen(i):
                    g, b = i // B, i % B
                    if i:
                        act.wait_ge(pe_eft, i)
                    nc.scalar.copy(ef_wide.rearrange("p (h d) -> p h d", d=HD),
                                   bc(ef[:, 1, b, g * HG:(g + 1) * HG].unsqueeze(2),
                                      [P, HG, HD])).then_inc(act_efw, 1)

                widen(0)
                for p_ in range(3):
                    tap(0, p_)
                    silu(0, p_)
                gate(0, 0)
                gate(0, 1)
                for i in range(STEPS):
                    more = i + 1 < STEPS
                    if more:
                        tap(i + 1, 0)
                    for c in range(2):
                        act.wait_ge(pe_xt, 2 * i + c + 1)
                        if i:
                            act.wait_ge(pool_xd, 2 * i)
                            act.wait_ge(pool_xe, i)
                        nc.scalar.copy(xtok[:, c], work[c][:, :]).then_inc(act_xt, 1)
                    act.wait_ge(pe_eft, i + 1)
                    if i:
                        act.wait_ge(dve_off, i)
                    nc.scalar.copy(ef_t, tiles(W0[:, :])).then_inc(act_eft, 1)
                    exps(4 * i)
                    exps(4 * i + 1)
                    if more:
                        tap(i + 1, 1)
                        tap(i + 1, 2)
                    if i:
                        squares(i - 1)
                    exps(4 * i + 2)
                    exps(4 * i + 3)
                    if more:
                        silu(i + 1, 0)
                        silu(i + 1, 1)
                        gate(i + 1, 0)
                        silu(i + 1, 2)
                        gate(i + 1, 1)
                        widen(i + 1)
                    if i % B == 0 and i // B + 1 < GROUPS:
                        split_hi(act, i // B + 1)
                squares(STEPS - 1)

            @block.gpsimd
            def _(pool):
                def decay_rows(u):
                    i, c, hf = u // 4, u // 2 % 2, u % 2
                    t, h0 = 2 * (i % B) + c, i // B * HG + 4 * hf
                    if u >= 4:
                        pool.wait_ge(pe_l, u - 3)
                    for s_, a in ((0, la_r[:, t, h0:h0 + 4].bitcast(F32)), (1, la[:, 1, t, h0:h0 + 4])):
                        last = nc.gpsimd.tensor_tensor(rbuf[:, s_, u % 4], bc(tri_le.unsqueeze(1), [P, 4, P]),
                                                       bc(a.unsqueeze(2), [P, 4, P]), ALU.mult)
                    last.then_inc(pool_r, 1)

                def scaled(i):
                    g, b = i // B, i % B
                    hs = slice(g * HG, (g + 1) * HG)

                    def times(dst, c, a):
                        return nc.gpsimd.tensor_tensor(dst.rearrange("p (h d) -> p h d", d=HD),
                                                       xtok[:, c].rearrange("p (h d) -> p h d", d=HD),
                                                       bc(a.unsqueeze(2), [P, HG, HD]), ALU.mult)
                    for c in range(2):
                        pool.wait_ge(act_xt, 2 * i + c + 1)
                        if i:
                            pool.wait_ge(pe_y, 2 * (i - 1) + c + 1)
                        times(xd[:, c], c, dt[:, 2 * b + c, hs]).then_inc(pool_xd, 1)
                        if c == 0:
                            if i:
                                pool.wait_ge(pe_off, i)
                            times(xe, 0, dte[:, b, hs]).then_inc(pool_xe, 1)

                def gated(i):
                    pool.wait_ge(dve_g, i + 1)
                    pool.wait_ge(act_sg, 2 * i + 2)
                    nc.gpsimd.tensor_tensor(gt[:, i % 2], gt[:, i % 2], sg[:, i % 2], ALU.mult).then_inc(pool_g, 1)

                def square_sum(i):
                    pool.wait_ge(act_sq, i + 1)
                    nc.gpsimd.tensor_tensor(sq[:, 0:2], sq[:, 0:2], sq[:, 2:4], ALU.add).then_inc(pool_sq, 1)
                    pool.wait_ge(pool_sq, 2 * i + 1)
                    nc.gpsimd.tensor_tensor(sq[:, 0], sq[:, 0], sq[:, 1], ALU.add).then_inc(pool_sq, 1)

                for u in range(4):
                    decay_rows(u)
                for i in range(STEPS):
                    g = i // B
                    if i:
                        gated(i - 1)
                    scaled(i)
                    if i + 1 < STEPS:
                        decay_rows(4 * i + 4)
                        decay_rows(4 * i + 5)
                    if i:
                        square_sum(i - 1)
                    if i % B == 0:
                        pool.wait_ge(ld_o[g % 2], 16 * (g // 2 + 1))
                        nc.gpsimd.tensor_tensor(w_out[:, g % 2], w_out[:, g % 2],
                                                bc(norm_w[:, XT * g:XT * (g + 1)].unsqueeze(2), [P, XT, D]),
                                                ALU.mult).then_inc(pool_w, 1)
                    if i % B == 1 and g + 1 < GROUPS:
                        split_lo(pool, g + 1)
                    if i + 1 < STEPS:
                        decay_rows(4 * i + 6)
                        decay_rows(4 * i + 7)
                gated(STEPS - 1)
                square_sum(STEPS - 1)

            @block.vector
            def _(dve):
                def conv_rest(i, p_):
                    n0 = 6 * (3 * i + p_)
                    dve.wait_ge(act_tap, 6 * i + 2 * p_ + 2)
                    for j in range(6):
                        m, sh = 2 * p_ + j % 2, j // 2 + 1
                        ct = conv_tile(i // B, m)
                        if j >= 2:
                            dve.wait_ge(dve_chain, n0 + j - 1)
                        nc.vector.scalar_tensor_tensor(
                            out=acc[:, p_, m % 2, sh:], in0=pair_of(i, p_)[:, (m % 2) * S:(m % 2 + 1) * S - sh],
                            scalar=conv_w[:, ct, TAPS - 1 - sh:TAPS - sh], in1=acc[:, p_, m % 2, sh:],
                            op0=ALU.mult, op1=ALU.add).then_inc(dve_chain, 1)
                    dve.wait_ge(dve_chain, n0 + 6)
                    nc.vector.engine_nop().then_inc(dve_conv, 1)

                def masked(u):
                    i, c = u // 4, u // 2 % 2
                    dve.wait_ge(act_e, u + 1)
                    if i >= 2:
                        dve.wait_ge(pe_y, 2 * (i - 2) + c + 1)
                    nc.vector.tensor_tensor(mbuf[:, i % 2, u % 4], ebuf[:, u % 2],
                                            bc(gm[:, i % 2, 2 * c * P:(2 * c + 1) * P].unsqueeze(1), [P, 4, P]),
                                            ALU.mult).then_inc(dve_m, 1)

                def scan_out(i):
                    dve.wait_ge(pe_y, 2 * i + 2)
                    if i >= 2:
                        dve.wait_ge(pe_out, i - 1)
                    for m in range(XT):
                        ct = XT * (i // B) + m
                        nc.vector.scalar_tensor_tensor(
                            out=gt[:, i % 2, m, :], in0=xc[:, i % 2, m, :], scalar=d_col[:, ct:ct + 1],
                            in1=(Y0, Y1)[m // 2][:, (m % 2) * S:(m % 2 + 1) * S], op0=ALU.mult,
                            op1=ALU.add).then_inc(dve_y, 1)
                    dve.wait_ge(dve_y, XT * (i + 1))
                    dve.wait_ge(dve_off, i + 1)
                    nc.vector.tensor_tensor(gt[:, i % 2, :, P:S], gt[:, i % 2, :, P:S], off, ALU.add).then_inc(dve_g, 1)

                def out_sum(i):
                    b = i % B
                    dve.wait_ge(pe_out, i + 1)
                    nc.vector.tensor_copy(ss[:, 2 * b:2 * b + 2, i // B], TB[:, 3 * P:3 * P + 2]).then_inc(dve_out, 1)
                    if i >= B:
                        dve.wait_ge(dve_out, 2 * (i - B) + 2)
                    ya = y_acc[:, 2 * b:2 * b + 2, :]
                    nc.vector.tensor_tensor(ya, OB[:, :].rearrange("p (c d) -> p c d", c=2), ya,
                                            ALU.add).then_inc(dve_out, 1)

                for p_ in range(3):
                    conv_rest(0, p_)
                for i in range(STEPS):
                    more = i + 1 < STEPS
                    if i:
                        scan_out(i - 1)
                    if more:
                        conv_rest(i + 1, 0)
                    dve.wait_ge(pe_g, i + 1)
                    if i >= 2:
                        dve.wait_ge(pe_off, i - 1)
                    nc.vector.tensor_tensor(gm[:, i % 2], TB[:, 0:3 * P], causal3, ALU.mult).then_inc(dve_gm, 1)
                    dve.wait_ge(dve_gm, i + 1)
                    masked(4 * i)
                    masked(4 * i + 1)
                    if more:
                        conv_rest(i + 1, 1)
                        conv_rest(i + 1, 2)
                    masked(4 * i + 2)
                    masked(4 * i + 3)
                    dve.wait_ge(pe_off, i + 1)
                    dve.wait_ge(act_eft, i + 1)
                    if i:
                        dve.wait_ge(dve_g, i)
                    nc.vector.tensor_tensor(off, tiles(W1[:, :]), ef_t, ALU.mult).then_inc(dve_off, 1)
                    if i:
                        out_sum(i - 1)
                scan_out(STEPS - 1)
                out_sum(STEPS - 1)

        take = carver()
        wg = take(2, 4, KD, I0)
        wu = take(2, 4, KD, I0)
        wd = take(2, 4, 2, D, parts=IT)
        wsg = take(KD, IS)
        wsu = take(KD, IS)
        wsd = take(NIS, D, parts=IT)
        gate_raw = take(D, parts=E0)
        back_t = take(2, 4, P)
        back = take(4, NT * P)
        sh_a = back[0:IT].rearrange("p e (a n) -> p (e a) n", a=2)[:, 0:NIS, :]
        xe_t = take(KD, 4 * P)
        silu_g = take(2, 2 * P, parts=IT)
        act_t = take(2, 2, P, parts=IT)
        oe = take(4, D)
        sh_s = take(2, 512, parts=IT)
        small = [take(NT, E0) for _ in range(9)]
        r_mx, r_sum, r_rec, rms, rms_std = (take(NT) for _ in range(5))
        m8 = take(NT, 8)
        i8 = take(NT, 8).bitcast(U32)
        i8f = take(NT, 8)
        takeh = carver(halves, HALVES)
        slot = takeh(NT, 4, P)
        h_r = takeh(2, NT, D)
        wsg_r = takeh(2, KD, IS)
        wsu_r = takeh(2, KD, IS)
        gate_t = takeh(2, KD, E0)
        ld_wu = [sem("ld_wu_even"), sem("ld_wu_odd")]
        act_sh, pool_sh, act_h, pool_h, dve_gw = (sem(n) for n in (
            "act_sh", "pool_sh", "act_h", "pool_h", "dve_gw"))
        lg_t = back_t.rearrange("p r e c -> p (r e c)")[0:E0, :]
        cum = take(NT - 1, E0)
        pool_res = sem("pool_res")

        names = ("ld_gate ld_sh dve_ms act_ms dve_res pe_gw act_gw pe_lg dve_rt act_ex dve_sel pe_pos "
                 "dve_pos pe_lgt act_lgt dve_cum pe_sg act_sg dve_sa pe_sd act_sy dve_p dve_q pe_disp act_xe pe_q act_qt pe_up act_s dve_a "
                 "pe_dn act_oe pe_comb dve_y").split()
        f = {n: sem("f_" + n) for n in names}
        (ld_gate, ld_sh, dve_ms, act_ms, dve_res, pe_gw, act_gw, pe_lg, dve_rt, act_ex, dve_sel, pe_pos,
         dve_pos, pe_lgt, act_lgt, dve_cum, pe_sg, act_sg, dve_sa, pe_sd, act_sy, dve_p, dve_q, pe_disp, act_xe, pe_q, act_qt, pe_up, act_s,
         dve_a, pe_dn, act_oe, pe_comb, dve_y) = (f[n] for n in names)
        NQ = E0 // 4

        def topk_select(dve, scores, k, chain, n0, eq, sel, m8, i8, i8f):
            for t in range(NT):
                nc.vector.max(m8[:, t, :], scores[:, t, :]).then_inc(chain, 1)
            for t in range(NT):
                dve.wait_ge(chain, n0 + t + 1)
                nc.vector.max_index(i8[:, t, :], m8[:, t, :], scores[:, t, :]).then_inc(chain, 1)
            dve.wait_ge(chain, n0 + 2 * NT)
            nc.vector.tensor_copy(i8f, i8).then_inc(chain, 1)
            n = n0 + 2 * NT + 1
            for r in range(k):
                dve.wait_ge(chain, n)
                nc.vector.tensor_tensor(eq if r else sel, bc(iota[:, 0:E0].unsqueeze(1), [P, NT, E0]),
                                        bc(i8f[:, :, r:r + 1], [P, NT, E0]), ALU.is_equal).then_inc(chain, 1)
                n += 1
                if r:
                    dve.wait_ge(chain, n)
                    nc.vector.tensor_tensor(sel, sel, eq, ALU.add).then_inc(chain, 1)
                    n += 1
            return n

        with nc.Block() as block:
            @block.sync
            def _(sp):
                sp.dma_start(gate_raw, A["L0_ffn_gate_w"]).then_inc(ld_gate, 16)
                load_shift_scale(sp, 1)
                sp.dma_start(wsg, A["L0_ffn_ws_gate"].rearrange("(k p) i -> p k i", p=P)).then_inc(ld_sh, 16)
                sp.dma_start(wsu, A["L0_ffn_ws_up"].rearrange("(k p) i -> p k i", p=P)).then_inc(ld_sh, 16)
                sp.dma_start(wsd, A["L0_ffn_ws_down"].rearrange("(j p) n -> p j n", p=IT)).then_inc(ld_sh, 16)
                for eq in range(NQ):
                    if eq == 2:
                        sp.wait_ge(dve_res, NT)
                        load_gate(sp, 1)
                        sp.wait_ge(norm_h, 2 * NT)
                        load_shift_scale(sp, 2)
                    if eq >= 2:
                        sp.wait_ge(pe_dn, 4 * (eq - 1))
                    e4, r_ = slice(4 * eq, 4 * eq + 4), eq % 2
                    sp.dma_start(wg[:, r_], A["L0_ffn_w_gate"][e4].rearrange("e (k p) i -> p e k i", p=P)).then_inc(ld_wu[r_], 16)
                    sp.dma_start(wu[:, r_], A["L0_ffn_w_up"][e4].rearrange("e (k p) i -> p e k i", p=P)).then_inc(ld_wu[r_], 16)
                    sp.dma_start(wd[:, r_], A["L0_ffn_w_down"][e4].rearrange("e (j p) n -> p e j n", p=IT)).then_inc(ld_wu[r_], 16)

            @block.tensor
            def _(pe):
                pe.wait_ge(ld_gate, 16)
                for k in range(KD):
                    last = nc.tensor.transpose(bank[4][:, k * E0:(k + 1) * E0], gate_raw[:, k * P:(k + 1) * P],
                                               ident[0:E0, 0:E0])
                last.then_inc(pe_gw, 1)
                norm_pe(pe, 1, bank[6:8])
                pe.wait_ge(pool_sh, 2)

                def shared_up(u):
                    th, j = u // NIS, u % NIS
                    pe.wait_ge(norm_hT, NT // 2 + (NT // 4) * (th + 1))
                    if u >= 2:
                        pe.wait_ge(dve_sa, u - 1)
                    tok, ij = slice(th * 512, (th + 1) * 512), slice(j * IT, (j + 1) * IT)
                    for w, bk in ((wsg_r, bank[u % 2]), (wsu_r, bank[2 + u % 2])):
                        for k in range(KD):
                            last = mm3(bk[0:IT, :], (w[:, 0, k, ij], w[:, 1, k, ij]),
                                       (hT_hi[:, k, tok], hT_lo[:, k, tok]), k == 0, k == KD - 1)
                    last.then_inc(pe_sg, 1)

                def shared_down(u):
                    pe.wait_ge(dve_sa, NIS * (u // 4 + 1))
                    if u >= 2:
                        pe.wait_ge(act_sy, u - 1)
                    for j in range(NIS):
                        last = nc.tensor.matmul(bank[6 + u % 2][:, 0:D], sh_a[:, j, u % 4 * P:(u % 4 + 1) * P], wsd[:, j, :],
                                                start=j == 0, stop=j == NIS - 1)
                    last.then_inc(pe_sd, 1)

                for u in range(NIS):
                    shared_up(u)
                pe.wait_ge(dve_gw, 1)
                pe.wait_ge(norm_hT, 2 * NT // 2)
                for th in range(2):
                    tok = slice(th * 512, (th + 1) * 512)
                    for k in range(KD):
                        last = mm3(bank[4 + th][0:E0, :], (gate_t[:, 0, k, :], gate_t[:, 1, k, :]),
                                   (hT_hi[:, k, tok], hT_lo[:, k, tok]), k == 0, k == KD - 1)
                    last.then_inc(pe_lgt, 1)
                shared_down(0)
                shared_down(1)
                pe.wait_ge(act_lgt, 2)
                for t in range(NT):
                    last = nc.tensor.transpose(bank[5][:, t * E0:(t + 1) * E0], lg_t[:, t * P:(t + 1) * P],
                                               ident[0:E0, 0:E0])
                last.then_inc(pe_lg, 1)
                shared_down(2)
                shared_down(3)
                shared_up(NIS)
                shared_up(NIS + 1)
                pe.wait_ge(dve_sel, 2)
                sel = small[4]
                pos = bank[5][:, P:2 * P]
                nc.tensor.matmul(pos, tri_lt, sel.rearrange("p t e -> p (t e)"), start=True, stop=False)
                nc.tensor.matmul(pos[:, E0:], ones, cum.rearrange("p t e -> p (t e)"), start=False, stop=True).then_inc(pe_pos, 1)
                for u in range(NIS + 2, 2 * NIS):
                    shared_up(u)
                for u in range(4, 8):
                    shared_down(u)

                def dispatch(eq):
                    for k in range(KD):
                        if eq:
                            pe.wait_ge(act_xe, 2 * eq)
                        for t in range(NT):
                            pe.wait_ge(dve_p, NT * eq + t + 1)
                            for s_ in range(2):
                                last = nc.tensor.matmul(bank[k][:, :], h_r[:, s_, t, k * P:(k + 1) * P],
                                                        slot[:, t].rearrange("p e c -> p (e c)"),
                                                        start=t + s_ == 0, stop=t == NT - 1 and s_ == 1)
                        last.then_inc(pe_disp, 1)

                def turn_back(u):
                    pe.wait_ge(dve_q, u + 1)
                    if u >= 2:
                        pe.wait_ge(act_qt, u - 1)
                    for e in range(4):
                        last = nc.tensor.transpose(bank[2 + u % 2][:, e * P:(e + 1) * P], back_t[:, u % 2, e, :], ident)
                    last.then_inc(pe_q, 1)

                def up(n):
                    eq, e = n // 4, n % 4
                    pe.wait_ge(act_xe, 2 * (eq + 1))
                    pe.wait_ge(ld_wu[eq % 2], 48 * (eq // 2 + 1))
                    if n >= 2:
                        pe.wait_ge(dve_a, n - 1)
                    if n == 1:
                        pe.wait_ge(dve_pos, 1)
                    for w, o in ((wg, 0), (wu, 2)):
                        for j in range(2):
                            for k in range(KD):
                                last = nc.tensor.matmul(bank[4 + n % 2][0:IT, (o + j) * P:(o + j + 1) * P],
                                                        w[:, eq % 2, e, k, j * IT:(j + 1) * IT],
                                                        xe_t[:, k, e * P:(e + 1) * P], start=k == 0, stop=k == KD - 1)
                    last.then_inc(pe_up, 1)

                def down(n):
                    eq, e = n // 4, n % 4
                    pe.wait_ge(dve_a, n + 1)
                    if e >= 2:
                        pe.wait_ge(act_oe, n - 1)
                    elif eq:
                        pe.wait_ge(dve_y, NT * eq - 1 + e)
                    for j in range(2):
                        last = nc.tensor.matmul(bank[6 + n % 2][:, 0:D], act_t[:, n % 2, j, :], wd[:, eq % 2, e, j, :],
                                                start=j == 0, stop=j == 1)
                    last.then_inc(pe_dn, 1)

                def combine(u):
                    eq, t = u // NT, u % NT
                    pe.wait_ge(act_oe, 4 * (eq + 1))
                    pe.wait_ge(act_qt, u + 1)
                    if t >= 2:
                        pe.wait_ge(dve_y, u - 1)
                    for e in range(4):
                        last = nc.tensor.matmul(bank[6 + t % 2][:, 0:D], back[:, e, t * P:(t + 1) * P], oe[:, e, :],
                                                start=e == 0, stop=e == 3)
                    last.then_inc(pe_comb, 1)

                pe.wait_ge(dve_sa, 2 * NIS)
                pe.wait_ge(act_sy, 2 * 4)
                pe.wait_ge(pool_h, 1)
                dispatch(0)
                for u in range(NT):
                    turn_back(u)
                up(0)
                for eq in range(NQ):
                    for n in range(4 * eq, 4 * eq + 4):
                        if n % 4 < 3:
                            up(n + 1)
                        down(n)
                    if eq + 1 < NQ:
                        dispatch(eq + 1)
                    for u in range(NT * eq, NT * (eq + 1)):
                        combine(u)
                        if eq + 1 < NQ:
                            turn_back(u + NT)
                    if eq + 1 < NQ:
                        up(4 * eq + 4)

            @block.scalar
            def _(act):
                act.wait_ge(dve_ms, 2)
                nc.scalar.activation(rms_std, rms_std, ACT.Sqrt).then_inc(act_ms, 1)
                act.wait_ge(ld_sh, 48)
                nc.scalar.copy(wsg_r[:, 0], wsg).then_inc(act_sh, 1)
                nc.scalar.copy(wsu_r[:, 0], wsu).then_inc(act_sh, 1)
                act.wait_ge(pe_gw, 1)
                nc.scalar.copy(gate_t[:, 0].rearrange("p k e -> p (k e)"), bank[4][:, 0:KD * E0]).then_inc(act_gw, 1)
                norm_act(act, 1)
                norm_act_copy(act, 1, bank[6:8])
                def shared_silu(u):
                    act.wait_ge(pe_sg, u + 1)
                    if u >= 2:
                        act.wait_ge(dve_sa, u - 1)
                    nc.scalar.activation(sh_s[:, u % 2], bank[u % 2][0:IT, :], ACT.Silu).then_inc(act_sg, 1)

                def shared_y(u):
                    act.wait_ge(pe_sd, u + 1)
                    nc.scalar.copy(y_acc[:, u, :], bank[6 + u % 2][:, 0:D]).then_inc(act_sy, 1)

                for u in range(NIS):
                    shared_silu(u)
                for th in range(2):
                    act.wait_ge(pe_lgt, th + 1)
                    nc.scalar.copy(lg_t[:, th * 512:(th + 1) * 512], bank[4 + th][0:E0, :]).then_inc(act_lgt, 1)
                for u in range(4):
                    shared_y(u)
                act.wait_ge(dve_rt, 2)
                nc.scalar.activation(small[1], small[0], ACT.Exp).then_inc(act_ex, 1)
                for u in range(NIS, 2 * NIS):
                    shared_silu(u)
                nc.scalar.copy(h_r[:, 0], h[:, :, :]).then_inc(act_h, 1)
                for u in range(4, 8):
                    shared_y(u)

                def slots_in(eq):
                    for k in range(KD):
                        act.wait_ge(pe_disp, 2 * eq + k + 1)
                        if eq:
                            act.wait_ge(pe_up, 4 * eq)
                        nc.scalar.copy(xe_t[:, k], bank[k][:, :]).then_inc(act_xe, 1)

                def back_copy(u):
                    t = u % NT
                    act.wait_ge(pe_q, u + 1)
                    if u >= NT:
                        act.wait_ge(pe_comb, u - NT + 1)
                    else:
                        act.wait_ge(pe_sd, 2 * 4)
                    nc.scalar.copy(back[:, :, t * P:(t + 1) * P],
                                   bank[2 + t % 2][:, :].rearrange("p (e c) -> p e c", e=4)).then_inc(act_qt, 1)

                def silu(n):
                    act.wait_ge(pe_up, n + 1)
                    if n >= 2:
                        act.wait_ge(dve_a, n - 1)
                    nc.scalar.activation(silu_g[:, n % 2], bank[4 + n % 2][0:IT, 0:2 * P], ACT.Silu).then_inc(act_s, 1)

                slots_in(0)
                for u in range(NT):
                    back_copy(u)
                silu(0)
                for eq in range(NQ):
                    for e in range(4):
                        if e < 3:
                            silu(4 * eq + e + 1)
                        act.wait_ge(pe_dn, 4 * eq + e + 1)
                        if eq:
                            act.wait_ge(pe_comb, NT * eq)
                        nc.scalar.copy(oe[:, e, :], bank[6 + e % 2][:, 0:D]).then_inc(act_oe, 1)
                    if eq + 1 < NQ:
                        slots_in(eq + 1)
                        for u in range(NT * (eq + 1), NT * (eq + 2)):
                            back_copy(u)
                        silu(4 * eq + 4)

            @block.gpsimd
            def _(pool):
                for t in range(NT):
                    pool.wait_ge(dve_res, t + 1)
                    nc.gpsimd.tensor_tensor(x[:, t, :], x[:, t, :], y_acc[:, t, :], ALU.add).then_inc(pool_res, 1)
                for i_, (w, wr) in enumerate(((wsg, wsg_r), (wsu, wsu_r))):
                    pool.wait_ge(act_sh, i_ + 1)
                    nc.gpsimd.tensor_tensor(wr[:, 1], w, wr[:, 0].bitcast(F32), ALU.subtract).then_inc(pool_sh, 1)
                norm_pool(pool, 1)
                pool.wait_ge(act_h, 1)
                nc.gpsimd.tensor_tensor(h_r[:, 1], h[:, :, :], h_r[:, 0].bitcast(F32), ALU.subtract).then_inc(pool_h, 1)

            @block.vector
            def _(dve):
                nc.vector.tensor_reduce(rms_std, ss[:, :, :], AX, ALU.add).then_inc(dve_ms, 1)
                dve.wait_ge(dve_ms, 1)
                nc.vector.tensor_scalar(rms_std, rms_std, 1.0 / INTER, EPS, ALU.mult, ALU.add).then_inc(dve_ms, 1)
                dve.wait_ge(act_ms, 1)
                nc.vector.reciprocal(rms, rms_std).then_inc(dve_ms, 1)
                dve.wait_ge(dve_ms, 3)
                for t in range(NT):
                    nc.vector.scalar_tensor_tensor(out=y_acc[:, t, :], in0=y_acc[:, t, :], scalar=rms[:, t:t + 1],
                                                   in1=mod[:, t // 2, 2 * D:3 * D], op0=ALU.mult,
                                                   op1=ALU.mult).then_inc(dve_res, 1)
                for t in range(NT):
                    dve.wait_ge(pool_res, t + 1)
                    norm_stats(1, t)
                norm_dve(dve, 1)
                dve.wait_ge(act_gw, 1)
                nc.vector.tensor_tensor(gate_t[:, 1].rearrange("p k e -> p (k e)"), bank[4][:, 0:KD * E0],
                                        gate_t[:, 0].rearrange("p k e -> p (k e)").bitcast(F32),
                                        ALU.subtract).then_inc(dve_gw, 1)
                norm_dve_lo(dve, 1, bank[6:8])

                def shared(u):
                    dve.wait_ge(act_sg, u + 1)
                    if u >= NIS:
                        dve.wait_ge(pe_sd, 4)
                    nc.vector.tensor_tensor(sh_a[:, u % NIS, :], bank[2 + u % 2][0:IT, :], sh_s[:, u % 2],
                                            ALU.mult).then_inc(dve_sa, 1)

                for u in range(NIS):
                    shared(u)
                lg = bank[5][:, 0:P].rearrange("p (t e) -> p t e", t=NT)
                pos = bank[5][:, P:2 * P].rearrange("p (t e) -> p t e", t=NT)
                shift, ex, prob, eqv, sel, wt, posd, qpos, qtmp = small
                dve.wait_ge(pe_lg, 1)
                nc.vector.tensor_reduce(r_mx, lg, AX, ALU.max).then_inc(dve_rt, 1)
                dve.wait_ge(dve_rt, 1)
                nc.vector.tensor_tensor(shift, lg, bc(r_mx.unsqueeze(2), [P, NT, E0]), ALU.subtract).then_inc(dve_rt, 1)
                dve.wait_ge(act_ex, 1)
                nc.vector.tensor_reduce(r_sum, ex, AX, ALU.add).then_inc(dve_rt, 1)
                dve.wait_ge(dve_rt, 3)
                nc.vector.reciprocal(r_rec, r_sum).then_inc(dve_rt, 1)
                dve.wait_ge(dve_rt, 4)
                nc.vector.tensor_tensor(prob, ex, bc(r_rec.unsqueeze(2), [P, NT, E0]), ALU.mult).then_inc(dve_rt, 1)
                dve.wait_ge(dve_rt, 5)
                n = topk_select(dve, prob, 2, dve_rt, 5, eqv, sel, m8, i8, i8f)
                dve.wait_ge(dve_rt, n)
                nc.vector.tensor_tensor(wt, prob, sel, ALU.mult).then_inc(dve_sel, 1)

                nc.vector.tensor_copy(cum[:, 0, :], sel[:, 0, :]).then_inc(dve_cum, 1)
                for t in range(1, NT - 1):
                    dve.wait_ge(dve_cum, t)
                    nc.vector.tensor_tensor(cum[:, t, :], cum[:, t - 1, :], sel[:, t, :],
                                            ALU.add).then_inc(dve_cum if t < NT - 2 else dve_sel, 1)
                for u in range(NIS, 2 * NIS):
                    shared(u)
                dve.wait_ge(pe_pos, 1)
                nc.vector.scalar_tensor_tensor(out=posd, in0=pos, scalar=1.0, in1=sel, op0=ALU.add,
                                               op1=ALU.mult).then_inc(dve_rt, 1)
                nc.vector.tensor_scalar(qtmp, pos, CAP - 1.0, 1.0, ALU.min, ALU.add).then_inc(dve_rt, 1)
                dve.wait_ge(dve_rt, n + 2)
                nc.vector.tensor_scalar(posd, posd, -1.0, None, ALU.add).then_inc(dve_rt, 1)
                nc.vector.tensor_tensor(qpos, qtmp, sel, ALU.mult).then_inc(dve_rt, 1)
                dve.wait_ge(dve_rt, n + 4)
                nc.vector.tensor_scalar(qpos, qpos, -1.0, None, ALU.add).then_inc(dve_pos, 1)
                dve.wait_ge(dve_pos, 1)

                def slots(eq, t):
                    if eq:
                        dve.wait_ge(pe_disp, 2 * eq)
                    for e in range(4):
                        last = nc.vector.tensor_scalar(slot[:, t, e, :], iota, posd[:, t, 4 * eq + e:4 * eq + e + 1],
                                                       None, ALU.is_equal)
                    last.then_inc(dve_p, 1)

                def slots_back(u):
                    eq, t = u // NT, u % NT
                    if u >= 2:
                        dve.wait_ge(pe_q, u - 1)
                    for e in range(4):
                        last = nc.vector.tensor_scalar(back_t[:, t % 2, e, :], iota,
                                                       qpos[:, t, 4 * eq + e:4 * eq + e + 1],
                                                       wt[:, t, 4 * eq + e:4 * eq + e + 1], ALU.is_equal, ALU.mult)
                    last.then_inc(dve_q, 1)

                for t in range(NT):
                    slots(0, t)
                for t in range(NT):
                    slots_back(t)
                dve.wait_ge(act_sy, 2 * 4)
                for eq in range(NQ):
                    more = eq + 1 < NQ
                    for e in range(4):
                        n = 4 * eq + e
                        dve.wait_ge(act_s, n + 1)
                        if n >= 2:
                            dve.wait_ge(pe_dn, n - 1)
                        nc.vector.tensor_tensor(act_t[:, n % 2].rearrange("p j c -> p (j c)"),
                                                bank[4 + n % 2][0:IT, 2 * P:4 * P], silu_g[:, n % 2],
                                                ALU.mult).then_inc(dve_a, 1)
                        if more:
                            slots(eq + 1, 2 * e)
                            slots(eq + 1, 2 * e + 1)
                    if more:
                        slots_back(NT * (eq + 1))
                    for t in range(NT):
                        u = NT * eq + t
                        if more and t + 1 < NT:
                            slots_back(u + NT + 1)
                        dve.wait_ge(pe_comb, u + 1)
                        if eq:
                            dve.wait_ge(dve_y, u - NT + 1)
                        nc.vector.tensor_tensor(y_acc[:, t, :], bank[6 + t % 2][:, 0:D], y_acc[:, t, :],
                                                ALU.add).then_inc(dve_y, 1)

        take = carver()
        w_raw = take(4, 2, D)
        prob_sb = take(4, 512)
        takeh = carver(halves, HALVES)
        w_t = takeh(3, 2, KD, D)
        w_o = takeh(2, 4, D)
        att_t = takeh(2, 4, P)
        wo_pad = take(2, AH, 32)
        qkp = take(2, 2, AH, 32)
        r_a = take(2 * AH, DH)
        r_b = take(2 * AH, DH)
        q_t = take(4, NT * P)
        k_t = take(4, NT * P)
        v_sb = take(NT, AH, 32)
        prob_t = w_raw.rearrange("p a b c -> p a (b c)")
        mx = take(4, 4)
        nmx = take(4, 4)
        rs = take(NT, AH)
        rrs = take(NT, AH)
        otmp = take(D)
        W1 = 3 * D
        late = carver()
        late(ARENA - (E1 + 1) * W1)
        w1_raw = late(E1 + 1, 3, D)
        EARLY = 14
        assert take(1).offset % ARENA <= ARENA - (E1 + 1 - EARLY) * W1

        def load_experts(eng, e0, e1):
            e = slice(e0, e1)
            eng.dma_start(w1_raw[:, e, 0, :], A["L1_ffn_expert_gate_w"][e].rearrange("e f h -> f e h")).then_inc(ld_w1, 16)
            eng.dma_start(w1_raw[:, e, 1, :], A["L1_ffn_expert_up_w"][e].rearrange("e f h -> f e h")).then_inc(ld_w1, 16)
            for e_ in range(e0, e1):
                eng.dma_start(w1_raw[:, e_, 2, :].rearrange("p (o f) -> p o f", o=2),
                              A["L1_ffn_expert_down_w"][e_].rearrange("(o p) f -> p o f", p=P)).then_inc(ld_w1, 16)

        names = ("ld_w dve_res pe_wt act_wt pe_qkv "
                 "act_v dve_ra dve_qk pe_qk act_qk pe_s dve_mask dve_mx dve_nm act_p pe_pt ev_pt_a "
                 "ev_pt_d pe_pv dve_rr pool_n act_at pe_wo dve_o dve_x dve_wt dve_at").split()
        g_ = {n: sem("a_" + n) for n in names}
        (ld_wq, dve_res1, pe_wt, act_wt, pe_qkv, act_v, dve_ra, dve_qk, pe_qk, act_qk, pe_s, dve_mask, dve_mx, dve_nm, act_p, pe_pt,
         act_pt, dve_pt, pe_pv, dve_rr, pool_n, act_at, pe_wo, dve_o, dve_x, dve_wt, dve_at) = (g_[n] for n in names)
        ld_w1 = sem("ld_w1")
        wo_bank = (bank[7], bank[3])

        def tile_done(u):
            return 2 * units[u][0] + units[u][1] if u >= 0 and units[u][2][-1] == 3 else None

        units = [(b, qt, js) for b in range(B) for qt, js in ((0, (0, 1, 2, 3)), (1, (0, 1)), (1, (2, 3)))]

        with nc.Block() as block:
            @block.sync
            def _(sp):
                for i_, nm in enumerate(("L1_attn_Wq", "L1_attn_Wk", "L1_attn_Wv", "L1_attn_Wo")):
                    sp.dma_start(w_raw[:, i_], A[nm].rearrange("(o p) d -> p o d", p=P)).then_inc(ld_wq, 16)
                sp.dma_start(w1_raw[:, E1, 0, :], A["L1_ffn_shared_gate_w"]).then_inc(ld_w1, 16)
                sp.dma_start(w1_raw[:, E1, 1, :], A["L1_ffn_shared_up_w"]).then_inc(ld_w1, 16)
                sp.dma_start(w1_raw[:, E1, 2, :].rearrange("p (o f) -> p o f", o=2),
                             A["L1_ffn_shared_down_w"].rearrange("(o p) f -> p o f", p=P)).then_inc(ld_w1, 16)
                load_experts(sp, EARLY, E1)
                sp.wait_ge(pool_res, 2 * NT)
                load_gate(sp, 2)
                sp.wait_ge(norm_h, 3 * NT)
                load_shift_scale(sp, 3)

            @block.tensor
            def _(pe):
                pe.wait_ge(ld_wq, 64)
                for i_ in range(3):
                    for k in range(KD):
                        for o in range(2):
                            last = nc.tensor.transpose(bank[4 + i_][:, (2 * k + o) * P:(2 * k + o + 1) * P],
                                                       w_raw[:, i_, o, k * P:(k + 1) * P], ident)
                    last.then_inc(pe_wt, 1)
                pe.wait_ge(pool_res, 2 * NT + 2)
                for jj in range(2):
                    for j in range(2):
                        for o in range(2):
                            last = nc.tensor.transpose(wo_bank[jj][:, (2 * j + o) * P:(2 * j + o + 1) * P],
                                                       wo_pad[:, o, 4 * (2 * jj + j):4 * (2 * jj + j + 1), :]
                                                       .rearrange("p a b -> p (a b)"), ident)
                    last.then_inc(pe_wt, 1)
                norm_pe(pe, 2, bank[0:2])
                pe.wait_ge(dve_wt, 3)
                pe.wait_ge(norm_hT, 3 * NT // 2)

                def qk_transposes(t):
                    pe.wait_ge(dve_qk, t + 1)
                    for s_ in range(2):
                        u = 2 * t + s_
                        if u >= 2:
                            pe.wait_ge(act_qk, u - 1)
                        for j in range(4):
                            last = nc.tensor.transpose(bank[4 + s_][:, j * P:(j + 1) * P],
                                                       qkp[:, t % 2, s_, 4 * j:4 * j + 4, :].rearrange("p a b -> p (a b)"),
                                                       ident)
                        last.then_inc(pe_qk, 1)

                for t in range(NT):
                    if t == 1:
                        pe.wait_ge(dve_wt, 5)
                    if t >= 2:
                        pe.wait_ge(dve_ra, 3 * (t - 1))
                        pe.wait_ge(act_v, t - 1)
                    ts = slice(t * P, (t + 1) * P)
                    for w, dst in ((0, bank[t % 2][:, 0:D]), (1, bank[t % 2][:, D:2 * D]), (2, bank[2 + t % 2][:, 0:D])):
                        for k in range(KD):
                            last = mm3(dst, (hT_hi[:, k, ts], hT_lo[:, k, ts]), (w_t[:, w, 0, k, :], w_t[:, w, 1, k, :]),
                                       k == 0, k == KD - 1)
                    last.then_inc(pe_qkv, 1)
                    if t:
                        qk_transposes(t - 1)
                qk_transposes(NT - 1)

                def scores(u):
                    b, qt, js = units[u]
                    nk = P * (qt + 1)
                    if u == 0:
                        pe.wait_ge(act_qk, 2 * NT)
                        pe.wait_ge(dve_ra, 3 * NT)
                        pe.wait_ge(act_v, NT)
                    for r in range(4):
                        if u:
                            pe.wait_ge(act_p, 4 * (u - 1) + r + 1)
                        for i_, j in enumerate(js):
                            last = nc.tensor.matmul(bank[r][:, i_ * nk:(i_ + 1) * nk],
                                                    q_t[32 * r:32 * r + DH, j, (2 * b + qt) * P:(2 * b + qt + 1) * P],
                                                    k_t[32 * r:32 * r + DH, j, 2 * b * P:2 * b * P + nk],
                                                    start=True, stop=True)
                        last.then_inc(pe_s, 1)

                def values(u, t_done):
                    b, qt, js = units[u]
                    for r in range(4):
                        pe.wait_ge(pool_n, 4 * u + r + 1)
                        if r < 2:
                            if u:
                                (pe.wait_ge(act_pt, 2 * u) if r == 0 else pe.wait_ge(dve_pt, 2 * u))
                        else:
                            (pe.wait_ge(act_pt, 2 * u + 1) if r == 2 else pe.wait_ge(dve_pt, 2 * u + 1))
                        for i_ in range(4):
                            last = nc.tensor.transpose(bank[4 + r % 2][:, i_ * P:(i_ + 1) * P],
                                                       prob_sb[:, r, i_ * P:(i_ + 1) * P], ident)
                        last.then_inc(pe_pt, 1)
                    if t_done is not None:
                        project(t_done)
                    if u == 0:
                        pe.wait_ge(pool_res, 2 * NT + 4)
                    if js[0] == 0 and u:
                        pe.wait_ge(dve_at, 2 * b + qt)
                    for r in range(4):
                        if r % 2 == 0:
                            pe.wait_ge(act_pt, 2 * u + r // 2 + 1)
                        else:
                            pe.wait_ge(dve_pt, 2 * u + r // 2 + 1)
                        for i_, j in enumerate(js):
                            hd = 4 * j + r
                            for kb in range(qt + 1):
                                blk = i_ * (qt + 1) + kb
                                last = nc.tensor.matmul(bank[6][32 * r:32 * r + 32, j * P:(j + 1) * P],
                                                        v_sb[:, 2 * b + kb, hd, :], prob_t[:, r, blk * P:(blk + 1) * P],
                                                        start=kb == 0, stop=kb == qt)
                    last.then_inc(pe_pv, 1)

                def project(t):
                    pe.wait_ge(dve_at, t + 1)
                    if t:
                        pe.wait_ge(dve_o, t)
                    for j in range(4):
                        last = mm3(bank[7][:, 0:D], (att_t[:, 0, j, :], att_t[:, 1, j, :]),
                                   (w_o[:, 0, j, :], w_o[:, 1, j, :]), j == 0, j == 3)
                    last.then_inc(pe_wo, 1)

                scores(0)
                for u in range(len(units)):
                    if u + 1 < len(units):
                        scores(u + 1)
                    values(u, tile_done(u - 1))
                project(NT - 1)

            @block.gpsimd
            def _(pool):
                pool.wait_ge(ld_gt, 32)
                for t in range(NT):
                    nc.gpsimd.tensor_tensor(y_acc[:, t, :], y_acc[:, t, :], mod[:, t // 2, 2 * D:3 * D],
                                            ALU.mult).then_inc(pool_res, 1)
                nc.gpsimd.memset(wo_pad[:, :, :, DH:32], 0.0).then_inc(pool_res, 1)
                pool.wait_ge(ld_wq, 64)
                nc.gpsimd.tensor_copy(wo_pad[:, :, :, 0:DH],
                                      w_raw[:, 3].rearrange("p o (h d) -> p o h d", d=DH)).then_inc(pool_res, 1)
                norm_pool(pool, 2)
                nc.gpsimd.memset(qkp[:, :, :, :, DH:32], 0.0).then_inc(pool_res, 1)
                nc.gpsimd.memset(v_sb[:, :, :, DH:32], 0.0).then_inc(pool_res, 1)
                for u, (b, qt, js) in enumerate(units):
                    nj, t = len(js), 2 * b + qt
                    for r in range(4):
                        pool.wait_ge(dve_rr, 4 * u + r + 1)
                        p3 = prob_sb[:, r].rearrange("p (j k) -> p j k", j=nj)
                        nc.gpsimd.tensor_tensor(p3, p3, bc(rrs[:, t, :].rearrange("p (j r) -> p j r", r=4)
                                                           [:, js[0]:js[0] + nj, r:r + 1], [P, nj, P * (qt + 1)]),
                                                ALU.mult).then_inc(pool_n, 1)

            @block.scalar
            def _(act):
                for i_ in range(3):
                    act.wait_ge(pe_wt, i_ + 1)
                    nc.scalar.copy(w_t[:, i_, 0].rearrange("p k d -> p (k d)"), bank[4 + i_][:, :]).then_inc(act_wt, 1)
                norm_act(act, 2)
                norm_act_copy(act, 2, bank[0:2])
                for jj in range(2):
                    act.wait_ge(pe_wt, 4 + jj)
                    nc.scalar.copy(w_o[:, 0, 2 * jj:2 * jj + 2].rearrange("p j d -> p (j d)"),
                                   wo_bank[jj][:, :]).then_inc(act_wt, 1)

                def qk_copies(t):
                    for s_ in range(2):
                        act.wait_ge(pe_qk, 2 * t + s_ + 1)
                        nc.scalar.copy((q_t, k_t)[s_][:, :, t * P:(t + 1) * P],
                                       bank[4 + s_][:, :].rearrange("p (j q) -> p j q", j=4)).then_inc(act_qk, 1)

                for t in range(NT):
                    act.wait_ge(pe_qkv, t + 1)
                    nc.scalar.copy(v_sb[:, t, :, 0:DH], bank[2 + t % 2][:, 0:D].rearrange("p (h d) -> p h d", d=DH)).then_inc(act_v, 1)
                    if t:
                        qk_copies(t - 1)
                qk_copies(NT - 1)

                def exps(u):
                    b, qt, js = units[u]
                    nk = P * (qt + 1)
                    for r in range(4):
                        act.wait_ge(dve_nm, 4 * u + r + 1)
                        if u:
                            act.wait_ge(pe_pt, 4 * (u - 1) + r + 1)
                        for i_, j in enumerate(js):
                            hd = 4 * j + r
                            last = nc.scalar.activation(prob_sb[:, r, i_ * nk:(i_ + 1) * nk], bank[r][:, i_ * nk:(i_ + 1) * nk],
                                                        ACT.Exp, bias=nmx[:, r, i_:i_ + 1], scale=DH ** -0.5,
                                                        accum_out=rs[:, 2 * b + qt, hd:hd + 1])
                        last.then_inc(act_p, 1)

                def heads_hi(u, t):
                    act.wait_ge(pe_pv, u + 1)
                    if t:
                        act.wait_ge(pe_wo, t)
                    nc.scalar.copy(att_t[:, 0].rearrange("p j q -> p (j q)"), bank[6][:, :]).then_inc(act_at, 1)

                exps(0)
                for u in range(len(units)):
                    if tile_done(u - 1) is not None:
                        heads_hi(u - 1, tile_done(u - 1))
                    for r in (0, 2):
                        act.wait_ge(pe_pt, 4 * u + r + 1)
                        if u:
                            act.wait_ge(pe_pv, u)
                        nc.scalar.copy(prob_t[:, r], bank[4][:, :]).then_inc(act_pt, 1)
                    if u + 1 < len(units):
                        exps(u + 1)
                heads_hi(len(units) - 1, NT - 1)

            @block.vector
            def _(dve):
                def qkv_lo():
                    for i_ in range(3):
                        dve.wait_ge(act_wt, i_ + 1)
                        nc.vector.tensor_tensor(w_t[:, i_, 1].rearrange("p k d -> p (k d)"), bank[4 + i_][:, :],
                                                w_t[:, i_, 0].rearrange("p k d -> p (k d)").bitcast(F32),
                                                ALU.subtract).then_inc(dve_wt, 1)

                for t in range(NT):
                    dve.wait_ge(pool_res, NT + t + 1)
                    nc.vector.tensor_tensor(x[:, t, :], x[:, t, :], y_acc[:, t, :], ALU.add).then_inc(dve_res1, 1)
                    dve.wait_ge(dve_res1, t + 1)
                    norm_stats(2, t)
                norm_dve(dve, 2, qkv_lo)
                norm_dve_lo(dve, 2, bank[0:2])
                for jj in range(2):
                    dve.wait_ge(act_wt, 4 + jj)
                    nc.vector.tensor_tensor(w_o[:, 1, 2 * jj:2 * jj + 2].rearrange("p j d -> p (j d)"), wo_bank[jj][:, :],
                                            w_o[:, 0, 2 * jj:2 * jj + 2].rearrange("p j d -> p (j d)").bitcast(F32),
                                            ALU.subtract).then_inc(dve_wt, 1)
                dve.wait_ge(ld_gt, 48)
                dve.wait_ge(pool_res, 2 * NT + 3)
                for t in range(NT):
                    c = t % 2
                    qk = bank[t % 2][:, :].rearrange("p (h d) -> p h d", d=DH)
                    n = 3 * t
                    dve.wait_ge(pe_qkv, t + 1)
                    if t:
                        dve.wait_ge(dve_qk, t)
                    nc.vector.tensor_tensor(r_a, qk, bc(rope[:, 0, c].unsqueeze(1), [P, 2 * AH, DH]),
                                            ALU.mult).then_inc(dve_ra, 1)
                    for o in range(2):
                        nc.vector.tensor_tensor(r_b[:, :, o::2], qk[:, :, 1 - o::2],
                                                bc(rope[:, 1, c, o::2].unsqueeze(1), [P, 2 * AH, DH // 2]),
                                                ALU.mult).then_inc(dve_ra, 1)
                    dve.wait_ge(dve_ra, n + 3)
                    if t >= 2:
                        dve.wait_ge(pe_qk, 2 * (t - 1))
                    nc.vector.tensor_tensor(qkp[:, t % 2].rearrange("p s h d -> p (s h) d")[:, :, 0:DH], r_a, r_b,
                                            ALU.add).then_inc(dve_qk, 1)

                def reciprocal(u, r):
                    b, qt, js = units[u]
                    dve.wait_ge(act_p, 4 * u + r + 1)

                    def heads(ap):
                        return ap[:, 2 * b + qt, :].rearrange("p (j r) -> p j r", r=4)[:, js[0]:js[0] + len(js), r]
                    nc.vector.reciprocal(heads(rrs), heads(rs)).then_inc(dve_rr, 1)

                def maxima(u):
                    b, qt, js = units[u]
                    nj, nk = len(js), P * (qt + 1)
                    for r in range(4):
                        v = 4 * u + r
                        s3 = bank[r][:, :].rearrange("p (j k) -> p j k", j=nj)
                        dve.wait_ge(pe_s, v + 1)
                        nc.vector.tensor_tensor(s3[:, :, qt * P:nk], s3[:, :, qt * P:nk],
                                                bc(neg_mask.unsqueeze(1), [P, nj, P]), ALU.add).then_inc(dve_mask, 1)
                        dve.wait_ge(dve_mask, v + 1)
                        if v >= 4:
                            dve.wait_ge(dve_nm, v - 3)
                        nc.vector.tensor_reduce(mx[:, r, 0:nj], s3, AX, ALU.max).then_inc(dve_mx, 1)
                        dve.wait_ge(dve_mx, v + 1)
                        if u:
                            dve.wait_ge(act_p, v - 3)
                        nc.vector.tensor_scalar(nmx[:, r, 0:nj], mx[:, r, 0:nj], -DH ** -0.5, None,
                                                ALU.mult).then_inc(dve_nm, 1)
                        if r:
                            reciprocal(u, r - 1)
                    reciprocal(u, 3)

                def heads_lo(t):
                    dve.wait_ge(act_at, t + 1)
                    if t:
                        dve.wait_ge(pe_wo, t)
                    nc.vector.tensor_tensor(att_t[:, 1].rearrange("p j q -> p (j q)"), bank[6][:, :],
                                            att_t[:, 0].rearrange("p j q -> p (j q)").bitcast(F32),
                                            ALU.subtract).then_inc(dve_at, 1)

                def residual(t):
                    dve.wait_ge(pe_wo, t + 1)
                    if t:
                        dve.wait_ge(dve_x, t)
                    nc.vector.tensor_tensor(otmp, bank[7][:, 0:D], mod[:, t // 2, 2 * D:3 * D],
                                            ALU.mult).then_inc(dve_o, 1)
                    dve.wait_ge(dve_o, t + 1)
                    nc.vector.tensor_tensor(x[:, t, :], x[:, t, :], otmp, ALU.add).then_inc(dve_x, 1)
                    dve.wait_ge(dve_x, t + 1)
                    norm_stats(3, t)

                maxima(0)
                for u in range(len(units)):
                    if tile_done(u - 1) is not None:
                        heads_lo(tile_done(u - 1))
                    for r in (1, 3):
                        dve.wait_ge(pe_pt, 4 * u + r + 1)
                        if u:
                            dve.wait_ge(pe_pv, u)
                        nc.vector.tensor_copy(prob_t[:, r], bank[5][:, :]).then_inc(dve_pt, 1)
                    if u + 1 < len(units):
                        maxima(u + 1)
                    if tile_done(u - 1) is not None:
                        residual(tile_done(u - 1))
                heads_lo(NT - 1)
                residual(NT - 1)

        take = carver()
        r_raw = take(D, parts=E1)
        bias_row = take(E1)
        assert take(1).offset % ARENA <= 8000
        takeh = carver(halves, HALVES)
        r_t = takeh(2, KD, E1)
        gu_t = takeh(2, 2, 4, F1)
        dn_t = take(2, D)
        s_sb = take(2, 512)
        a_sb = take(2, 512)
        lg1_t = s_sb.rearrange("p a b -> p (a b)")[0:E1, :]
        sc1, ch1, eq1, sel1, w1, comb = (take(NT, E1) for _ in range(6))
        s1, rc1 = take(NT), take(NT)
        m8 = take(NT, 8)
        i8 = take(NT, 8).bitcast(U32)
        i8f = take(NT, 8)
        names = ("ld_r act_sc dve_rt dve_comb pe_wg act_wg pe_wd act_wd pe_up act_s dve_a pe_dn "
                 "out_a out_d pool_fin dve_x ld_out dve_wg").split()
        g_ = {n: sem("e_" + n) for n in names}
        (ld_r, act_sc, dve_rt1, dve_comb1, pe_wg, act_wg, pe_wd, act_wd, pe_up1, act_s1, dve_a1,
         pe_dn1, act_y1, dve_y1, pool_fin, dve_x1, st_out, dve_wg) = (g_[n] for n in names)
        order = [E1] + list(range(EARLY, E1)) + list(range(EARLY))
        NE = len(order)

        with nc.Block() as block:
            @block.sync
            def _(sp):
                load_gate(sp, 3)
                sp.dma_start(r_raw, A["L1_ffn_router_w"]).then_inc(ld_r, 16)
                sp.dma_start(bias_row, A["L1_ffn_router_bias"].partition_broadcast(P)).then_inc(ld_r, 16)
                load_experts(sp, 0, EARLY)
                ov = out.rearrange("b (c p) d -> p (b c) d", p=P)
                for t in range(NT):
                    sp.wait_ge(dve_x1, t + 1)
                    sp.dma_start(ov[:, t, :], x[:, t, :]).then_inc(st_out, 16)
                sp.wait_ge(st_out, 16 * NT)

            @block.tensor
            def _(pe):

                def logits():
                    pe.wait_ge(dve_gw, 2)
                    for th in range(2):
                        pe.wait_ge(norm_hT, 3 * NT // 2 + (NT // 4) * (th + 1))
                        tok = slice(th * 512, (th + 1) * 512)
                        for k in range(KD):
                            last = mm3(bank[6 + th][0:E1, :], (r_t[:, 0, k, :], r_t[:, 1, k, :]),
                                       (hT_hi[:, k, tok], hT_lo[:, k, tok]), k == 0, k == KD - 1)
                        last.then_inc(pe_lgt, 1)

                def turn_logits():
                    pe.wait_ge(act_lgt, 4)
                    for t in range(NT):
                        last = nc.tensor.transpose(bank[5][:, t * E1:(t + 1) * E1], lg1_t[:, t * P:(t + 1) * P],
                                                   ident[0:E1, 0:E1])
                    last.then_inc(pe_lg, 1)

                early = 16 * (3 + 2 + E1 - EARLY)
                late_all = early + 16 * (2 + EARLY)

                def weights(n):
                    e = order[n]
                    pe.wait_ge(ld_w1, late_all if e < EARLY else early)
                    if n:
                        pe.wait_ge(dve_wg, n)
                        pe.wait_ge(act_wd, n)
                    for s_ in range(2):
                        for k in range(KD):
                            last = nc.tensor.transpose(bank[0][:, (2 * s_ + k) * P:(2 * s_ + k + 1) * P],
                                                       w1_raw[:, e, s_, k * P:(k + 1) * P], ident)
                    last.then_inc(pe_wg, 1)
                    for o in range(2):
                        last = nc.tensor.transpose(bank[1][:, o * P:(o + 1) * P], w1_raw[:, e, 2, o * P:(o + 1) * P], ident)
                    last.then_inc(pe_wd, 1)

                def up(n, th):
                    u = 2 * n + th
                    pe.wait_ge(dve_wg, n + 1)
                    if u >= 2:
                        pe.wait_ge(dve_a1, u - 1)
                    if u == 1:
                        pe.wait_ge(act_sc, 1)
                    for s_, bk in ((0, bank[2 + th]), (1, bank[4 + th])):
                        for k in range(KD):
                            tok = slice(th * 512, (th + 1) * 512)
                            last = mm3(bk[:, :], (gu_t[:, n % 2, 0, 2 * s_ + k, :], gu_t[:, n % 2, 1, 2 * s_ + k, :]),
                                       (hT_hi[:, k, tok], hT_lo[:, k, tok]), k == 0, k == KD - 1)
                    last.then_inc(pe_up1, 1)

                def down(n, th):
                    u = 2 * n + th
                    pe.wait_ge(dve_a1, u + 1)
                    pe.wait_ge(act_wd, n + 1)
                    for pr in range(2):
                        v = 2 * u + pr
                        if v >= 2:
                            w = v - 2
                            pe.wait_ge(*((act_y1, w + 1) if w < 4 else (dve_y1, 2 * (w - 4) + 2)))
                        for q_ in range(2):
                            last = nc.tensor.matmul(bank[6 + pr][:, q_ * D:(q_ + 1) * D],
                                                    a_sb[:, th, (2 * pr + q_) * P:(2 * pr + q_ + 1) * P], dn_t[:, n % 2, :],
                                                    start=True, stop=True)
                        last.then_inc(pe_dn1, 1)

                weights(0)
                pe.wait_ge(ld_r, 32)
                for k in range(KD):
                    last = nc.tensor.transpose(bank[4][:, k * E1:(k + 1) * E1], r_raw[:, k * P:(k + 1) * P],
                                               ident[0:E1, 0:E1])
                last.then_inc(pe_gw, 1)
                norm_pe(pe, 3, bank[2:4])
                logits()
                turn_logits()
                up(0, 0)
                weights(1)
                up(0, 1)
                for n in range(NE):
                    down(n, 0)
                    if n + 1 < NE:
                        up(n + 1, 0)
                    down(n, 1)
                    if n + 2 < NE:
                        weights(n + 2)
                    if n + 1 < NE:
                        up(n + 1, 1)

            @block.gpsimd
            def _(pool):
                norm_pool(pool, 3)
                pool.wait_ge(ld_gt, 64)
                for t in range(NT):
                    pool.wait_ge(dve_y1, NT * (NE - 2) + t + 1)
                    nc.gpsimd.tensor_tensor(y_acc[:, t, :], y_acc[:, t, :], mod[:, t // 2, 2 * D:3 * D],
                                            ALU.mult).then_inc(pool_fin, 1)

            @block.scalar
            def _(act):
                def weights(n):
                    act.wait_ge(pe_wg, n + 1)
                    if n >= 2:
                        act.wait_ge(pe_up1, 2 * (n - 1))
                    nc.scalar.copy(gu_t[:, n % 2, 0].rearrange("p a b -> p (a b)"), bank[0][:, :]).then_inc(act_wg, 1)
                    act.wait_ge(pe_wd, n + 1)
                    if n >= 2:
                        act.wait_ge(pe_dn1, 4 * (n - 1))
                    nc.scalar.copy(dn_t[:, n % 2], bank[1][:, 0:D]).then_inc(act_wd, 1)

                norm_act(act, 3)
                weights(0)
                act.wait_ge(pe_gw, 2)
                nc.scalar.copy(r_t[:, 0].rearrange("p k e -> p (k e)"), bank[4][:, 0:KD * E1]).then_inc(act_gw, 1)
                norm_act_copy(act, 3, bank[2:4])
                for th in range(2):
                    act.wait_ge(pe_lgt, 3 + th)
                    nc.scalar.copy(lg1_t[:, th * 512:(th + 1) * 512], bank[6 + th][0:E1, :]).then_inc(act_lgt, 1)
                act.wait_ge(pe_lg, 2)
                nc.scalar.activation(sc1.rearrange("p t e -> p (t e)"), bank[5][:, 0:P], ACT.Sigmoid).then_inc(act_sc, 1)

                for n in range(NE):
                    for th in range(2):
                        u = 2 * n + th
                        act.wait_ge(pe_up1, u + 1)
                        if u >= 2:
                            act.wait_ge(dve_a1, u - 1)
                        nc.scalar.activation(s_sb[:, th], bank[2 + th][:, :], ACT.Silu).then_inc(act_s1, 1)
                        if th == 0 and n + 1 < NE:
                            weights(n + 1)
                    if n == 0:
                        for v in range(4):
                            act.wait_ge(pe_dn1, v + 1)
                            nc.scalar.copy(y_acc[:, 2 * v:2 * v + 2, :],
                                           bank[6 + v % 2][:, :].rearrange("p (a b) -> p a b", a=2)).then_inc(act_y1, 1)

            @block.vector
            def _(dve):
                norm_dve(dve, 3)
                dve.wait_ge(act_gw, 2)
                nc.vector.tensor_tensor(r_t[:, 1].rearrange("p k e -> p (k e)"), bank[4][:, 0:KD * E1],
                                        r_t[:, 0].rearrange("p k e -> p (k e)").bitcast(F32),
                                        ALU.subtract).then_inc(dve_gw, 1)
                norm_dve_lo(dve, 3, bank[2:4])

                def weights_lo(n):
                    dve.wait_ge(act_wg, n + 1)
                    if n >= 2:
                        dve.wait_ge(pe_up1, 2 * (n - 1))
                    nc.vector.tensor_tensor(gu_t[:, n % 2, 1].rearrange("p a b -> p (a b)"), bank[0][:, :],
                                            gu_t[:, n % 2, 0].rearrange("p a b -> p (a b)").bitcast(F32),
                                            ALU.subtract).then_inc(dve_wg, 1)

                def product(u):
                    th = u % 2
                    dve.wait_ge(act_s1, u + 1)
                    if u >= 2:
                        dve.wait_ge(pe_dn1, 2 * (u - 1))
                    nc.vector.tensor_tensor(a_sb[:, th], bank[4 + th][:, :], s_sb[:, th], ALU.mult).then_inc(dve_a1, 1)

                def sums(u):
                    n, th = u // 2, u % 2
                    e = order[n]
                    for pr in range(2):
                        v = 2 * u + pr
                        dve.wait_ge(pe_dn1, v + 1)
                        for q_ in range(2):
                            t = 4 * th + 2 * pr + q_
                            if n >= 2:
                                dve.wait_ge(dve_y1, NT * (n - 2) + t + 1)
                            nc.vector.scalar_tensor_tensor(out=y_acc[:, t, :], in0=bank[6 + pr][:, q_ * D:(q_ + 1) * D],
                                                           scalar=comb[:, t, e:e + 1], in1=y_acc[:, t, :],
                                                           op0=ALU.mult, op1=ALU.add).then_inc(dve_y1, 1)

                weights_lo(0)
                product(0)
                weights_lo(1)
                product(1)
                dve.wait_ge(ld_r, 32)
                dve.wait_ge(act_sc, 1)
                nc.vector.tensor_tensor(ch1, sc1, bc(bias_row.unsqueeze(1), [P, NT, E1]), ALU.add).then_inc(dve_rt1, 1)
                dve.wait_ge(dve_rt1, 1)
                n = topk_select(dve, ch1, K1, dve_rt1, 1, eq1, sel1, m8, i8, i8f)
                dve.wait_ge(dve_rt1, n)
                nc.vector.tensor_tensor(w1, sc1, sel1, ALU.mult).then_inc(dve_rt1, 1)
                dve.wait_ge(dve_rt1, n + 1)
                nc.vector.tensor_reduce(s1, w1, AX, ALU.add).then_inc(dve_rt1, 1)
                dve.wait_ge(dve_rt1, n + 2)
                nc.vector.tensor_scalar(s1, s1, 1e-20, None, ALU.add).then_inc(dve_rt1, 1)
                dve.wait_ge(dve_rt1, n + 3)
                nc.vector.reciprocal(rc1, s1).then_inc(dve_rt1, 1)
                dve.wait_ge(dve_rt1, n + 4)
                nc.vector.tensor_tensor(comb, w1, bc(rc1.unsqueeze(2), [P, NT, E1]), ALU.mult).then_inc(dve_comb1, 1)
                dve.wait_ge(dve_comb1, 1)
                dve.wait_ge(act_y1, 4)
                for u in range(2, 2 * NE):
                    product(u)
                    if u >= 3:
                        sums(u - 1)
                    if u % 2 == 0 and u // 2 + 1 < NE:
                        weights_lo(u // 2 + 1)
                sums(2 * NE - 1)
                for t in range(NT):
                    dve.wait_ge(pool_fin, t + 1)
                    nc.vector.tensor_tensor(x[:, t, :], x[:, t, :], y_acc[:, t, :], ALU.add).then_inc(dve_x1, 1)


_INS = ['L0_attn_hidden_states', 'L0_attn_Wz', 'L0_attn_Wx', 'L0_attn_WB', 'L0_attn_WC', 'L0_attn_Wdt',
        'L0_attn_conv_w', 'L0_attn_conv_b', 'L0_attn_dt_bias', 'L0_attn_A_log', 'L0_attn_D', 'L0_attn_norm_w',
        'L0_attn_Wout', 'L0_ffn_gate_w', 'L0_ffn_w_gate', 'L0_ffn_w_up', 'L0_ffn_w_down', 'L0_ffn_ws_gate',
        'L0_ffn_ws_up', 'L0_ffn_ws_down', 'L0_c', 'L0_wmod', 'L1_attn_Wq', 'L1_attn_Wk', 'L1_attn_Wv', 'L1_attn_Wo',
        'L1_ffn_router_w', 'L1_ffn_router_bias', 'L1_ffn_expert_gate_w', 'L1_ffn_expert_up_w',
        'L1_ffn_expert_down_w', 'L1_ffn_shared_gate_w', 'L1_ffn_shared_up_w', 'L1_ffn_shared_down_w', 'L1_c',
        'L1_wmod']


def constants():
    import numpy as np
    k = np.arange(P)[:, None]
    j = np.arange(P)[None, :]
    c = np.zeros((P, C_ALL), np.float32)
    c[:, C_ID:C_ID + P] = k == j
    c[:, C_GT:C_GT + P] = k > j
    c[:, C_LE:C_LE + P] = k <= j
    c[:, C_ONE:C_ONE + P] = 1.0
    c[:, C_LE2:C_LE2 + P] = k <= j
    c[:, C_LT:C_LT + P] = k < j
    c[:, C_NEG:C_NEG + P] = np.where(j > k, -1e30, 0.0)
    c[:, C_IOTA:C_IOTA + P] = np.broadcast_to(j, (P, P))
    theta = (np.float32(10000.0) ** (np.float32(-2.0) * np.arange(DH // 2, dtype=np.float32) / np.float32(DH)))
    ang = np.arange(S, dtype=np.float32)[:, None] * theta.astype(np.float32)[None, :]
    cos, sin = np.cos(ang).astype(np.float32), np.sin(ang).astype(np.float32)
    tab = np.zeros((2, S, DH), np.float32)
    tab[0, :, 0::2] = cos
    tab[0, :, 1::2] = cos
    tab[1, :, 0::2] = -sin
    tab[1, :, 1::2] = sin
    c[:, C_ROPE:] = tab.reshape(2, 2, P, DH).transpose(2, 0, 1, 3).reshape(P, -1)
    return c


def kernel(**inputs):
    import numpy as _np
    import concourse.bacc as _bacc
    from concourse import mybir as _mybir
    from concourse.bass_utils import run_bass_kernel_spmd as _run

    nc = _bacc.Bacc("TRN2", target_bir_lowering=False, num_devices=1)
    arrays, aps = {}, {}
    for name in _INS:
        a = _np.ascontiguousarray(inputs[name])
        arrays[f"in_{name}"] = a
        aps[name] = nc.dram_tensor(f"in_{name}", a.shape, _mybir.dt.from_np(a.dtype), kind="ExternalInput").ap()
    arrays["const_in"] = constants()
    aps["const"] = nc.dram_tensor("const_in", arrays["const_in"].shape, F32, kind="ExternalInput").ap()
    aps["mod_rows"] = nc.dram_tensor("mod_rows", (2, B, 6 * D), F32, kind="Internal").ap()
    out = nc.dram_tensor("out_0", (B, S, D), F32, kind="ExternalOutput").ap()
    build(nc, aps, out)
    r = _run(nc, [arrays], core_ids=[0])
    return r.results[0]["out_0"]
```
